# Optimizing a Trainium2 kernel written in Bass

```python
import numpy as np
import jax
import jax.numpy as jnp

def _softmax(x, axis=-1):
    return jax.nn.softmax(x, axis=axis)

def _gelu(x):
    return jax.nn.gelu(x, approximate=True)

def _silu(x):
    return jax.nn.silu(x)

def _sigmoid(x):
    return jax.nn.sigmoid(x)

def _layernorm(x, axis=-1, eps=1e-05):
    m = jnp.mean(x, axis=axis, keepdims=True)
    v = jnp.var(x, axis=axis, keepdims=True)
    return (x - m) / jnp.sqrt(v + eps)

def _scatter_add(tgt, idx, src, axis=0):
    return tgt.at[idx].add(src)

def _segment_sum(src, seg, n):
    return jax.ops.segment_sum(src, seg, n)
kernel_name = 'mk_xattn_seq_d4_seqx_r8_403a2b'

def setup_inputs(seed: int=0):
    np.random.seed(seed)
    _w = jnp.asarray

    def _rec_inputs():
        import jax
        import jax.numpy as jnp
        _rk = jax.random.key(seed)
        x = -0.0003929 + 0.9999 * jax.random.normal(jax.random.fold_in(_rk, 1), (4, 256, 256), jnp.float32)
        _lenS = 256 - jax.random.randint(jax.random.fold_in(_rk, 7), (4,), 0, max(1, 256 // 4) + 1, jnp.int32)
        _lenS2 = 256 - jax.random.randint(jax.random.fold_in(_rk, 8), (4,), 0, max(1, 256 // 4) + 1, jnp.int32)
        _ctx_1024P = jax.random.normal(jax.random.fold_in(_rk, 11), (4, 16, 128), jnp.float32)
        _ctx_1024c = jax.random.dirichlet(jax.random.fold_in(_rk, 511), 0.3 * jnp.ones((16,), jnp.float32), (4, 256))
        _ctx_1024t = jnp.einsum('bsk,bkd->bsd', _ctx_1024c, _ctx_1024P)
        _ctx_1024t = _ctx_1024t * jax.lax.rsqrt(jnp.mean(jnp.square(_ctx_1024t)) + 1e-12) * 0.953939
        ctx_1024 = 0.00191187 + 0.999416 * (_ctx_1024t + 0.3 * jax.random.normal(jax.random.fold_in(_rk, 611), (4, 256, 128), jnp.float32))
        pos_1xS = jnp.broadcast_to(jnp.arange(256, dtype=jnp.int32), (1, 256))
        _validS = jnp.arange(256)[None, :] < _lenS[:, None]
        _validS2 = jnp.arange(256)[None, :] < _lenS2[:, None]
        _causal = jnp.tril(jnp.ones((256, 256), dtype=bool))
        mask_BxS2_bk0 = jnp.logical_not(jnp.broadcast_to(_validS2[:, :], (4, 256)))
        mask_BxS_ik0 = jnp.where(jnp.broadcast_to(_validS[:, :], (4, 256)), 0, 1).astype(jnp.int32)
        return (x, ctx_1024, pos_1xS, mask_BxS2_bk0, mask_BxS_ik0)
    x, ctx_1024, pos_1xS, mask_BxS2_bk0, mask_BxS_ik0 = _rec_inputs()

    def _L0_xattn_setup():
        import jax, jax.numpy as jnp
        import numpy as np
        DIM = 256
        DIM_MEDIA = 128
        HEADS = 16
        DIM_HEAD = 64
        INNER = HEADS * DIM_HEAD
        FF_INNER = 4 * DIM
        B, N_TOK, N_LAT = (4, 256, 64)
        EPS = 1e-05

        def layernorm(x, g, b):
            mu = jnp.mean(x, axis=-1, keepdims=True)
            var = jnp.var(x, axis=-1, keepdims=True)
            return (x - mu) * jax.lax.rsqrt(var + EPS) * g + b
        key = jax.random.key(seed)
        ks = jax.random.split(key, 12)
        x = jax.random.normal(ks[0], (B, N_TOK, DIM), dtype=jnp.float32)
        media = jax.random.normal(ks[1], (B, N_LAT, DIM_MEDIA), dtype=jnp.float32)
        media_mask = jax.random.randint(ks[2], (B, N_LAT), 0, 2).astype(bool)
        media_mask = media_mask.at[:, 0].set(True)
        s = lambda d: 1.0 / np.sqrt(d)
        Wq = jax.random.normal(ks[3], (DIM, INNER), dtype=jnp.float32) * s(DIM)
        Wkv = jax.random.normal(ks[4], (DIM_MEDIA, 2 * INNER), dtype=jnp.float32) * s(DIM_MEDIA)
        Wo = jax.random.normal(ks[5], (INNER, DIM), dtype=jnp.float32) * s(INNER)
        W1 = jax.random.normal(ks[6], (DIM, FF_INNER), dtype=jnp.float32) * s(DIM)
        W2 = jax.random.normal(ks[7], (FF_INNER, DIM), dtype=jnp.float32) * s(FF_INNER)
        return {'x': x, 'media': media, 'media_mask': media_mask, 'ln_q_g': jnp.ones((DIM,), jnp.float32), 'ln_q_b': jnp.zeros((DIM,), jnp.float32), 'Wq': Wq, 'Wkv': Wkv, 'Wo': Wo, 'attn_gate': jax.random.normal(ks[8], (1,), jnp.float32) * 0.5, 'ln_ff_g': jnp.ones((DIM,), jnp.float32), 'ln_ff_b': jnp.zeros((DIM,), jnp.float32), 'W1': W1, 'W2': W2, 'ff_gate': jax.random.normal(ks[9], (1,), jnp.float32) * 0.5}
    _L0_xattn_all = _L0_xattn_setup()
    _L0_xattn_in = {k: v for k, v in _L0_xattn_all.items() if k in ('ln_q_g', 'ln_q_b', 'Wq', 'Wkv', 'Wo', 'attn_gate', 'ln_ff_g', 'ln_ff_b', 'W1', 'W2', 'ff_gate')}
    del _L0_xattn_all

    def _L1_xattn_setup():
        import jax, jax.numpy as jnp
        import numpy as np
        H = 256
        NH = 16
        HD = H // NH
        CH = 128
        CC = 128
        CHD = CC // NH
        I = 688
        B = 2
        L = 256
        LE = 128
        EPS = 1e-06

        def rms_norm(x, w):
            xf = x.astype(jnp.float32)
            var = jnp.mean(xf * xf, axis=-1, keepdims=True)
            return (w * (xf * jax.lax.rsqrt(var + EPS))).astype(x.dtype)

        def expert_mask(tt):
            vm = jnp.zeros(tt.shape, dtype=bool)
            vm = vm.at[:, :-1].set((tt[:, :-1] == 1) & (tt[:, 1:] == 1))
            return vm

        def rotate_half(x):
            d = x.shape[-1] // 2
            return jnp.concatenate([-x[..., d:], x[..., :d]], axis=-1)

        def apply_rotary(q, k, position_ids, seq_len):
            inv = 1.0 / 10000.0 ** (jnp.arange(0, HD, 2, dtype=jnp.float32) / HD)
            t = jnp.arange(seq_len, dtype=jnp.float32)
            freqs = jnp.outer(t, inv)
            emb = jnp.concatenate([freqs, freqs], axis=-1)
            cos = jnp.cos(emb)[position_ids][:, None].astype(q.dtype)
            sin = jnp.sin(emb)[position_ids][:, None].astype(q.dtype)
            return (q * cos + rotate_half(q) * sin, k * cos + rotate_half(k) * sin)

        def sdpa(q, k, v, causal):
            scale = 1.0 / np.sqrt(q.shape[-1])
            scores = jnp.einsum('bhqd,bhkd->bhqk', q * scale, k)
            if causal:
                mask = jnp.tril(jnp.ones((q.shape[-2], k.shape[-2]), dtype=bool))
                scores = jnp.where(mask, scores, jnp.finfo(jnp.float32).min)
            p = jax.nn.softmax(scores.astype(jnp.float32), axis=-1).astype(q.dtype)
            return jnp.einsum('bhqk,bhkd->bhqd', p, v)

        def heads(x, nh, hd):
            b, l, _ = x.shape
            return x.reshape(b, l, nh, hd).transpose(0, 2, 1, 3)
        key = jax.random.key(seed)
        ks = jax.random.split(key, 20)
        s = 0.02
        f32 = jnp.float32
        return {'hidden_states': jax.random.normal(ks[0], (B, L, H), f32), 'encoder_outputs': jax.random.normal(ks[1], (B, LE, CH), f32), 'token_type_ids': jax.random.randint(ks[2], (B, L), 0, 2, jnp.int32), 'position_ids': jnp.arange(L, dtype=jnp.int32)[None, :], 'ln_in_w': jnp.ones((H,), f32), 'ln_post_attn_w': jnp.ones((H,), f32), 'ln_post_cross_w': jnp.ones((H,), f32), 'v_qkv': jax.random.normal(ks[3], (H, 3 * H), f32) * s, 'l_qkv': jax.random.normal(ks[4], (H, 3 * H), f32) * s, 'v_dense': jax.random.normal(ks[5], (H, H), f32) * s, 'l_dense': jax.random.normal(ks[6], (H, H), f32) * s, 'cq_w': jax.random.normal(ks[7], (H, CC), f32) * s, 'ckv_w': jax.random.normal(ks[8], (CH, 2 * CC), f32) * s, 'cdense_w': jax.random.normal(ks[9], (CC, H), f32) * s, 'v_gate': jax.random.normal(ks[10], (H, I), f32) * s, 'v_up': jax.random.normal(ks[11], (H, I), f32) * s, 'v_down': jax.random.normal(ks[12], (I, H), f32) * s, 'l_gate': jax.random.normal(ks[13], (H, I), f32) * s, 'l_up': jax.random.normal(ks[14], (H, I), f32) * s, 'l_down': jax.random.normal(ks[15], (I, H), f32) * s}
    _L1_xattn_all = _L1_xattn_setup()
    _L1_xattn_in = {k: v for k, v in _L1_xattn_all.items() if k in ('ln_in_w', 'ln_post_attn_w', 'ln_post_cross_w', 'v_qkv', 'l_qkv', 'v_dense', 'l_dense', 'cq_w', 'ckv_w', 'cdense_w', 'v_gate', 'v_up', 'v_down', 'l_gate', 'l_up', 'l_down')}
    del _L1_xattn_all

    def _L2_xattn_setup():
        import jax, jax.numpy as jnp
        import numpy as np
        EPS = 1e-06

        def _rmsnorm(x, w):
            var = jnp.mean(jnp.square(x), axis=-1, keepdims=True)
            return x * jax.lax.rsqrt(var + EPS) * w
        key = jax.random.key(seed)
        ks = jax.random.split(key, 6)
        B, N, M = (4, 512, 256)
        d_model, memory_dim = (256, 128)
        hidden_states = jax.random.normal(ks[0], (B, N, d_model), dtype=jnp.float32)
        memory = jax.random.normal(ks[1], (B, M, memory_dim), dtype=jnp.float32)
        W_mem = jax.random.normal(ks[2], (d_model, memory_dim), dtype=jnp.float32) / np.sqrt(memory_dim)
        W_gate = jax.random.normal(ks[3], (d_model, 2 * d_model), dtype=jnp.float32) / np.sqrt(2 * d_model)
        b_gate = jax.random.normal(ks[4], (d_model,), dtype=jnp.float32) * 0.01
        norm_w = jnp.ones((d_model,), dtype=jnp.float32)
        return {'hidden_states': hidden_states, 'memory': memory, 'W_mem': W_mem, 'W_gate': W_gate, 'b_gate': b_gate, 'norm_w': norm_w}
    _L2_xattn_all = _L2_xattn_setup()
    _L2_xattn_in = {k: v for k, v in _L2_xattn_all.items() if k in ('W_mem', 'W_gate', 'b_gate', 'norm_w')}
    del _L2_xattn_all

    def _L3_xattn_setup():
        import jax, jax.numpy as jnp
        import numpy as np
        DIM = 256
        DIM_MEDIA = 128
        HEADS = 16
        DIM_HEAD = 64
        INNER = HEADS * DIM_HEAD
        FF_INNER = 4 * DIM
        B, N_TOK, N_LAT = (4, 256, 64)
        EPS = 1e-05

        def layernorm(x, g, b):
            mu = jnp.mean(x, axis=-1, keepdims=True)
            var = jnp.var(x, axis=-1, keepdims=True)
            return (x - mu) * jax.lax.rsqrt(var + EPS) * g + b
        key = jax.random.key(seed)
        ks = jax.random.split(key, 12)
        x = jax.random.normal(ks[0], (B, N_TOK, DIM), dtype=jnp.float32)
        media = jax.random.normal(ks[1], (B, N_LAT, DIM_MEDIA), dtype=jnp.float32)
        media_mask = jax.random.randint(ks[2], (B, N_LAT), 0, 2).astype(bool)
        media_mask = media_mask.at[:, 0].set(True)
        s = lambda d: 1.0 / np.sqrt(d)
        Wq = jax.random.normal(ks[3], (DIM, INNER), dtype=jnp.float32) * s(DIM)
        Wkv = jax.random.normal(ks[4], (DIM_MEDIA, 2 * INNER), dtype=jnp.float32) * s(DIM_MEDIA)
        Wo = jax.random.normal(ks[5], (INNER, DIM), dtype=jnp.float32) * s(INNER)
        W1 = jax.random.normal(ks[6], (DIM, FF_INNER), dtype=jnp.float32) * s(DIM)
        W2 = jax.random.normal(ks[7], (FF_INNER, DIM), dtype=jnp.float32) * s(FF_INNER)
        return {'x': x, 'media': media, 'media_mask': media_mask, 'ln_q_g': jnp.ones((DIM,), jnp.float32), 'ln_q_b': jnp.zeros((DIM,), jnp.float32), 'Wq': Wq, 'Wkv': Wkv, 'Wo': Wo, 'attn_gate': jax.random.normal(ks[8], (1,), jnp.float32) * 0.5, 'ln_ff_g': jnp.ones((DIM,), jnp.float32), 'ln_ff_b': jnp.zeros((DIM,), jnp.float32), 'W1': W1, 'W2': W2, 'ff_gate': jax.random.normal(ks[9], (1,), jnp.float32) * 0.5}
    _L3_xattn_all = _L3_xattn_setup()
    _L3_xattn_in = {k: v for k, v in _L3_xattn_all.items() if k in ('ln_q_g', 'ln_q_b', 'Wq', 'Wkv', 'Wo', 'attn_gate', 'ln_ff_g', 'ln_ff_b', 'W1', 'W2', 'ff_gate')}
    del _L3_xattn_all
    return {'x': x, 'ctx_1024': ctx_1024, 'pos_1xS': pos_1xS, 'mask_BxS2_bk0': mask_BxS2_bk0, 'mask_BxS_ik0': mask_BxS_ik0, 'L0_xattn_ln_q_g': _L0_xattn_in['ln_q_g'], 'L0_xattn_ln_q_b': _L0_xattn_in['ln_q_b'], 'L0_xattn_Wq': _L0_xattn_in['Wq'], 'L0_xattn_Wkv': _L0_xattn_in['Wkv'], 'L0_xattn_Wo': _L0_xattn_in['Wo'], 'L0_xattn_attn_gate': _L0_xattn_in['attn_gate'], 'L0_xattn_ln_ff_g': _L0_xattn_in['ln_ff_g'], 'L0_xattn_ln_ff_b': _L0_xattn_in['ln_ff_b'], 'L0_xattn_W1': _L0_xattn_in['W1'], 'L0_xattn_W2': _L0_xattn_in['W2'], 'L0_xattn_ff_gate': _L0_xattn_in['ff_gate'], 'L1_xattn_ln_in_w': _L1_xattn_in['ln_in_w'], 'L1_xattn_ln_post_attn_w': _L1_xattn_in['ln_post_attn_w'], 'L1_xattn_ln_post_cross_w': _L1_xattn_in['ln_post_cross_w'], 'L1_xattn_v_qkv': _L1_xattn_in['v_qkv'], 'L1_xattn_l_qkv': _L1_xattn_in['l_qkv'], 'L1_xattn_v_dense': _L1_xattn_in['v_dense'], 'L1_xattn_l_dense': _L1_xattn_in['l_dense'], 'L1_xattn_cq_w': _L1_xattn_in['cq_w'], 'L1_xattn_ckv_w': _L1_xattn_in['ckv_w'], 'L1_xattn_cdense_w': _L1_xattn_in['cdense_w'], 'L1_xattn_v_gate': _L1_xattn_in['v_gate'], 'L1_xattn_v_up': _L1_xattn_in['v_up'], 'L1_xattn_v_down': _L1_xattn_in['v_down'], 'L1_xattn_l_gate': _L1_xattn_in['l_gate'], 'L1_xattn_l_up': _L1_xattn_in['l_up'], 'L1_xattn_l_down': _L1_xattn_in['l_down'], 'L2_xattn_W_mem': _L2_xattn_in['W_mem'], 'L2_xattn_W_gate': _L2_xattn_in['W_gate'], 'L2_xattn_b_gate': _L2_xattn_in['b_gate'], 'L2_xattn_norm_w': _L2_xattn_in['norm_w'], 'L3_xattn_ln_q_g': _L3_xattn_in['ln_q_g'], 'L3_xattn_ln_q_b': _L3_xattn_in['ln_q_b'], 'L3_xattn_Wq': _L3_xattn_in['Wq'], 'L3_xattn_Wkv': _L3_xattn_in['Wkv'], 'L3_xattn_Wo': _L3_xattn_in['Wo'], 'L3_xattn_attn_gate': _L3_xattn_in['attn_gate'], 'L3_xattn_ln_ff_g': _L3_xattn_in['ln_ff_g'], 'L3_xattn_ln_ff_b': _L3_xattn_in['ln_ff_b'], 'L3_xattn_W1': _L3_xattn_in['W1'], 'L3_xattn_W2': _L3_xattn_in['W2'], 'L3_xattn_ff_gate': _L3_xattn_in['ff_gate']}

def reference(x, ctx_1024, pos_1xS, mask_BxS2_bk0, mask_BxS_ik0, L0_xattn_ln_q_g, L0_xattn_ln_q_b, L0_xattn_Wq, L0_xattn_Wkv, L0_xattn_Wo, L0_xattn_attn_gate, L0_xattn_ln_ff_g, L0_xattn_ln_ff_b, L0_xattn_W1, L0_xattn_W2, L0_xattn_ff_gate, L1_xattn_ln_in_w, L1_xattn_ln_post_attn_w, L1_xattn_ln_post_cross_w, L1_xattn_v_qkv, L1_xattn_l_qkv, L1_xattn_v_dense, L1_xattn_l_dense, L1_xattn_cq_w, L1_xattn_ckv_w, L1_xattn_cdense_w, L1_xattn_v_gate, L1_xattn_v_up, L1_xattn_v_down, L1_xattn_l_gate, L1_xattn_l_up, L1_xattn_l_down, L2_xattn_W_mem, L2_xattn_W_gate, L2_xattn_b_gate, L2_xattn_norm_w, L3_xattn_ln_q_g, L3_xattn_ln_q_b, L3_xattn_Wq, L3_xattn_Wkv, L3_xattn_Wo, L3_xattn_attn_gate, L3_xattn_ln_ff_g, L3_xattn_ln_ff_b, L3_xattn_W1, L3_xattn_W2, L3_xattn_ff_gate):
    import jax
    import jax.numpy as jnp

    def _L0_xattn_ref(x, media, media_mask, ln_q_g, ln_q_b, Wq, Wkv, Wo, attn_gate, ln_ff_g, ln_ff_b, W1, W2, ff_gate):
        import jax, jax.numpy as jnp
        import numpy as np
        DIM = 256
        DIM_MEDIA = 128
        HEADS = 16
        DIM_HEAD = 64
        INNER = HEADS * DIM_HEAD
        FF_INNER = 4 * DIM
        B, N_TOK, N_LAT = (4, 256, 64)
        EPS = 1e-05

        def layernorm(x, g, b):
            mu = jnp.mean(x, axis=-1, keepdims=True)
            var = jnp.var(x, axis=-1, keepdims=True)
            return (x - mu) * jax.lax.rsqrt(var + EPS) * g + b
        scale = DIM_HEAD ** (-0.5)
        qn = layernorm(x, ln_q_g, ln_q_b)
        q = qn @ Wq * scale
        kv = media @ Wkv
        k, v = jnp.split(kv, 2, axis=-1)
        split_heads = lambda t: t.reshape(t.shape[0], t.shape[1], HEADS, DIM_HEAD).transpose(0, 2, 1, 3)
        q, k, v = (split_heads(q), split_heads(k), split_heads(v))
        sim = jnp.einsum('bhid,bhjd->bhij', q, k)
        neg_inf = jnp.finfo(sim.dtype).min
        sim = jnp.where(media_mask[:, None, None, :], sim, neg_inf)
        attn = jax.nn.softmax(sim, axis=-1)
        out = jnp.einsum('bhij,bhjd->bhid', attn, v)
        out = out.transpose(0, 2, 1, 3).reshape(x.shape[0], x.shape[1], INNER)
        attn_out = out @ Wo
        x = x + jnp.tanh(attn_gate) * attn_out
        h = layernorm(x, ln_ff_g, ln_ff_b)
        h = jax.nn.gelu(h @ W1, approximate=False) @ W2
        x = x + jnp.tanh(ff_gate) * h
        return x

    def _L1_xattn_ref(hidden_states, encoder_outputs, token_type_ids, position_ids, ln_in_w, ln_post_attn_w, ln_post_cross_w, v_qkv, l_qkv, v_dense, l_dense, cq_w, ckv_w, cdense_w, v_gate, v_up, v_down, l_gate, l_up, l_down):
        import jax, jax.numpy as jnp
        import numpy as np
        H = 256
        NH = 16
        HD = H // NH
        CH = 128
        CC = 128
        CHD = CC // NH
        I = 688
        B = 2
        L = 256
        LE = 128
        EPS = 1e-06

        def rms_norm(x, w):
            xf = x.astype(jnp.float32)
            var = jnp.mean(xf * xf, axis=-1, keepdims=True)
            return (w * (xf * jax.lax.rsqrt(var + EPS))).astype(x.dtype)

        def expert_mask(tt):
            vm = jnp.zeros(tt.shape, dtype=bool)
            vm = vm.at[:, :-1].set((tt[:, :-1] == 1) & (tt[:, 1:] == 1))
            return vm

        def rotate_half(x):
            d = x.shape[-1] // 2
            return jnp.concatenate([-x[..., d:], x[..., :d]], axis=-1)

        def apply_rotary(q, k, position_ids, seq_len):
            inv = 1.0 / 10000.0 ** (jnp.arange(0, HD, 2, dtype=jnp.float32) / HD)
            t = jnp.arange(seq_len, dtype=jnp.float32)
            freqs = jnp.outer(t, inv)
            emb = jnp.concatenate([freqs, freqs], axis=-1)
            cos = jnp.cos(emb)[position_ids][:, None].astype(q.dtype)
            sin = jnp.sin(emb)[position_ids][:, None].astype(q.dtype)
            return (q * cos + rotate_half(q) * sin, k * cos + rotate_half(k) * sin)

        def sdpa(q, k, v, causal):
            scale = 1.0 / np.sqrt(q.shape[-1])
            scores = jnp.einsum('bhqd,bhkd->bhqk', q * scale, k)
            if causal:
                mask = jnp.tril(jnp.ones((q.shape[-2], k.shape[-2]), dtype=bool))
                scores = jnp.where(mask, scores, jnp.finfo(jnp.float32).min)
            p = jax.nn.softmax(scores.astype(jnp.float32), axis=-1).astype(q.dtype)
            return jnp.einsum('bhqk,bhkd->bhqd', p, v)

        def heads(x, nh, hd):
            b, l, _ = x.shape
            return x.reshape(b, l, nh, hd).transpose(0, 2, 1, 3)
        b, l, _ = hidden_states.shape
        vm = expert_mask(token_type_ids)[..., None]
        residual = hidden_states
        x = rms_norm(hidden_states, ln_in_w)
        mixed = jnp.where(vm, x @ v_qkv, x @ l_qkv)
        q, k, v = jnp.split(mixed, 3, axis=-1)
        q, k, v = (heads(q, NH, HD), heads(k, NH, HD), heads(v, NH, HD))
        q, k = apply_rotary(q, k, position_ids, l)
        ctx = sdpa(q, k, v, causal=True)
        ctx = ctx.transpose(0, 2, 1, 3).reshape(b, l, H)
        attn_out = jnp.where(vm, ctx @ v_dense, ctx @ l_dense)
        hidden_states = residual + attn_out
        ci = rms_norm(hidden_states, ln_post_cross_w)
        cq = heads(ci @ cq_w, NH, CHD)
        ckv = encoder_outputs @ ckv_w
        ck, cv = jnp.split(ckv, 2, axis=-1)
        ck, cv = (heads(ck, NH, CHD), heads(cv, NH, CHD))
        cctx = sdpa(cq, ck, cv, causal=False)
        cctx = cctx.transpose(0, 2, 1, 3).reshape(b, l, CC)
        hidden_states = hidden_states + cctx @ cdense_w
        mi = rms_norm(hidden_states, ln_post_attn_w)
        v_out = jax.nn.silu(mi @ v_gate) * (mi @ v_up) @ v_down
        l_out = jax.nn.silu(mi @ l_gate) * (mi @ l_up) @ l_down
        hidden_states = hidden_states + jnp.where(vm, v_out, l_out)
        return hidden_states

    def _L2_xattn_ref(hidden_states, memory, W_mem, W_gate, b_gate, norm_w):
        import jax, jax.numpy as jnp
        import numpy as np
        EPS = 1e-06

        def _rmsnorm(x, w):
            var = jnp.mean(jnp.square(x), axis=-1, keepdims=True)
            return x * jax.lax.rsqrt(var + EPS) * w
        D = hidden_states.shape[-1]
        memory_proj = jnp.einsum('bme,de->bmd', memory, W_mem)
        scores = jnp.einsum('bnd,bmd->bnm', hidden_states, memory_proj) / jnp.sqrt(jnp.float32(D))
        attn = jax.nn.softmax(scores, axis=-1)
        memory_context = jnp.einsum('bnm,bmd->bnd', attn, memory_proj)
        gate_input = jnp.concatenate([hidden_states, memory_context], axis=-1)
        gate = jax.nn.sigmoid(jnp.einsum('bnf,df->bnd', gate_input, W_gate) + b_gate)
        fused = hidden_states + gate * memory_context
        return _rmsnorm(fused, norm_w)

    def _L3_xattn_ref(x, media, media_mask, ln_q_g, ln_q_b, Wq, Wkv, Wo, attn_gate, ln_ff_g, ln_ff_b, W1, W2, ff_gate):
        import jax, jax.numpy as jnp
        import numpy as np
        DIM = 256
        DIM_MEDIA = 128
        HEADS = 16
        DIM_HEAD = 64
        INNER = HEADS * DIM_HEAD
        FF_INNER = 4 * DIM
        B, N_TOK, N_LAT = (4, 256, 64)
        EPS = 1e-05

        def layernorm(x, g, b):
            mu = jnp.mean(x, axis=-1, keepdims=True)
            var = jnp.var(x, axis=-1, keepdims=True)
            return (x - mu) * jax.lax.rsqrt(var + EPS) * g + b
        scale = DIM_HEAD ** (-0.5)
        qn = layernorm(x, ln_q_g, ln_q_b)
        q = qn @ Wq * scale
        kv = media @ Wkv
        k, v = jnp.split(kv, 2, axis=-1)
        split_heads = lambda t: t.reshape(t.shape[0], t.shape[1], HEADS, DIM_HEAD).transpose(0, 2, 1, 3)
        q, k, v = (split_heads(q), split_heads(k), split_heads(v))
        sim = jnp.einsum('bhid,bhjd->bhij', q, k)
        neg_inf = jnp.finfo(sim.dtype).min
        sim = jnp.where(media_mask[:, None, None, :], sim, neg_inf)
        attn = jax.nn.softmax(sim, axis=-1)
        out = jnp.einsum('bhij,bhjd->bhid', attn, v)
        out = out.transpose(0, 2, 1, 3).reshape(x.shape[0], x.shape[1], INNER)
        attn_out = out @ Wo
        x = x + jnp.tanh(attn_gate) * attn_out
        h = layernorm(x, ln_ff_g, ln_ff_b)
        h = jax.nn.gelu(h @ W1, approximate=False) @ W2
        x = x + jnp.tanh(ff_gate) * h
        return x
    x = _L0_xattn_ref(x, ctx_1024, mask_BxS2_bk0, L0_xattn_ln_q_g, L0_xattn_ln_q_b, L0_xattn_Wq, L0_xattn_Wkv, L0_xattn_Wo, L0_xattn_attn_gate, L0_xattn_ln_ff_g, L0_xattn_ln_ff_b, L0_xattn_W1, L0_xattn_W2, L0_xattn_ff_gate)
    x = _L1_xattn_ref(x, ctx_1024, mask_BxS_ik0, pos_1xS, L1_xattn_ln_in_w, L1_xattn_ln_post_attn_w, L1_xattn_ln_post_cross_w, L1_xattn_v_qkv, L1_xattn_l_qkv, L1_xattn_v_dense, L1_xattn_l_dense, L1_xattn_cq_w, L1_xattn_ckv_w, L1_xattn_cdense_w, L1_xattn_v_gate, L1_xattn_v_up, L1_xattn_v_down, L1_xattn_l_gate, L1_xattn_l_up, L1_xattn_l_down)
    x = _L2_xattn_ref(x, ctx_1024, L2_xattn_W_mem, L2_xattn_W_gate, L2_xattn_b_gate, L2_xattn_norm_w)
    x = _L3_xattn_ref(x, ctx_1024, mask_BxS2_bk0, L3_xattn_ln_q_g, L3_xattn_ln_q_b, L3_xattn_Wq, L3_xattn_Wkv, L3_xattn_Wo, L3_xattn_attn_gate, L3_xattn_ln_ff_g, L3_xattn_ln_ff_b, L3_xattn_W1, L3_xattn_W2, L3_xattn_ff_gate)
    return x

_drawn_inputs = setup_inputs


def setup_inputs(seed=0):
    import zlib

    import numpy as np

    out = dict(_drawn_inputs(seed))
    spreads = {'L0_xattn_ln_q_g': (1.0, 0.6),
     'L0_xattn_ln_q_b': (0.0, 0.8),
     'L0_xattn_ln_ff_g': (1.0, 0.6),
     'L0_xattn_ln_ff_b': (0.0, 0.8),
     'L1_xattn_ln_in_w': (1.0, 0.6),
     'L1_xattn_ln_post_attn_w': (1.0, 0.6),
     'L1_xattn_ln_post_cross_w': (1.0, 0.6),
     'L2_xattn_norm_w': (1.0, 0.2),
     'L3_xattn_ln_q_g': (1.0, 0.6),
     'L3_xattn_ln_q_b': (0.0, 0.8),
     'L3_xattn_ln_ff_g': (1.0, 0.6),
     'L3_xattn_ln_ff_b': (0.0, 0.8)}
    factors = {'L0_xattn_W1': 2.695,
     'L1_xattn_v_qkv': 8.0,
     'L1_xattn_v_dense': 8.0,
     'L1_xattn_l_dense': 2.826,
     'L1_xattn_cq_w': 59.184,
     'L1_xattn_v_gate': 5.495,
     'L1_xattn_v_up': 5.456,
     'L1_xattn_v_down': 5.497,
     'L2_xattn_b_gate': 60.131,
     'L3_xattn_W1': 2.906}
    for name, (base, spread) in spreads.items():
        noise = np.random.default_rng([zlib.crc32(name.encode()), seed]).standard_normal(out[name].shape)
        drawn = base * np.exp(spread * noise) if base else spread * noise
        out[name] = jnp.asarray(drawn.astype(out[name].dtype))
    for name, factor in factors.items():
        out[name] = (out[name] * factor).astype(out[name].dtype)
    return out
```

```python
from contextlib import ExitStack

import numpy as np
import concourse.bass as bass
from concourse import mybir

F32 = mybir.dt.float32
F32R = mybir.dt.float32r
I32 = mybir.dt.int32
U8 = mybir.dt.uint8
ALU = mybir.AluOpType
ACT = mybir.ActivationFunctionType
AX_X = mybir.AxisListType.X

P = 128
B, T, D = 4, 256, 256
TT, KD = T // P, D // P
DC = 128
SLOTS = 2
ITERS = B // SLOTS
H = 16
XD, INNER = 64, 1024
KI = INNER // P
FF = 1024
SD = D // H
CD = DC // H
MLP = 688
MT = -(-MLP // P)
MLAST = MLP - (MT - 1) * P
NEG = 1.0e30
BIG = 3.0e38
LN_EPS, RMS_EPS = 1e-5, 1e-6

RINGS = {"scores": (0, 3), "probsT": (3, 2), "main": (5, 3)}
PROBS, PTS, SMALL, MASKED = 4, 8, 8, 2
LAG_T, LAG_O = 3, 5
PHASES = {0: "x", 1: "self", 2: "cross", 3: "mem", 4: "x"}


def schedule():
    order = []

    def each(kind, phase, n=1):
        for s in range(SLOTS):
            for i in range(n):
                order.append((kind, phase, s, i))

    def attention(phase, heads):
        items = [(s, h) for s in range(SLOTS) for h in range(heads)]
        batch = min(4, heads)
        for i in range(len(items) + LAG_O + batch):
            if i < len(items):
                order.append(("scores", phase, *items[i]))
            if 0 <= i - 1 < len(items):
                order.append(("probs", phase, *items[i - 1]))
            if 0 <= i - LAG_T < len(items):
                order.append(("probsT", phase, *items[i - LAG_T]))
            o = i - LAG_O
            if 0 <= o < len(items) and o % batch == batch - 1:
                order.append(("values", phase, items[o][0], items[o][1] // batch))

    each("ctxT", 0)
    for phase in (0, 4):
        if phase == 4:
            each("norm", 1)
            each("hT", 1)
            tiles = [(s, t) for s in range(SLOTS) for t in range(TT)]
            for n in range(len(tiles) + 1):
                if n < len(tiles):
                    order.append(("qk", 1, *tiles[n]))
                    order.append(("v", 1, *tiles[n]))
                    order.append(("rotary", 1, *tiles[n]))
                if n:
                    s, t = tiles[n - 1]
                    order.extend(("stackT", 1, s, 4 * t + u) for u in range(4))
            attention(1, H)
            for s in range(SLOTS):
                order.append(("out", 1, s, 0))
                order.append(("norm", 2, s, 0))
            for s in range(SLOTS):
                order.append(("ckv", 2, s, 0))
            for s in range(SLOTS):
                order.append(("ksplit", 2, s, 0))
                order.extend(("stackT", 2, s, t) for t in range(TT))
            each("hT", 2)
            each("cq", 2)
            for s in range(SLOTS):
                order.append(("qsplit", 2, s, 0))
                order.extend(("stackT", 2, s, TT + t) for t in range(TT))
            attention(2, H)
            for s in range(SLOTS):
                order.append(("out", 2, s, 0))
                order.append(("norm", 5, s, 0))
            each("mem", 3, 2)
            for s in range(SLOTS):
                order.append(("hT", 5, s, 0))
                order.extend(("gateup", 5, s, i) for i in range(MT))
            each("down", 5)
            each("hT", 3)
            attention(3, 1)
            each("mctxT", 3)
            each("mgate", 3)
            each("fuse", 3)
        each("norm", phase)
        for s in range(SLOTS):
            order.extend(("kproj", phase, s, i) for i in range(4))
            order.extend(("vproj", phase, s, i) for i in range(4))
        for s in range(SLOTS):
            order.append(("hT", phase, s, 0))
            order.extend(("qproj", phase, s, i) for i in range(4))
        attention(phase, H)
        for s in range(SLOTS):
            order.append(("out", phase, s, 0))
            order.append(("norm", phase + 6, s, 0))
        for s in range(SLOTS):
            order.append(("hT", phase + 6, s, 0))
            order.extend(("ff1", phase + 6, s, i) for i in range(4))
        each("ff2", phase + 6)
    return order


RING_OF = {"scores": "scores", "probsT": "probsT"}
NO_BANK = {"norm", "rotary", "ksplit", "qsplit", "probs", "fuse"}


def head_of(phase, i):
    kind = PHASES[phase]
    if kind == "self":
        return 8 * (i // 8) + 2 * (i % 4) + i % 8 // 4
    if kind == "cross":
        return 4 * (i % 4) + i // 4
    return i


def values_bank(phase, s, b):
    per = {"x": 1, "self": 2, "cross": 4, "mem": 1}[PHASES[phase]]
    return ("O", phase, s, b // per), b % per == 0, b % per == per - 1


def fused_layers(
    nc, x_in, ctx_in, pos_in, media_mask_in, expert_mask_in, xw, l1, l2, consts, out,
):
    order = schedule()

    unit, used, fills, filled_before = {}, {r: 0 for r in RINGS}, {}, [0] * 8
    for kind, phase, s, i in order:
        if kind in NO_BANK:
            continue
        key = (kind, phase, s, i)
        if kind == "values":
            key, opens, _ = values_bank(phase, s, i)
            if not opens:
                continue
        ring = RING_OF.get(kind, "main")
        first, banks = RINGS[ring]
        unit[key] = (first + used[ring] % banks, used[ring] // banks)
        used[ring] += 1
        if kind != "values":
            filled_before[unit[key][0]] += 1
            fills[key] = filled_before[unit[key][0]]

    nth, seen = {}, {}
    for step in order:
        seen[step[0]] = seen.get(step[0], 0) + 1
        nth[step] = seen[step[0]]

    with ExitStack() as ctx:
        top = [-(-nc.sbuf_base // 64) * 64]

        def place(name, shape, dtype=F32, at=None):
            size = int(np.prod(shape[1:])) * (1 if dtype == U8 else 4)
            offset = top[0] if at is None else at
            if at is None:
                top[0] += -(-size // 64) * 64
                assert top[0] <= nc.sbuf_usable_end, (name, top[0])
            tensor = nc.alloc_sbuf_tensor_at(name, list(shape), dtype, offset=offset)
            return tensor.ap() if hasattr(tensor, "ap") else tensor

        def region(size):
            at = top[0]
            top[0] += size
            assert top[0] <= nc.sbuf_usable_end, top[0]
            return at

        KB = 1024
        w_q = place("w_q", [P, KD, INNER])
        w_kv = place("w_kv", [P, 2 * INNER])
        w_o = place("w_o", [P, KI, D])
        w_ff = region((4 * KD * MLP + 2 * MT * D) * 4)
        w_1 = place("w_1", [P, KD, FF], at=w_ff)
        w_2 = place("w_2", [P, KI, D], at=w_ff + KD * FF * 4)
        w_gu = place("w_gu", [P, 4, KD, MLP], at=w_ff)
        w_down = place("w_down", [P, 2, MT, D], at=w_ff + 4 * KD * MLP * 4)
        w_qkv = place("w_qkv", [P, 2, KD, 3 * D])
        w_dense = place("w_dense", [P, 2, 2, D])
        w_cq = place("w_cq", [P, KD, DC])
        w_ckv = place("w_ckv", [P, 2 * DC])
        w_cdense = place("w_cdense", [P, D])
        w_gate = place("w_gate", [P, 2 * KD, D])
        w_memT = place("w_memT", [P, D])
        ident = place("ident", [P, P])
        causal = place("causal", [P, 2 * P])
        iota = place("iota", [P, TT])
        gains = place("gains", [P, 22])
        rot = place("rot", [P, TT, 2, 2, SD])
        half = place("half", [P, TT])
        gates = place("gates", [P, 4])
        gates_raw = place("gates_raw", [P, 4])
        b_gate = place("b_gate", [P, D])
        norm_w = place("norm_w", [P, D])
        expert = place("expert", [P, SLOTS, 2, T])
        media = place("media", [P, SLOTS, T])
        media_raw = place("media_raw", [P, SLOTS, T], U8)
        x, h, hT, ctxT, kmem, vmem = [], [], [], [], [], []
        qT, kT, v, g_act, qs, ks, qc, kc, vs, vc, sg, acts, slot_at = ([] for _ in range(13))
        for s in range(SLOTS):
            x.append(place(f"x{s}", [P, TT, D]))
            h.append(place(f"h{s}", [P, TT, D]))
            hT.append(place(f"hT{s}", [P, 2, KD, T]))
            ctxT.append(place(f"ctxT{s}", [P, T]))
            kmem.append(place(f"kmem{s}", [P, KD, T]))
            vmem.append(place(f"vmem{s}", [P, TT, D]))
            big = region(24 * KB)
            slot_at.append(big)
            qT.append(place(f"qT{s}", [P, KI, T], at=big))
            kT.append(place(f"kT{s}", [P, KI, T], at=big + 8 * KB))
            v.append(place(f"v{s}", [P, TT, INNER], at=big + 16 * KB))
            g_act.append(place(f"g_act{s}", [P, KI, T], at=big))
            qs.append(place(f"qs{s}", [P, 8, T], F32R, at=big))
            ks.append(place(f"ks{s}", [P, 8, T], F32R, at=big + 8 * KB))
            qc.append(place(f"qc{s}", [P, 4, T], F32R, at=big))
            kc.append(place(f"kc{s}", [P, 4, T], F32R, at=big + 8 * KB))
            vs.append(place(f"vs{s}", [P, TT, H, 32], at=big + 16 * KB))
            vc.append(place(f"vc{s}", [P, TT, H, 32], at=big + 20 * KB))
            sg.append(place(f"sg{s}", [P, MT, T], at=big))
            acts.append(place(f"acts{s}", [P, 2, MT, T], at=big + 6 * KB))
        ctx_in_sb = [h[s] for s in range(SLOTS)]
        masked = place("masked", [P, MASKED, TT, T])
        probs_at = region(PROBS * TT * T * 4)
        probs = place("probs", [P, PROBS, TT, T], at=probs_at)
        probsT_at = region(PTS * 2 * T * 4)
        probsT = place("probsT", [P, PTS, 2 * T], at=probsT_at)
        negmax = place("negmax", [P, SMALL, TT])
        sums = place("sums", [P, SMALL, TT])
        rsum = place("rsum", [P, SMALL, TT])
        stats = place("stats", [P, SLOTS, TT, 6])
        mv = place("mv", [P, SLOTS, TT, 2])
        ms = place("ms", [P, SLOTS, TT])
        rstd = place("rstd", [P, SLOTS, TT])
        q_tmp = place("q_tmp", [P, 2, H, 4, SD], at=probsT_at)
        k_tmp = place("k_tmp", [P, 2, H, 2, 2, SD], at=probsT_at + 8 * KB)
        rot_a = place("rot_a", [P, 2, H, SD], at=probs_at)
        rot_b = place("rot_b", [P, 2, H, SD], at=probs_at + 2 * KB)
        qc_tmp = place("qc_tmp", [P, TT * H, 4, CD], at=probsT_at)
        kc_tmp = place("kc_tmp", [P, TT * H, 2, 2, CD], at=probsT_at + 4 * KB)
        qc_raw = place("qc_raw", [P, TT * H, CD], at=probsT_at + 8 * KB)
        pos_raw = place("pos_raw", [P, T], I32, at=probsT_at)
        pos_f = place("pos_f", [P, T], at=probsT_at + KB)
        pos_n = place("pos_n", [P, T], at=probsT_at + 2 * KB)
        onehot = place("onehot", [P, TT, T], at=probsT_at + 3 * KB)
        rot_tab = place("rot_tab", [P, TT, 64], at=probsT_at + 5 * KB)
        wmem_raw = place("wmem_raw", [P, KD, DC], at=probsT_at + 6 * KB)
        gain_rows = place("gain_rows", [22, P], at=probsT_at + 7 * KB)
        wgate_raw = place("wgate_raw", [P, KD, 2 * D], at=probsT_at + 8 * KB)
        expert_raw = place("expert_raw", [P, SLOTS, T], I32)
        qT_at = [slot_at[s] for s in range(SLOTS)]
        mctx = [place(f"mctx{s}", [P, TT, D], at=qT_at[s]) for s in range(SLOTS)]
        mz = [place(f"mz{s}", [P, TT, D], at=qT_at[s] + 2 * KB) for s in range(SLOTS)]
        mg = [place(f"mg{s}", [P, TT, D], at=qT_at[s] + 4 * KB) for s in range(SLOTS)]

        bank = [ctx.enter_context(nc.psum_tensor(f"bank{i}", [P, 512], F32)) for i in range(8)]

        def sem(name):
            return ctx.enter_context(nc.semaphore(name))

        filled = [sem(f"bank{i}_filled") for i in range(8)]
        drained = [sem(f"bank{i}_drained") for i in range(8)]
        negmax_ready = sem("negmax_ready")
        exp_ready = sem("exp_ready")
        probs_ready = sem("probs_ready")
        values_done = sem("values_done")
        h_ready = sem("h_ready")
        var_ready = sem("var_ready")
        rstd_ready = sem("rstd_ready")
        stack_ready = sem("stack_ready")
        split_ready = sem("split_ready")
        silu_ready = sem("silu_ready")
        acts_ready = sem("acts_ready")
        mgate_exp = sem("mgate_exp")
        v_zeroed = sem("v_zeroed")
        dve_step = sem("dve_step")
        x_loaded = sem("x_loaded")
        ctx_loaded = sem("ctx_loaded")
        masks_loaded = sem("masks_loaded")
        attn3_loaded = sem("attn3_loaded")
        mlp_loaded = sem("mlp_loaded")
        ff3_loaded = sem("ff3_loaded")
        out_stored = sem("out_stored")
        engines_done = sem("engines_done")
        per_iteration = [s.num for s in (
            *filled, *drained, negmax_ready, exp_ready, probs_ready, values_done, h_ready, var_ready,
            rstd_ready, stack_ready, split_ready, silu_ready, acts_ready, mgate_exp, v_zeroed, dve_step,
            x_loaded, ctx_loaded, masks_loaded, attn3_loaded, mlp_loaded,
            ff3_loaded, out_stored, engines_done)]
        assert per_iteration == list(range(per_iteration[0], per_iteration[0] + len(per_iteration)))
        iteration_open = sem("iteration_open")
        attn0_loaded = sem("attn0_loaded")
        ff0_loaded = sem("ff0_loaded")
        l1_loaded = sem("l1_loaded")
        params_loaded = sem("params_loaded")
        setup_pe = sem("setup_pe")
        setup_dve = sem("setup_dve")
        setup_act = sem("setup_act")
        setup_pool = sem("setup_pool")
        setup_step = sem("setup_step")

        ATTN_DMAS, FF_DMAS, MLP_DMAS, L1_DMAS, PARAM_DMAS = 3, 2, 4 + 2 * 2, 7, 7 + 11 + 4 + 2

        GAIN = {0: 0, 6: 4, 4: 8, 10: 12, 1: 16, 5: 18, 2: 20}

        def bank_of(key):
            return bank[unit[key][0]]

        def wait_filled(eng, key):
            eng.wait_ge(filled[unit[key][0]], fills[key])

        def wait_drained(eng, key):
            b, n = unit[key]
            eng.wait_ge(drained[b], n + 1)

        def wait_free(pe, key):
            b, n = unit[key]
            if n:
                pe.wait_ge(drained[b], n)

        unit_kinds_act = {"ctxT", "kproj", "qproj", "ff1", "v", "stackT", "mem", "gateup", "mctxT"}

        def heads_of(phase):
            return 1 if PHASES[phase] == "mem" else H

        def head_no(phase, s, hd):
            return nth[("scores", phase, s, hd)] - 1

        def by_no():
            return {head_no(p_, s_, i_): (p_, s_, i_) for k_, p_, s_, i_ in order if k_ == "scores"}

        head_at = by_no()
        split_no = {step: n + 1 for n, step in enumerate(st for st in order if st[0] in ("ksplit", "qsplit"))}
        root_no = {step: n + 1 for n, step in enumerate(st for st in order if st[0] in ("norm", "fuse"))}

        block = ctx.enter_context(nc.Block())

        @block.sync
        def _(sp):
            def load_attention(layer, done):
                sp.dma_start(w_kv[:, :], xw[layer]["Wkv"]).then_inc(done, 16)
                sp.dma_start(w_q[:, :, :], xw[layer]["Wq"].rearrange("(k p) n -> p k n", p=P)).then_inc(done, 16)
                sp.dma_start(w_o[:, :, :], xw[layer]["Wo"].rearrange("(k p) n -> p k n", p=P)).then_inc(done, 16)

            def load_ff(layer, done):
                sp.dma_start(w_1[:, :, :], xw[layer]["W1"].rearrange("(k p) n -> p k n", p=P)).then_inc(done, 16)
                sp.dma_start(w_2[:, :, :], xw[layer]["W2"].rearrange("(k p) n -> p k n", p=P)).then_inc(done, 16)

            def load_mlp(done):
                for n, w in enumerate(("v_gate", "l_gate", "v_up", "l_up")):
                    sp.dma_start(w_gu[:, n, :, :], l1[w].rearrange("(k p) n -> p k n", p=P)).then_inc(done, 16)
                for n, w in enumerate(("v_down", "l_down")):
                    full = (MT - 1) * P
                    sp.dma_start(w_down[:, n, 0:MT - 1, :],
                                 l1[w][0:full, :].rearrange("(k p) n -> p k n", p=P)).then_inc(done, 16)
                    sp.dma_start(w_down[0:MLAST, n, MT - 1, :], l1[w][full:MLP, :]).then_inc(done, 16)

            sp.dma_start(ident[:, :], consts["ident"]).then_inc(params_loaded, 16)
            sp.dma_start(causal[:, :], consts["causal"]).then_inc(params_loaded, 16)
            sp.dma_start(iota[:, :], consts["iota"]).then_inc(params_loaded, 16)
            sp.dma_start(rot_tab[:, :, :], consts["rot"].rearrange("(k p) n -> p k n", p=P)).then_inc(params_loaded, 16)
            sp.dma_start(pos_raw[:, :], pos_in.partition_broadcast(P).rearrange("p a t -> p (a t)")).then_inc(params_loaded, 16)
            sp.dma_start(wmem_raw[:, :, :], l2["W_mem"].rearrange("(k p) n -> p k n", p=P)).then_inc(params_loaded, 16)
            sp.dma_start(wgate_raw[:, :, :], l2["W_gate"].rearrange("(k p) n -> p k n", p=P)).then_inc(params_loaded, 16)
            for n, g in enumerate((xw[0]["ln_q_g"], xw[0]["ln_q_b"], xw[0]["ln_ff_g"], xw[0]["ln_ff_b"],
                                   xw[3]["ln_q_g"], xw[3]["ln_q_b"], xw[3]["ln_ff_g"], xw[3]["ln_ff_b"],
                                   l1["ln_in_w"], l1["ln_post_attn_w"], l1["ln_post_cross_w"])):
                sp.dma_start(gain_rows[2 * n:2 * n + 2, :], g.rearrange("(k p) -> k p", p=P)).then_inc(params_loaded, 16)
            for n, g in enumerate((xw[0]["attn_gate"], xw[0]["ff_gate"], xw[3]["attn_gate"], xw[3]["ff_gate"])):
                sp.dma_start(gates_raw[:, n:n + 1], g.partition_broadcast(P)).then_inc(params_loaded, 16)
            sp.dma_start(b_gate[:, :], l2["b_gate"].partition_broadcast(P)).then_inc(params_loaded, 16)
            sp.dma_start(norm_w[:, :], l2["norm_w"].partition_broadcast(P)).then_inc(params_loaded, 16)

            with sp.Fori(0, ITERS) as it:
                for s in range(SLOTS):
                    sp.dma_start(ctx_in_sb[s][:, :, 0:DC],
                                 ctx_in[it * SLOTS + s].rearrange("(t p) d -> p t d", p=P)).then_inc(ctx_loaded, 16)
                for s in range(SLOTS):
                    sp.dma_start(x[s][:, :, :],
                                 x_in[it * SLOTS + s].rearrange("(t p) d -> p t d", p=P)).then_inc(x_loaded, 16)
                for s in range(SLOTS):
                    sp.dma_start(media_raw[:, s, :], media_mask_in[it * SLOTS + s].partition_broadcast(P)).then_inc(masks_loaded, 16)
                    sp.dma_start(expert_raw[:, s, :], expert_mask_in[it * SLOTS + s].partition_broadcast(P)).then_inc(masks_loaded, 16)
                wait_filled(sp, ("out", 0, SLOTS - 1, 0))
                load_attention(3, attn3_loaded)
                wait_filled(sp, ("ff2", 6, SLOTS - 1, 0))
                load_mlp(mlp_loaded)
                wait_filled(sp, ("down", 5, SLOTS - 1, 0))
                load_ff(3, ff3_loaded)
                wait_filled(sp, ("out", 4, SLOTS - 1, 0))
                load_attention(0, attn0_loaded)
                wait_filled(sp, ("ff2", 10, SLOTS - 1, 0))
                load_ff(0, ff0_loaded)
                for s in range(SLOTS):
                    wait_drained(sp, ("ff2", 10, s, 0))
                    sp.dma_start(out[it * SLOTS + s].rearrange("(t p) d -> p t d", p=P), x[s][:, :, :]).then_inc(out_stored, 16)
                sp.wait_ge(out_stored, 16 * SLOTS)
                sp.wait_ge(engines_done, 4)
                sp.sem_clear(range(per_iteration[0], per_iteration[-1] + 1))
                sp.sem_inc(iteration_open, 1)
            sp.wait_ge(attn0_loaded, 16 * ATTN_DMAS * (ITERS + 1))
            sp.wait_ge(ff0_loaded, 16 * FF_DMAS * (ITERS + 1))

        @block.tensor
        def _(pe):
            mm, tr = nc.tensor.matmul, nc.tensor.transpose

            pe.wait_ge(params_loaded, 16 * PARAM_DMAS)
            tr(bank[5][:, 0:22], gain_rows[:, :], ident[0:22, 0:22])
            for k in range(KD):
                tr(bank[5][:, 128 + 128 * k:256 + 128 * k], wmem_raw[:, k, :], ident[:, :])
            for f in range(2 * KD):
                for k in range(KD):
                    last = tr(bank[3 + f // 2][:, D * (f % 2) + P * k:D * (f % 2) + P * k + P],
                              wgate_raw[:, k, P * f:P * f + P], ident[:, :])
            last.then_inc(setup_pe, 1)
            pe.wait_ge(setup_dve, 1)
            for t in range(TT):
                for k in range(TT):
                    last = mm(bank[6][:, 64 * t:64 * t + 64], onehot[:, k, t * P:(t + 1) * P], rot_tab[:, k, :],
                              start=(k == 0), stop=(k == TT - 1))
            last.then_inc(setup_pe, 1)
            pe.wait_ge(setup_dve, 2)
            pe.wait_ge(setup_act, 1)

            def scores(phase, s, hd):
                key, n = ("scores", phase, s, hd), head_no(phase, s, hd)
                if n >= RINGS["scores"][1]:
                    before = n - RINGS["scores"][1]
                    taken = negmax_ready if PHASES[head_at[before][0]] in ("x", "self") else exp_ready
                    pe.wait_ge(taken, before + 1)
                S = bank_of(key)[:, :].rearrange("p (t k) -> p t k", t=TT)
                kind = PHASES[phase]
                if kind == "x":
                    if hd % 4 == 0:
                        wait_drained(pe, ("qproj", phase, s, hd // 4))
                        wait_drained(pe, ("kproj", phase, s, hd // 4))
                    j, r = hd // 2, slice(XD * (hd % 2), XD * (hd % 2) + XD)
                    for t in range(TT):
                        last = mm(S[:, t, :], qT[s][r, j, t * P:(t + 1) * P], kT[s][r, j, :], start=True, stop=True)
                elif kind == "self":
                    if hd == 0:
                        for u in range(8):
                            wait_drained(pe, ("stackT", phase, s, u))
                    head = head_of(phase, hd)
                    j, r = head // 2, slice(64 * (head % 2), 64 * (head % 2) + 64)
                    for t in range(TT):
                        n = (t + 1) * P
                        last = mm(S[:, t, 0:n], qs[s][r, j, t * P:(t + 1) * P], ks[s][r, j, 0:n], start=True, stop=True)
                elif kind == "cross":
                    if hd == 0:
                        for u in range(2 * TT):
                            wait_drained(pe, ("stackT", phase, s, u))
                    head = head_of(phase, hd)
                    j, r = head // 4, slice(32 * (head % 4), 32 * (head % 4) + 32)
                    for t in range(TT):
                        last = mm(S[:, t, :], qc[s][r, j, t * P:(t + 1) * P], kc[s][r, j, :], start=True, stop=True,
                                  tile_position=(32 * (head % 4), 0))
                else:
                    wait_drained(pe, ("hT", 3, s, 0))
                    wait_drained(pe, ("mem", 3, s, 0))
                    for t in range(TT):
                        for k in range(KD):
                            last = mm(S[:, t, :], hT[s][:, 0, k, t * P:(t + 1) * P], kmem[s][:, k, :],
                                      start=(k == 0), stop=(k == KD - 1))
                last.then_inc(filled[unit[key][0]], 1)

            def probs_transposed(phase, s, hd):
                key, n = ("probsT", phase, s, hd), head_no(phase, s, hd)
                wait_free(pe, key)
                pe.wait_ge(probs_ready, nth[("probs", phase, s, hd)])
                PT = bank_of(key)
                for t in range(TT):
                    for k in range(TT):
                        if PHASES[phase] == "self":
                            if k > t:
                                continue
                            at = t * P if k == 0 else 2 * P
                        else:
                            at = k * T + t * P
                        last = tr(PT[:, at:at + P], probs[:, n % PROBS, t, k * P:(k + 1) * P], ident[:, :])
                last.then_inc(filled[unit[key][0]], 1)

            def values(phase, s, b):
                kind = PHASES[phase]
                key, opens, closes = values_bank(phase, s, b)
                if opens:
                    wait_free(pe, key)
                O = bank_of(key)
                heads = [0] if kind == "mem" else [4 * b + a for a in range(4)]
                if b == 0:
                    if kind == "x":
                        for u in range(4):
                            wait_drained(pe, ("vproj", phase, s, u))
                    elif kind == "self":
                        for t in range(TT):
                            wait_drained(pe, ("v", 1, s, t))
                    elif kind == "cross":
                        wait_drained(pe, ("ckv", 2, s, 0))
                    else:
                        wait_drained(pe, ("mem", 3, s, 1))
                for hd in heads:
                    wait_drained(pe, ("probsT", phase, s, hd))
                if kind == "mem":
                    pt = probsT[:, head_no(phase, s, 0) % PTS, :].rearrange("p (k q) -> p k q", k=TT)
                    for t in range(TT):
                        for k in range(TT):
                            last = mm(O[:, t * D:(t + 1) * D], pt[:, k, t * P:(t + 1) * P], vmem[s][:, k, :],
                                      start=(k == 0), stop=(k == TT - 1))
                    last.then_inc(values_done, 1)
                    return
                for pair in ([0, 1], [2, 3]) if kind == "x" else ([0, 1, 2, 3],):
                    for k in range(TT):
                        for a in pair:
                            hd = heads[a]
                            pt = probsT[:, head_no(phase, s, hd) % PTS, :]
                            if kind == "x":
                                last = mm(O[XD * (a % 2):XD * (a % 2) + XD, T * (a // 2):T * (a // 2) + T],
                                          v[s][:, k, hd * XD:(hd + 1) * XD], pt[:, k * T:(k + 1) * T],
                                          start=(k == 0), stop=(k == TT - 1))
                            elif kind == "self":
                                first, final = b % 2 == 0 and k == 0, b % 2 == 1 and k == TT - 1
                                q0 = k * P
                                last = mm(O[32 * a:32 * a + 32, q0:T], vs[s][:, k, head_of(phase, hd), :],
                                          pt[:, k * T:k * T + T - q0], start=first, stop=final,
                                          tile_position=(0, 32 * a))
                            else:
                                first, final = b == 0 and k == 0, b == 3 and k == TT - 1
                                last = mm(O[32 * a:32 * a + 32, 0:T], vc[s][:, k, head_of(phase, hd), :],
                                          pt[:, k * T:(k + 1) * T], start=first, stop=final,
                                          tile_position=(0, 32 * a))
                last.then_inc(values_done, 1)

            def products(key, pieces):
                wait_free(pe, key)
                for cols, terms in pieces:
                    rows = terms[0][0].shape[-1]
                    for n, (stationary, moving) in enumerate(terms):
                        last = mm(bank_of(key)[0:rows, cols], stationary, moving,
                                  start=(n == 0), stop=(n == len(terms) - 1))
                last.then_inc(filled[unit[key][0]], 1)

            def turn(key, tiles):
                wait_free(pe, key)
                for n, tile in enumerate(tiles):
                    last = tr(bank_of(key)[:, n * P:(n + 1) * P], tile, ident[:, :])
                last.then_inc(filled[unit[key][0]], 1)

            tok = lambda t: slice(t * P, (t + 1) * P)
            wide = lambda t: slice(t * T, (t + 1) * T)

            with pe.Fori(0, ITERS) as it:
                for step in order:
                    kind, phase, s, i = step
                    if kind == "scores":
                        scores(phase, s, i)
                    elif kind == "probsT":
                        probs_transposed(phase, s, i)
                    elif kind == "values":
                        values(phase, s, i)
                    elif kind == "ctxT":
                        if s == 0:
                            pe.wait_ge(ctx_loaded, 16 * SLOTS)
                        turn(step, [ctx_in_sb[s][:, t, 0:DC] for t in range(TT)])
                    elif kind == "hT":
                        if phase == 3:
                            wait_drained(pe, ("down", 5, s, 0))
                            src = x[s]
                        else:
                            pe.wait_ge(h_ready, nth[("norm", phase, s, 0)])
                            src = h[s]
                        turn(step, [src[:, t, tok(k)] for k in range(KD) for t in range(TT)])
                    elif kind == "mctxT":
                        wait_drained(pe, ("O", 3, s, 0))
                        turn(step, [mctx[s][:, t, tok(k)] for k in range(KD) for t in range(TT)])
                    elif kind == "kproj":
                        if s == 0 and i == 0:
                            wait_drained(pe, ("ctxT", 0, SLOTS - 1, 0))
                            if phase == 0:
                                pe.wait_ge(attn0_loaded, it * (16 * ATTN_DMAS) + 16 * ATTN_DMAS)
                            else:
                                pe.wait_ge(attn3_loaded, 16 * ATTN_DMAS)
                        products(step, [(wide(n), [(w_kv[:, tok(2 * i + n)], ctxT[s][:, :])]) for n in range(2)])
                    elif kind == "vproj":
                        t, c = i // 2, i % 2
                        products(step, [(slice(0, 512), [(ctxT[s][:, tok(t)], w_kv[:, INNER + 512 * c:INNER + 512 * c + 512])])])
                    elif kind == "qproj":
                        if i == 0:
                            wait_drained(pe, ("hT", phase, s, 0))
                        products(step, [(wide(n), [(w_q[:, k, tok(2 * i + n)], hT[s][:, 0, k, :]) for k in range(KD)])
                                        for n in range(2)])
                    elif kind == "out" and PHASES[phase] == "x":
                        for b in range(4):
                            wait_drained(pe, ("O", phase, s, b))
                        products(step, [(wide(t), [(qT[s][:, k, tok(t)], w_o[:, k, :]) for k in range(KI)])
                                        for t in range(TT)])
                    elif kind == "ff1":
                        if i == 0:
                            wait_drained(pe, ("hT", phase, s, 0))
                            if s == 0:
                                if phase == 6:
                                    pe.wait_ge(ff0_loaded, it * (16 * FF_DMAS) + 16 * FF_DMAS)
                                else:
                                    pe.wait_ge(ff3_loaded, 16 * FF_DMAS)
                        products(step, [(wide(n), [(w_1[:, k, tok(2 * i + n)], hT[s][:, 0, k, :]) for k in range(KD)])
                                        for n in range(2)])
                    elif kind == "ff2":
                        for u in range(4):
                            wait_drained(pe, ("ff1", phase, s, u))
                        products(step, [(wide(t), [(g_act[s][:, k, tok(t)], w_2[:, k, :]) for k in range(KI)])
                                        for t in range(TT)])
                    elif kind == "qk":
                        if i == 0:
                            wait_drained(pe, ("hT", 1, s, 0))
                            if s == 0:
                                pe.wait_ge(l1_loaded, 16 * L1_DMAS)
                        products(step, [(slice(0, 512), [(hT[s][:, e, k, tok(i)], w_qkv[:, e, k, 0:512])
                                                         for e in range(2) for k in range(KD)])])
                    elif kind == "v":
                        products(step, [(slice(0, 256), [(hT[s][:, e, k, tok(i)], w_qkv[:, e, k, 512:768])
                                                         for e in range(2) for k in range(KD)])])
                    elif kind == "stackT":
                        if phase == 1:
                            t, u = i // 4, i % 4
                            if u == 0:
                                pe.wait_ge(stack_ready, nth[("rotary", 1, s, t)])
                            buf = (s * TT + t) % 2
                            if u < 2:
                                tiles = [q_tmp[:, buf, 8 * u + 2 * j:8 * u + 2 * j + 2, :, :] for j in range(4)]
                            else:
                                tiles = [k_tmp[:, buf, 8 * (u - 2) + 2 * j:8 * (u - 2) + 2 * j + 2, :, :, :] for j in range(4)]
                        else:
                            t, which = i % TT, i // TT
                            if t == 0:
                                pe.wait_ge(split_ready, split_no[("ksplit", "qsplit")[which], 2, s, 0])
                            if which == 0:
                                tiles = [kc_tmp[:, H * t + 4 * j:H * t + 4 * j + 4, :, :, :] for j in range(4)]
                            else:
                                tiles = [qc_tmp[:, H * t + 4 * j:H * t + 4 * j + 4, :, :] for j in range(4)]
                        turn(step, tiles)
                    elif kind == "out" and phase == 1:
                        for g in range(2):
                            wait_drained(pe, ("O", 1, s, g))
                        products(step, [(wide(t), [(hT[s][:, e, g, tok(t)], w_dense[:, e, g, :])
                                                   for e in range(2) for g in range(2)]) for t in range(TT)])
                    elif kind == "ckv":
                        products(step, [(wide(t), [(ctxT[s][:, tok(t)], w_ckv[:, :])]) for t in range(TT)])
                    elif kind == "cq":
                        wait_drained(pe, ("hT", 2, s, 0))
                        products(step, [(tok(t), [(hT[s][:, 0, k, tok(t)], w_cq[:, k, :]) for k in range(KD)])
                                        for t in range(TT)])
                    elif kind == "out" and phase == 2:
                        wait_drained(pe, ("O", 2, s, 0))
                        products(step, [(wide(t), [(hT[s][:, 1, 0, tok(t)], w_cdense[:, :])]) for t in range(TT)])
                    elif kind == "gateup":
                        if i == 0:
                            wait_drained(pe, ("hT", 5, s, 0))
                            if s == 0:
                                pe.wait_ge(mlp_loaded, 16 * MLP_DMAS)
                        cols = slice(i * P, min(MLP, (i + 1) * P))
                        products(step, [(wide(n), [(w_gu[:, 2 * n + e, k, cols], hT[s][:, e, k, :])
                                                   for e in range(2) for k in range(KD)]) for n in range(2)])
                    elif kind == "down":
                        pe.wait_ge(acts_ready, nth[("gateup", 5, s, MT - 1)])
                        rows = [slice(0, P if m < MT - 1 else MLAST) for m in range(MT)]
                        products(step, [(wide(t), [(acts[s][rows[m], e, m, tok(t)], w_down[rows[m], e, m, :])
                                                   for m in range(MT) for e in range(2)]) for t in range(TT)])
                    elif kind == "mem":
                        if i == 0:
                            products(step, [(wide(k), [(w_memT[:, tok(k)], ctxT[s][:, :])]) for k in range(KD)])
                        else:
                            products(step, [(wide(t), [(ctxT[s][:, tok(t)], w_memT[:, :])]) for t in range(TT)])
                    elif kind == "mgate":
                        wait_drained(pe, ("mctxT", 3, s, 0))
                        products(step, [(wide(t), [(hT[s][:, e, k, tok(t)], w_gate[:, 2 * e + k, :])
                                                   for e in range(2) for k in range(KD)]) for t in range(TT)])
                pe.drain().then_inc(engines_done, 1)
                pe.wait_ge(iteration_open, it + 1)

        @block.scalar
        def _(act):
            def copy(dst, src, scale=1.0):
                return nc.scalar.activation(dst, src, ACT.Copy, scale=scale)

            def by_k(w):
                return w.rearrange("(k p) n -> p k n", p=P)

            act.dma_start(w_kv[:, :], xw[0]["Wkv"]).then_inc(attn0_loaded, 16)
            act.dma_start(w_q[:, :, :], by_k(xw[0]["Wq"])).then_inc(attn0_loaded, 16)
            act.dma_start(w_o[:, :, :], by_k(xw[0]["Wo"])).then_inc(attn0_loaded, 16)
            act.dma_start(w_1[:, :, :], by_k(xw[0]["W1"])).then_inc(ff0_loaded, 16)
            act.dma_start(w_2[:, :, :], by_k(xw[0]["W2"])).then_inc(ff0_loaded, 16)
            for e, w in enumerate(("v_qkv", "l_qkv")):
                act.dma_start(w_qkv[:, e, :, :], by_k(l1[w])).then_inc(l1_loaded, 16)
            for e, w in enumerate(("v_dense", "l_dense")):
                act.dma_start(w_dense[:, e, :, :], by_k(l1[w])).then_inc(l1_loaded, 16)
            act.dma_start(w_cq[:, :, :], by_k(l1["cq_w"])).then_inc(l1_loaded, 16)
            act.dma_start(w_ckv[:, :], l1["ckv_w"]).then_inc(l1_loaded, 16)
            act.dma_start(w_cdense[:, :], l1["cdense_w"]).then_inc(l1_loaded, 16)

            act.wait_ge(params_loaded, 16 * PARAM_DMAS)
            nc.scalar.activation(gates[:, :], gates_raw[:, :], ACT.Tanh).then_inc(setup_act, 1)

            with act.Fori(0, ITERS) as it:
                for step in order:
                    kind, phase, s, i = step
                    if kind in unit_kinds_act or (kind == "hT" and phase == 3):
                        wait_filled(act, step)
                        src = bank_of(step)
                        free = drained[unit[step][0]]
                    if kind == "ctxT":
                        copy(ctxT[s][:, :], src[:, 0:T]).then_inc(free, 1)
                    elif kind == "hT" and phase == 3:
                        copy(hT[s][:, 0, :, :], src[:, :].rearrange("p (k t) -> p k t", k=KD)).then_inc(free, 1)
                    elif kind == "mctxT":
                        copy(hT[s][:, 1, :, :], src[:, :].rearrange("p (k t) -> p k t", k=KD)).then_inc(free, 1)
                    elif kind == "kproj":
                        copy(kT[s][:, 2 * i:2 * i + 2, :], src[:, :].rearrange("p (k t) -> p k t", k=2)).then_inc(free, 1)
                    elif kind == "qproj":
                        copy(qT[s][:, 2 * i:2 * i + 2, :], src[:, :].rearrange("p (k t) -> p k t", k=2),
                             -float(XD) ** -0.5).then_inc(free, 1)
                    elif kind == "ff1":
                        nc.scalar.activation(g_act[s][:, 2 * i:2 * i + 2, :], src[:, :].rearrange("p (k t) -> p k t", k=2),
                                             ACT.Gelu).then_inc(free, 1)
                    elif kind == "v":
                        if i == 0:
                            act.wait_ge(v_zeroed, 2 * s + 1)
                        pairs = vs[s][:, i, :, :].rearrange("p (j c) d -> p j (c d)", c=2)
                        halves = src[:, 0:D].rearrange("p (j c d) -> p j c d", c=2, d=SD)
                        copy(pairs[:, :, 0:SD], halves[:, :, 0, :])
                        copy(pairs[:, :, 3 * SD:4 * SD], halves[:, :, 1, :]).then_inc(free, 1)
                    elif kind == "stackT":
                        block4 = src[:, :].rearrange("p (j q) -> p j q", j=4)
                        if phase == 1:
                            t, u = i // 4, i % 4
                            dst = (qs if u < 2 else ks)[s][:, 4 * (u % 2):4 * (u % 2) + 4, t * P:(t + 1) * P]
                        else:
                            t = i % TT
                            dst = (kc if i < TT else qc)[s][:, :, t * P:(t + 1) * P]
                        copy(dst, block4).then_inc(free, 1)
                    elif kind == "mem":
                        copy((kmem, vmem)[i][s][:, :, :], src[:, :].rearrange("p (k t) -> p k t", k=2),
                             (float(D) ** -0.5, 1.0)[i]).then_inc(free, 1)
                    elif kind == "gateup":
                        rows = slice(0, P if i < MT - 1 else MLAST)
                        nc.scalar.activation(sg[s][rows, i, :], src[rows, 0:T], ACT.Silu).then_inc(silu_ready, 1)
                    elif kind == "probs":
                        what, n = PHASES[phase], head_no(phase, s, i)
                        key = ("scores", phase, s, i)
                        act.wait_ge(negmax_ready, n + 1)
                        if n >= PROBS:
                            wait_filled(act, ("probsT", *head_at[n - PROBS]))
                        if n >= SMALL:
                            act.wait_ge(probs_ready, n - SMALL + 1)
                        for t in range(TT):
                            cols = (t + 1) * P if what == "self" else T
                            if what in ("x", "self"):
                                scores, sign = masked[:, n % MASKED, t, 0:cols], -1.0
                            else:
                                scores, sign = bank_of(key)[:, t * T:t * T + cols], 1.0
                            last = nc.scalar.activation(probs[:, n % PROBS, t, 0:cols], scores, ACT.Exp,
                                                        bias=negmax[:, n % SMALL, t:t + 1], scale=sign,
                                                        accum_out=sums[:, n % SMALL, t:t + 1])
                        last.then_inc(exp_ready, 1)
                    elif kind == "probsT":
                        n, cols = head_no(phase, s, i), 3 * P if PHASES[phase] == "self" else 2 * T
                        if n >= PTS:
                            p_, s_, i_ = head_at[n - PTS]
                            act.wait_ge(values_done, nth[("values", p_, s_, i_ // min(4, heads_of(p_)))])
                        wait_filled(act, step)
                        copy(probsT[:, n % PTS, 0:cols], bank_of(step)[:, 0:cols]).then_inc(drained[unit[step][0]], 1)
                    elif kind == "mgate":
                        wait_drained(act, step)
                        nc.scalar.activation(mg[s][:, :, :], mz[s][:, :, :], ACT.Exp, scale=-1.0).then_inc(mgate_exp, 1)
                act.drain().then_inc(engines_done, 1)
                act.wait_ge(iteration_open, it + 1)

        @block.gpsimd
        def _(pool):
            nc.gpsimd.memset(half[:, :], -0.5).then_inc(setup_pool, 1)
            pool.wait_ge(setup_pool, 1)
            with pool.Fori(0, ITERS) as it:
                for step in order:
                    kind, phase, s, i = step
                    if kind in ("norm", "fuse"):
                        pool.wait_ge(var_ready, root_no[step])
                        nc.gpsimd.tensor_tensor(rstd[:, s, :], ms[:, s, :], half[:, :], ALU.pow).then_inc(rstd_ready, 1)
                    elif kind == "values" and phase == 0 and i == 3:
                        pool.wait_ge(values_done, nth[step])
                        nc.gpsimd.memset(vs[s][:, :, :, :], 0.0).then_inc(v_zeroed, 1)
                        nc.gpsimd.memset(vc[s][:, :, :, :], 0.0).then_inc(v_zeroed, 1)
                pool.drain().then_inc(engines_done, 1)
                pool.wait_ge(iteration_open, it + 1)

        @block.vector
        def _(dve):
            steps = [0]

            def then(ins):
                steps[0] += 1
                ins.then_inc(dve_step, 1)
                dve.wait_ge(dve_step, steps[0])

            def setup_then(ins):
                setup[0] += 1
                ins.then_inc(setup_step, 1)
                dve.wait_ge(setup_step, setup[0])

            ts, tt, copy = nc.vector.tensor_scalar, nc.vector.tensor_tensor, nc.vector.tensor_copy
            stt = nc.vector.scalar_tensor_tensor
            setup = [0]

            dve.wait_ge(params_loaded, 16 * PARAM_DMAS)
            setup_then(copy(pos_f[:, :], pos_raw[:, :]))
            setup_then(ts(pos_n[:, :], pos_f[:, :], 0.0, float(T), ALU.is_lt, ALU.mult))
            setup_then(tt(pos_f[:, :], pos_f[:, :], pos_n[:, :], ALU.add))
            setup_then(ts(pos_n[:, :], pos_f[:, :], 0.0, float(T - 1), ALU.max, ALU.min))
            for k in range(TT):
                last = ts(onehot[:, k, :], pos_n[:, :], iota[:, k:k + 1], None, ALU.is_equal)
            last.then_inc(setup_dve, 1)
            dve.wait_ge(setup_pe, 2)
            for f in range(2):
                copy(w_gate[:, 2 * f:2 * f + 2, :], bank[3 + f][:, :].rearrange("p (k d) -> p k d", k=2))
            copy(gains[:, :], bank[5][:, 0:22])
            copy(w_memT[:, :], bank[5][:, 128:384])
            copy(rot[:, :, :, :, :].rearrange("p t a b d -> p (t a b d)"), bank[6][:, 0:128]).then_inc(setup_dve, 1)
            dve.wait_ge(setup_dve, 2)
            dve.wait_ge(setup_act, 1)

            def root(s, step, mean_square):
                for t in range(TT):
                    last = nc.vector.bn_aggr(mv[:, s, t, :], stats[:, s, t, :])
                then(last)
                if mean_square:
                    then(tt(ms[:, s, :], mv[:, s, :, 0], mv[:, s, :, 0], ALU.mult))
                    stt(out=ms[:, s, :], in0=ms[:, s, :], scalar=RMS_EPS, in1=mv[:, s, :, 1],
                        op0=ALU.add, op1=ALU.add).then_inc(var_ready, 1)
                else:
                    ts(ms[:, s, :], mv[:, s, :, 1], LN_EPS, None, ALU.add).then_inc(var_ready, 1)
                dve.wait_ge(rstd_ready, root_no[step])

            def statistics(s, src):
                for t in range(TT):
                    last = nc.vector.bn_stats(stats[:, s, t, :], src[:, t, :])
                then(last)

            BEFORE_NORM = {1: ("ff2", 6), 2: ("out", 1), 5: ("out", 2), 6: ("out", 0), 10: ("out", 4)}

            with dve.Fori(0, ITERS) as it:
                dve.wait_ge(masks_loaded, 16 * 2 * SLOTS)
                ts(media[:, :, :], media_raw[:, :, :], 0.0, NEG, ALU.is_equal, ALU.mult)
                eq = masked[:, 0, :, :]
                then(ts(eq, expert_raw[:, :, :], 1.0, None, ALU.is_equal))
                tt(expert[:, :, 0, 0:T - 1], eq[:, :, 0:T - 1], eq[:, :, 1:T], ALU.mult)
                then(nc.vector.memset(expert[:, :, 0, T - 1:T], 0.0))
                then(ts(expert[:, :, 1, :], expert[:, :, 0, :], -1.0, 1.0, ALU.mult, ALU.add))
                for step in order:
                    kind, phase, s, i = step
                    what = PHASES.get(phase)
                    if kind in ("out", "vproj", "hT", "qk", "ff2", "gateup", "down", "ckv", "cq", "mgate") and phase != 3 or kind == "mgate":
                        src = bank_of(step)
                        free = drained[unit[step][0]]
                    if kind == "norm":
                        if phase == 0:
                            if s == 0:
                                dve.wait_ge(x_loaded, 16 * SLOTS)
                            wait_drained(dve, ("ctxT", 0, s, 0))
                        elif phase in BEFORE_NORM:
                            wait_drained(dve, (*BEFORE_NORM[phase], s, 0))
                        rms = phase in (1, 2, 5)
                        statistics(s, x[s])
                        root(s, step, rms)
                        for t in range(TT):
                            if rms:
                                last = ts(h[s][:, t, :], x[s][:, t, :], rstd[:, s, t:t + 1], None, ALU.mult)
                            else:
                                last = ts(h[s][:, t, :], x[s][:, t, :], mv[:, s, t, 0:1], rstd[:, s, t:t + 1],
                                          ALU.subtract, ALU.mult)
                        last.then_inc(h_ready, 1)
                    elif kind == "hT" and phase != 3:
                        wait_filled(dve, step)
                        for k in range(KD):
                            c, cols = GAIN[phase] + k, slice(k * T, (k + 1) * T)
                            if phase in (1, 5):
                                for e in range(2):
                                    last = stt(out=hT[s][:, e, k, :], in0=src[:, cols], scalar=gains[:, c:c + 1],
                                               in1=expert[:, s, e, :], op0=ALU.mult, op1=ALU.mult)
                            elif phase == 2:
                                last = ts(hT[s][:, 0, k, :], src[:, cols], gains[:, c:c + 1], None, ALU.mult)
                            else:
                                last = ts(hT[s][:, 0, k, :], src[:, cols], gains[:, c:c + 1],
                                          gains[:, c + KD:c + KD + 1], ALU.mult, ALU.add)
                        last.then_inc(free, 1)
                    elif kind == "vproj":
                        wait_filled(dve, step)
                        t, c = i // 2, i % 2
                        copy(v[s][:, t, 512 * c:512 * c + 512], src[:, :]).then_inc(free, 1)
                    elif kind == "scores":
                        n = head_no(phase, s, i)
                        wait_filled(dve, step)
                        if n >= SMALL:
                            dve.wait_ge(exp_ready, n - SMALL + 1)
                        if what in ("x", "self"):
                            if n >= MASKED:
                                dve.wait_ge(exp_ready, n - MASKED + 1)
                            for t in range(TT):
                                if what == "x":
                                    cols, mask = T, media[:, s, :]
                                else:
                                    cols, mask = (t + 1) * P, causal[:, (TT - 1 - t) * P:TT * P]
                                last = nc.vector.tensor_tensor_reduce(
                                    out=masked[:, n % MASKED, t, 0:cols], in0=bank_of(step)[:, t * T:t * T + cols],
                                    in1=mask, scale=1.0, scalar=BIG, op0=ALU.add, op1=ALU.min,
                                    accum_out=negmax[:, n % SMALL, t:t + 1])
                            last.then_inc(negmax_ready, 1)
                        else:
                            nc.vector.tensor_reduce(negmax[:, n % SMALL, :],
                                                    bank_of(step)[:, :].rearrange("p (t k) -> p t k", t=TT),
                                                    AX_X, ALU.max, negate=True).then_inc(negmax_ready, 1)
                    elif kind == "probs":
                        n = head_no(phase, s, i)
                        dve.wait_ge(exp_ready, n + 1)
                        recip = nc.vector.reciprocal(rsum[:, n % SMALL, :], sums[:, n % SMALL, :])
                        if what == "mem":
                            recip.then_inc(probs_ready, 1)
                            continue
                        then(recip)
                        for t in range(TT):
                            cols = (t + 1) * P if what == "self" else T
                            p_t = probs[:, n % PROBS, t, 0:cols]
                            last = ts(p_t, p_t, rsum[:, n % SMALL, t:t + 1], None, ALU.mult)
                        last.then_inc(probs_ready, 1)
                    elif kind == "values":
                        key, _, closes = values_bank(phase, s, i)
                        if not closes:
                            continue
                        dve.wait_ge(values_done, nth[step])
                        O = bank_of(key)
                        if what == "x":
                            last = copy(qT[s][:, 2 * i:2 * i + 2, :], O[:, :].rearrange("p (k t) -> p k t", k=2))
                        elif what == "self":
                            for e in range(2):
                                last = tt(hT[s][:, e, i // 2, :], O[:, 0:T], expert[:, s, e, :], ALU.mult)
                        elif what == "cross":
                            last = copy(hT[s][:, 1, 0, :], O[:, 0:T])
                        else:
                            n = head_no(phase, s, 0)
                            dve.wait_ge(probs_ready, n + 1)
                            for t in range(TT):
                                last = ts(mctx[s][:, t, :], O[:, t * D:(t + 1) * D], rsum[:, n % SMALL, t:t + 1],
                                          None, ALU.mult)
                        last.then_inc(drained[unit[key][0]], 1)
                    elif kind in ("out", "ff2", "down"):
                        wait_filled(dve, step)
                        delta = src[:, :].rearrange("p (t d) -> p t d", t=TT)
                        if kind == "ff2" or what == "x":
                            g = {0: 0, 6: 1, 4: 2, 10: 3}[phase]
                            stt(out=x[s][:, :, :], in0=delta, scalar=gates[:, g:g + 1], in1=x[s][:, :, :],
                                op0=ALU.mult, op1=ALU.add).then_inc(free, 1)
                        else:
                            tt(x[s][:, :, :], delta, x[s][:, :, :], ALU.add).then_inc(free, 1)
                    elif kind == "rotary":
                        qk = ("qk", 1, s, i)
                        wait_filled(dve, qk)
                        src = bank_of(qk)[:, :].rearrange("p (w h d) -> p w h d", w=2, h=H)
                        n = s * TT + i
                        buf, half_d = n % 2, SD // 2
                        if n >= 2:
                            wait_filled(dve, ("stackT", 1, (n - 2) // TT, 4 * ((n - 2) % TT) + 3))
                        if n:
                            dve.wait_ge(stack_ready, n)
                        cos = rot[:, i, :, 0, :].unsqueeze(2)
                        sin = rot[:, i, :, 1, :].unsqueeze(2)
                        tt(rot_a, src, cos.to_broadcast([P, 2, H, SD]), ALU.mult)
                        tt(rot_b[:, :, :, 0:half_d], src[:, :, :, half_d:SD],
                           sin[:, :, :, 0:half_d].to_broadcast([P, 2, H, half_d]), ALU.mult)
                        ins = tt(rot_b[:, :, :, half_d:SD], src[:, :, :, 0:half_d],
                                 sin[:, :, :, half_d:SD].to_broadcast([P, 2, H, half_d]), ALU.mult)
                        ins.then_inc(drained[unit[qk][0]], 1)
                        wait_drained(dve, qk)
                        then(tt(rot_a, rot_a, rot_b, ALU.add))
                        q, k = rot_a[:, 0, :, :], rot_a[:, 1, :, :]
                        q2 = q.unsqueeze(2).to_broadcast([P, H, 2, SD])
                        copy(q_tmp[:, buf, :, 0:2, :].bitcast(F32R), q2)
                        k2 = k.unsqueeze(2).to_broadcast([P, H, 2, SD])
                        then(copy(k_tmp[:, buf, :, :, 0, :].bitcast(F32R), k2))
                        tt(q_tmp[:, buf, :, 2:4, :], q2, q_tmp[:, buf, :, 0:2, :], ALU.subtract)
                        tt(k_tmp[:, buf, :, :, 1, :], k2, k_tmp[:, buf, :, :, 0, :], ALU.subtract).then_inc(stack_ready, 1)
                    elif kind == "ksplit":
                        ckv = ("ckv", 2, s, 0)
                        wait_filled(dve, ckv)
                        if s:
                            wait_filled(dve, ("stackT", 2, s - 1, TT - 1))
                        both = bank_of(ckv)[:, :].rearrange("p (t w h d) -> p t w h d", t=TT, w=2, h=H)
                        for t in range(TT):
                            k2 = both[:, t, 0, :, :].unsqueeze(2).to_broadcast([P, H, 2, CD])
                            last = copy(kc_tmp[:, H * t:H * t + H, :, 0, :].bitcast(F32R), k2)
                        then(last)
                        for t in range(TT):
                            k2 = both[:, t, 0, :, :].unsqueeze(2).to_broadcast([P, H, 2, CD])
                            last = tt(kc_tmp[:, H * t:H * t + H, :, 1, :], k2,
                                      kc_tmp[:, H * t:H * t + H, :, 0, :], ALU.subtract)
                        last.then_inc(split_ready, 1)
                        dve.wait_ge(v_zeroed, 2 * s + 2)
                        for c in range(4):
                            for t in range(TT):
                                heads = vc[s][:, t, :, :].rearrange("p (a c) d -> p a c d", c=4)
                                vals = both[:, t, 1, :, :].rearrange("p (a c) d -> p a c d", c=4)
                                last = copy(heads[:, :, c, CD * c:CD * c + CD], vals[:, :, c, :])
                        last.then_inc(drained[unit[ckv][0]], 1)
                    elif kind == "qsplit":
                        cq = ("cq", 2, s, 0)
                        wait_filled(dve, cq)
                        if s:
                            wait_filled(dve, ("stackT", 2, s - 1, 2 * TT - 1))
                        flat = bank_of(cq)[:, 0:TT * DC].rearrange("p (h d) -> p h d", d=CD)
                        ins = ts(qc_raw, flat, float(CD) ** -0.5, None, ALU.mult)
                        ins.then_inc(drained[unit[cq][0]], 1)
                        wait_drained(dve, cq)
                        q2 = qc_raw[:, :, :].unsqueeze(2).to_broadcast([P, TT * H, 2, CD])
                        then(copy(qc_tmp[:, :, 0:2, :].bitcast(F32R), q2))
                        tt(qc_tmp[:, :, 2:4, :], q2, qc_tmp[:, :, 0:2, :], ALU.subtract).then_inc(split_ready, 1)
                    elif kind == "gateup":
                        rows = slice(0, P if i < MT - 1 else MLAST)
                        dve.wait_ge(silu_ready, nth[step])
                        ins = tt(sg[s][rows, i, :], src[rows, T:2 * T], sg[s][rows, i, :], ALU.mult)
                        ins.then_inc(free, 1)
                        wait_drained(dve, step)
                        for e in range(2):
                            last = tt(acts[s][rows, e, i, :], sg[s][rows, i, :], expert[rows, s, e, :], ALU.mult)
                        last.then_inc(acts_ready, 1)
                    elif kind == "mgate":
                        wait_filled(dve, step)
                        tt(mz[s][:, :, :], src[:, :].rearrange("p (t d) -> p t d", t=TT),
                           b_gate[:, :].unsqueeze(1).to_broadcast([P, TT, D]), ALU.add).then_inc(free, 1)
                    elif kind == "fuse":
                        dve.wait_ge(mgate_exp, s + 1)
                        then(ts(mg[s], mg[s], 1.0, None, ALU.add))
                        then(nc.vector.reciprocal(mg[s], mg[s]))
                        then(tt(mg[s], mg[s], mctx[s], ALU.mult))
                        then(tt(x[s], x[s], mg[s], ALU.add))
                        statistics(s, x[s])
                        root(s, step, True)
                        for t in range(TT):
                            last = stt(out=x[s][:, t, :], in0=x[s][:, t, :], scalar=rstd[:, s, t:t + 1],
                                       in1=norm_w[:, :], op0=ALU.mult, op1=ALU.mult)
                        then(last)
                dve.drain().then_inc(engines_done, 1)
                dve.wait_ge(iteration_open, it + 1)


_X = ["ln_q_g", "ln_q_b", "Wq", "Wkv", "Wo", "attn_gate", "ln_ff_g", "ln_ff_b", "W1", "W2", "ff_gate"]
_L1 = ["ln_in_w", "ln_post_attn_w", "ln_post_cross_w", "v_qkv", "l_qkv", "v_dense", "l_dense", "cq_w", "ckv_w",
       "cdense_w", "v_gate", "v_up", "v_down", "l_gate", "l_up", "l_down"]
_L2 = ["W_mem", "W_gate", "b_gate", "norm_w"]


def _constants():
    f = np.float32
    causal = np.zeros((P, 2 * P), f)
    causal[:, P:] = np.triu(np.full((P, P), NEG, f), 1)
    inv = f(1.0) / np.power(f(10000.0), np.arange(0, SD, 2, dtype=f) / f(SD), dtype=f)
    angle = np.outer(np.arange(T, dtype=f), inv)
    cos, sin = np.cos(angle), np.sin(angle)
    rows = np.concatenate([cos, cos, -sin, sin], -1)
    rot = np.concatenate([rows * f(-float(SD) ** -0.5), rows], -1).astype(f)
    iota = np.arange(T, dtype=f).reshape(TT, P).T.copy()
    return {"ident": np.eye(P, dtype=f), "causal": causal, "iota": iota, "rot": rot}


def kernel(**inputs):
    import concourse.bacc as _bacc
    from concourse.bass_utils import run_bass_kernel_spmd as _run

    nc = _bacc.Bacc("TRN2", target_bir_lowering=False, num_devices=1)
    arrays = {}

    def feed(name, a):
        a = np.ascontiguousarray(a)
        arrays[name] = a
        return nc.dram_tensor(name, a.shape, mybir.dt.from_np(a.dtype), kind="ExternalInput").ap()

    x = feed("x", inputs["x"])
    ctx = feed("ctx", inputs["ctx_1024"])
    pos = feed("pos", inputs["pos_1xS"])
    media = feed("media_mask", inputs["mask_BxS2_bk0"])
    expert = feed("expert_mask", inputs["mask_BxS_ik0"])
    xw = {n: {k: feed(f"L{n}_{k}", inputs[f"L{n}_xattn_{k}"]) for k in _X} for n in (0, 3)}
    l1 = {k: feed(f"L1_{k}", inputs[f"L1_xattn_{k}"]) for k in _L1}
    l2 = {k: feed(f"L2_{k}", inputs[f"L2_xattn_{k}"]) for k in _L2}
    consts = {k: feed(f"const_{k}", a) for k, a in _constants().items()}
    out = nc.dram_tensor("out", (B, T, D), F32, kind="ExternalOutput").ap()
    fused_layers(nc, x, ctx, pos, media, expert, xw, l1, l2, consts, out)
    r = _run(nc, [arrays], core_ids=[0])
    return r.results[0]["out"]
```

```python
from contextlib import ExitStack

import numpy as np
import concourse.bass as bass
from concourse import mybir

F32 = mybir.dt.float32
F32R = mybir.dt.float32r
I32 = mybir.dt.int32
U8 = mybir.dt.uint8
ALU = mybir.AluOpType
ACT = mybir.ActivationFunctionType
AX_X = mybir.AxisListType.X

P = 128
B, T, D = 4, 256, 256
TT, KD = T // P, D // P
DC = 128
SLOTS = 2
ITERS = B // SLOTS
H = 16
XD, INNER = 64, 1024
KI = INNER // P
FF = 1024
SD = D // H
CD = DC // H
MLP = 688
MT = -(-MLP // P)
MLAST = MLP - (MT - 1) * P
NEG = 1.0e30
BIG = 3.0e38
LN_EPS, RMS_EPS = 1e-5, 1e-6

RINGS = {"scores": (0, 3), "probsT": (3, 2), "main": (5, 3)}
PROBS, PTS, SMALL, MASKED = 4, 8, 8, 2
LAG_T, LAG_O = 3, 5
PHASES = {0: "x", 1: "self", 2: "cross", 3: "mem", 4: "x"}


def schedule():
    order = []

    def each(kind, phase, n=1):
        for s in range(SLOTS):
            for i in range(n):
                order.append((kind, phase, s, i))

    def attention(phase, heads, filler=()):
        items = [(s, h) for s in range(SLOTS) for h in range(heads)]
        batch = min(4, heads)
        for i in range(len(items) + LAG_O + batch):
            if i == len(items):
                order.extend(filler)
            if i < len(items):
                order.append(("scores", phase, *items[i]))
            if 0 <= i - 1 < len(items):
                order.append(("probs", phase, *items[i - 1]))
            if 0 <= i - LAG_T < len(items):
                order.append(("probsT", phase, *items[i - LAG_T]))
            o = i - LAG_O
            if 0 <= o < len(items) and o % batch == batch - 1:
                order.append(("values", phase, items[o][0], items[o][1] // batch))

    def step(kind, phase, s, i=0):
        order.append((kind, phase, s, i))

    def run(kind, phase, s, n, first=0):
        order.extend((kind, phase, s, i) for i in range(first, n))

    def onward(last, last_phase, phase, filler=()):
        step(last, last_phase, 0)
        step("norm", phase, 0)
        step(last, last_phase, 1)
        order.extend(filler)
        step("hT", phase, 0)
        step("norm", phase, 1)

    def feed_forward(phase):
        run("ff1", phase, 0, 2)
        step("hT", phase, 1)
        run("ff1", phase, 0, 4, 2)
        run("ff1", phase, 1, 4)

    each("ctxT", 0)
    each("norm", 0)
    for s in range(SLOTS):
        run("kproj", 0, s, 4)
        run("vproj", 0, s, 4)
    for s in range(SLOTS):
        step("hT", 0, s)
        run("qproj", 0, s, 4)
    attention(0, H)
    onward("out", 0, 6, [("ckv", 2, s, 0) for s in range(SLOTS)])
    each("ksplit", 2)
    step("rows", 1, 0)
    feed_forward(6)
    for s in range(SLOTS):
        run("stackT", 2, s, TT)
    onward("ff2", 6, 1)
    tiles = [(s, t) for s in range(SLOTS) for t in range(TT)]
    for n in range(len(tiles) + 1):
        if n == 1:
            step("hT", 1, 1)
        if n < len(tiles):
            for kind in ("qk", "v", "rotary"):
                step(kind, 1, *tiles[n])
        if n:
            s, t = tiles[n - 1]
            run("stackT", 1, s, 4 * t + 4, 4 * t)
    attention(1, H)
    onward("out", 1, 2)
    step("cq", 2, 0)
    step("qsplit", 2, 0)
    step("hT", 2, 1)
    step("cq", 2, 1)
    step("qsplit", 2, 1)
    for s in range(SLOTS):
        run("stackT", 2, s, 2 * TT, TT)
    attention(2, H)
    onward("out", 2, 5, [("mem", 3, s, i) for s in range(SLOTS) for i in range(2)])
    run("gateup", 5, 0, 2)
    step("hT", 5, 1)
    run("gateup", 5, 0, MT, 2)
    run("gateup", 5, 1, MT)
    each("down", 5)
    each("hT", 3)
    attention(3, 1, [("kproj", 4, 0, i) for i in range(4)])
    each("mctxT", 3)
    run("vproj", 4, 0, 4)
    each("mgate", 3)
    step("fuse", 3, 0)
    step("norm", 4, 0)
    run("kproj", 4, 1, 4)
    step("fuse", 3, 1)
    step("norm", 4, 1)
    run("vproj", 4, 1, 4)
    for s in range(SLOTS):
        step("hT", 4, s)
        run("qproj", 4, s, 4)
    attention(4, H)
    onward("out", 4, 10)
    feed_forward(10)
    each("ff2", 10)
    return order


RING_OF = {"scores": "scores", "probsT": "probsT"}
NO_BANK = {"norm", "rotary", "ksplit", "qsplit", "probs", "fuse"}


def head_of(phase, i):
    kind = PHASES[phase]
    if kind == "self":
        return 8 * (i // 8) + 2 * (i % 4) + i % 8 // 4
    if kind == "cross":
        return 4 * (i % 4) + i // 4
    return i


def values_bank(phase, s, b):
    per = {"x": 1, "self": 2, "cross": 4, "mem": 1}[PHASES[phase]]
    return ("O", phase, s, b // per), b % per == 0, b % per == per - 1


def fused_layers(
    nc, x_in, ctx_in, pos_in, media_mask_in, expert_mask_in, gains_in, gates_in, fusion_rows_in, xw, l1, l2, consts, out,
):
    order = schedule()

    unit, used, fills, filled_before = {}, {r: 0 for r in RINGS}, {}, [0] * 8
    others = 0
    for kind, phase, s, i in order:
        if kind in NO_BANK:
            continue
        key = (kind, phase, s, i)
        if kind == "values":
            key, opens, _ = values_bank(phase, s, i)
            if not opens:
                continue
        ring = RING_OF.get(kind)
        if ring is None:
            ring = "main" if kind == "values" or others % 5 in (0, 2, 4) else "probsT"
            others += kind != "values"
        first, banks = RINGS[ring]
        unit[key] = (first + used[ring] % banks, used[ring] // banks)
        used[ring] += 1
        if kind != "values":
            filled_before[unit[key][0]] += 1
            fills[key] = filled_before[unit[key][0]]

    nth, seen = {}, {}
    for step in order:
        seen[step[0]] = seen.get(step[0], 0) + 1
        nth[step] = seen[step[0]]

    with ExitStack() as ctx:
        top = [-(-nc.sbuf_base // 64) * 64]

        def place(name, shape, dtype=F32, at=None):
            size = int(np.prod(shape[1:])) * (1 if dtype == U8 else 4)
            offset = top[0] if at is None else at
            if at is None:
                top[0] += -(-size // 64) * 64
                assert top[0] <= nc.sbuf_usable_end, (name, top[0])
            tensor = nc.alloc_sbuf_tensor_at(name, list(shape), dtype, offset=offset)
            return tensor.ap() if hasattr(tensor, "ap") else tensor

        def region(size):
            at = top[0]
            top[0] += size
            assert top[0] <= nc.sbuf_usable_end, top[0]
            return at

        KB = 1024
        w_q = place("w_q", [P, KD, INNER])
        w_kv = place("w_kv", [P, 2 * INNER])
        w_o = place("w_o", [P, KI, D])
        w_ff = region((4 * KD * MLP + 2 * MT * D) * 4)
        w_1 = place("w_1", [P, KD, FF], at=w_ff)
        w_2 = place("w_2", [P, KI, D], at=w_ff + KD * FF * 4)
        w_gu = place("w_gu", [P, 4, KD, MLP], at=w_ff)
        w_down = place("w_down", [P, 2, MT, D], at=w_ff + 4 * KD * MLP * 4)
        w_qkv = place("w_qkv", [P, 2, KD, 3 * D])
        w_dense = place("w_dense", [P, 2, 2, D])
        w_cq = place("w_cq", [P, KD, DC])
        w_ckv = place("w_ckv", [P, 2 * DC])
        w_cdense = place("w_cdense", [P, D])
        w_gate = place("w_gate", [P, 2 * KD, D])
        w_memT = place("w_memT", [P, D])
        ident = place("ident", [P, P])
        causal = place("causal", [P, 2 * P])
        iota = place("iota", [P, TT])
        gains = place("gains", [P, 22])
        rot = place("rot", [P, TT, 2, 2, SD])
        half = place("half", [P, TT])
        gates = place("gates", [P, 4])
        gates_raw = place("gates_raw", [P, 4])
        fusion_rows = place("fusion_rows", [P, 2, D])
        expert = place("expert", [P, SLOTS, 2, T])
        media = place("media", [P, SLOTS, T])
        media_raw = place("media_raw", [P, SLOTS, T], U8)
        x, h, hT, ctxT, kmem, vmem = [], [], [], [], [], []
        qT, kT, v, g_act, qs, ks, qc, kc, vs, vc, sg, acts, slot_at = ([] for _ in range(13))
        for s in range(SLOTS):
            x.append(place(f"x{s}", [P, TT, D]))
            h.append(place(f"h{s}", [P, TT, D]))
            hT.append(place(f"hT{s}", [P, 2, KD, T]))
            ctxT.append(place(f"ctxT{s}", [P, T]))
            kmem.append(place(f"kmem{s}", [P, KD, T]))
            vmem.append(place(f"vmem{s}", [P, TT, D]))
            big = region(24 * KB)
            slot_at.append(big)
            qT.append(place(f"qT{s}", [P, KI, T], at=big))
            kT.append(place(f"kT{s}", [P, KI, T], at=big + 8 * KB))
            v.append(place(f"v{s}", [P, TT, INNER], at=big + 16 * KB))
            g_act.append(place(f"g_act{s}", [P, KI, T], at=big))
            qs.append(place(f"qs{s}", [P, 8, T], F32R, at=big))
            ks.append(place(f"ks{s}", [P, 8, T], F32R, at=big + 8 * KB))
            qc.append(place(f"qc{s}", [P, 4, T], F32R, at=big))
            kc.append(place(f"kc{s}", [P, 4, T], F32R))
            vs.append(place(f"vs{s}", [P, TT, H, 32], at=big + 16 * KB))
            vc.append(place(f"vc{s}", [P, TT, H, 32], at=big + 20 * KB))
            sg.append(place(f"sg{s}", [P, MT, T], at=big))
            acts.append(place(f"acts{s}", [P, 2, MT, T], at=big + 6 * KB))
        ctx_in_sb = [h[s] for s in range(SLOTS)]
        masked = place("masked", [P, MASKED, TT, T])
        probs_at = region(PROBS * TT * T * 4)
        probs = place("probs", [P, PROBS, TT, T], at=probs_at)
        probsT_at = region(PTS * 2 * T * 4)
        probsT = place("probsT", [P, PTS, 2 * T], at=probsT_at)
        negmax = place("negmax", [P, SMALL, TT])
        sums = place("sums", [P, SMALL, TT])
        rsum = place("rsum", [P, SMALL, TT])
        stats = place("stats", [P, SLOTS, TT, 6])
        mv = place("mv", [P, SLOTS, TT, 2])
        ms = place("ms", [P, SLOTS, TT])
        rstd = place("rstd", [P, SLOTS, TT])
        q_tmp = place("q_tmp", [P, 2, H, 4, SD], at=probsT_at)
        k_tmp = place("k_tmp", [P, 2, H, 2, 2, SD], at=probsT_at + 8 * KB)
        rot_a = place("rot_a", [P, 2, H, SD], at=probs_at)
        rot_b = place("rot_b", [P, 2, H, SD], at=probs_at + 2 * KB)
        qc_tmp = place("qc_tmp", [P, SLOTS, TT * H, 4, CD], at=probsT_at)
        kc_tmp = place("kc_tmp", [P, SLOTS, TT * H, 2, 2, CD], at=probsT_at + 8 * KB)
        qc_raw = place("qc_raw", [P, SLOTS, TT * H, CD], at=probs_at + 4 * KB)
        pos_raw = place("pos_raw", [P, T], I32, at=probsT_at)
        pos_f = place("pos_f", [P, T], at=probsT_at + KB)
        pos_n = place("pos_n", [P, T], at=probsT_at + 2 * KB)
        onehot = place("onehot", [P, TT, T])
        rot_tab = place("rot_tab", [P, TT, 64])
        expert_raw = place("expert_raw", [P, SLOTS, T], I32)
        qT_at = [slot_at[s] for s in range(SLOTS)]
        mctx = [place(f"mctx{s}", [P, TT, D], at=qT_at[s]) for s in range(SLOTS)]
        mz = [place(f"mz{s}", [P, TT, D], at=qT_at[s] + 2 * KB) for s in range(SLOTS)]
        mg = [place(f"mg{s}", [P, TT, D], at=qT_at[s] + 4 * KB) for s in range(SLOTS)]

        bank = [ctx.enter_context(nc.psum_tensor(f"bank{i}", [P, 512], F32)) for i in range(8)]

        def sem(name):
            return ctx.enter_context(nc.semaphore(name))

        filled = [sem(f"bank{i}_filled") for i in range(8)]
        drained = [sem(f"bank{i}_drained") for i in range(8)]
        negmax_ready = sem("negmax_ready")
        exp_ready = sem("exp_ready")
        probs_ready = sem("probs_ready")
        values_done = sem("values_done")
        h_ready = sem("h_ready")
        var_ready = sem("var_ready")
        rstd_ready = sem("rstd_ready")
        stack_ready = sem("stack_ready")
        split_ready = sem("split_ready")
        silu_ready = sem("silu_ready")
        acts_ready = sem("acts_ready")
        mgate_ready = sem("mgate_ready")
        vs_zeroed = sem("vs_zeroed")
        vc_zeroed = sem("vc_zeroed")
        dve_step = sem("dve_step")
        ff0_loaded = sem("ff0_loaded")
        attn3_loaded = sem("attn3_loaded")
        mlp_loaded = sem("mlp_loaded")
        ff3_loaded = sem("ff3_loaded")
        engines_done = sem("engines_done")
        per_iteration = [s.num for s in (
            *filled, *drained, negmax_ready, exp_ready, probs_ready, values_done, h_ready, var_ready,
            rstd_ready, stack_ready, split_ready, silu_ready, acts_ready, mgate_ready, vs_zeroed, vc_zeroed, dve_step,
            ff0_loaded, attn3_loaded, mlp_loaded, ff3_loaded, engines_done)]
        assert per_iteration == list(range(per_iteration[0], per_iteration[0] + len(per_iteration)))
        iteration_open = sem("iteration_open")
        ident_loaded = sem("ident_loaded")
        ctx_loaded = sem("ctx_loaded")
        x_loaded = sem("x_loaded")
        masks_loaded = sem("masks_loaded")
        wk_loaded, wv_loaded, wq_loaded, wo_loaded = (sem(f"layer0_w{n}_loaded") for n in "kvqo")
        x_free = sem("x_free")
        pos_loaded = sem("pos_loaded")
        ckv_loaded = sem("ckv_loaded")
        l1_loaded = sem("l1_loaded")
        gates_loaded = sem("gates_loaded")
        gains_loaded = sem("gains_loaded")
        rot_tab_loaded = sem("rot_tab_loaded")
        late_loaded = sem("late_loaded")
        setup_dve = sem("setup_dve")
        setup_act = sem("setup_act")
        setup_pool = sem("setup_pool")
        setup_step = sem("setup_step")

        ATTN_DMAS, FF_DMAS, MLP_DMAS, L1_DMAS, LATE_DMAS = 4, 2, 4 + 2 * 2, 6, 4

        GAIN = {0: 0, 6: 4, 4: 8, 10: 12, 1: 16, 5: 18, 2: 20}

        def bank_of(key):
            return bank[unit[key][0]]

        def wait_filled(eng, key):
            eng.wait_ge(filled[unit[key][0]], fills[key])

        def wait_drained(eng, key):
            b, n = unit[key]
            eng.wait_ge(drained[b], n + 1)

        def wait_free(pe, key):
            b, n = unit[key]
            if n:
                pe.wait_ge(drained[b], n)

        unit_kinds_act = {"ctxT", "kproj", "vproj", "qproj", "ff1", "v", "stackT", "mem", "gateup", "mctxT"}

        def heads_of(phase):
            return 1 if PHASES[phase] == "mem" else H

        def head_no(phase, s, hd):
            return nth[("scores", phase, s, hd)] - 1

        def by_no():
            return {head_no(p_, s_, i_): (p_, s_, i_) for k_, p_, s_, i_ in order if k_ == "scores"}

        head_at = by_no()
        split_no = {step: n + 1 for n, step in enumerate(st for st in order if st[0] in ("ksplit", "qsplit"))}
        root_no = {step: n + 1 for n, step in enumerate(st for st in order if st[0] in ("norm", "fuse"))}

        block = ctx.enter_context(nc.Block())

        @block.sync
        def _(sp):
            def load_attention(layer, done):
                sp.dma_start(w_kv[:, 0:INNER], xw[layer]["Wkv"][:, 0:INNER]).then_inc(done[0], 16)
                sp.dma_start(w_kv[:, INNER:], xw[layer]["Wkv"][:, INNER:]).then_inc(done[1], 16)
                sp.dma_start(w_q[:, :, :], xw[layer]["Wq"].rearrange("(k p) n -> p k n", p=P)).then_inc(done[2], 16)
                sp.dma_start(w_o[:, :, :], xw[layer]["Wo"].rearrange("(k p) n -> p k n", p=P)).then_inc(done[3], 16)

            def load_ff(layer, done):
                sp.dma_start(w_1[:, :, :], xw[layer]["W1"].rearrange("(k p) n -> p k n", p=P)).then_inc(done, 16)
                sp.dma_start(w_2[:, :, :], xw[layer]["W2"].rearrange("(k p) n -> p k n", p=P)).then_inc(done, 16)

            def load_mlp(done):
                for n, w in enumerate(("v_gate", "l_gate", "v_up", "l_up")):
                    sp.dma_start(w_gu[:, n, :, :], l1[w].rearrange("(k p) n -> p k n", p=P)).then_inc(done, 16)
                for n, w in enumerate(("v_down", "l_down")):
                    full = (MT - 1) * P
                    sp.dma_start(w_down[:, n, 0:MT - 1, :],
                                 l1[w][0:full, :].rearrange("(k p) n -> p k n", p=P)).then_inc(done, 16)
                    sp.dma_start(w_down[0:MLAST, n, MT - 1, :], l1[w][full:MLP, :]).then_inc(done, 16)

            def load_ctx(first):
                for s in range(SLOTS):
                    sp.dma_start(ctx_in_sb[s][:, :, 0:DC],
                                 ctx_in[first + s].rearrange("(t p) d -> p t d", p=P)).then_inc(ctx_loaded, 16)

            def load_x(first):
                for s in range(SLOTS):
                    sp.dma_start(x[s][:, :, :], x_in[first + s].rearrange("(t p) d -> p t d", p=P)).then_inc(x_loaded, 16)
                for s in range(SLOTS):
                    sp.dma_start(media_raw[:, s, :], media_mask_in[first + s].partition_broadcast(P)).then_inc(masks_loaded, 16)
                    sp.dma_start(expert_raw[:, s, :], expert_mask_in[first + s].partition_broadcast(P)).then_inc(masks_loaded, 16)

            load_ctx(0)
            sp.dma_start(ident[:, :], consts["ident"]).then_inc(ident_loaded, 16)
            sp.dma_start(gates_raw[:, :], gates_in.partition_broadcast(P)).then_inc(gates_loaded, 16)
            sp.dma_start(gains[:, :], gains_in).then_inc(gains_loaded, 16)
            sp.dma_start(pos_raw[:, :], pos_in.partition_broadcast(P).rearrange("p a t -> p (a t)")).then_inc(pos_loaded, 16)
            sp.dma_start(iota[:, :], consts["iota"]).then_inc(pos_loaded, 16)
            sp.sem_inc(x_free, 16 * SLOTS)

            with sp.Fori(0, ITERS) as it:
                sp.wait_ge(x_free, it * (16 * SLOTS) + 16 * SLOTS)
                load_x(it * SLOTS)
                wait_filled(sp, ("qproj", 0, SLOTS - 1, 3))
                load_ff(0, ff0_loaded)
                wait_filled(sp, ("out", 0, SLOTS - 1, 0))
                load_attention(3, [attn3_loaded] * 4)
                wait_filled(sp, ("ff2", 6, SLOTS - 1, 0))
                load_mlp(mlp_loaded)
                wait_filled(sp, ("down", 5, SLOTS - 1, 0))
                load_ff(3, ff3_loaded)
                wait_filled(sp, ("out", 4, SLOTS - 1, 0))
                load_attention(0, [wk_loaded, wv_loaded, wq_loaded, wo_loaded])
                wait_filled(sp, ("ff2", 10, SLOTS - 1, 0))
                load_ctx(it * -SLOTS + (ITERS - 1) * SLOTS)
                for s in range(SLOTS):
                    wait_drained(sp, ("ff2", 10, s, 0))
                    sp.dma_start(out[it * SLOTS + s].rearrange("(t p) d -> p t d", p=P), x[s][:, :, :]).then_inc(x_free, 16)
                sp.wait_ge(engines_done, 4)
                sp.sem_clear(range(per_iteration[0], per_iteration[-1] + 1))
                sp.sem_inc(iteration_open, 1)
            sp.wait_ge(x_free, 16 * SLOTS * (ITERS + 1))
            for loaded in (wk_loaded, wv_loaded, wq_loaded, wo_loaded):
                sp.wait_ge(loaded, 16 * (ITERS + 1))
            sp.wait_ge(ctx_loaded, 16 * SLOTS * (ITERS + 1))

        @block.tensor
        def _(pe):
            mm, tr = nc.tensor.matmul, nc.tensor.transpose

            pe.wait_ge(ident_loaded, 16)

            def scores(phase, s, hd):
                key, n = ("scores", phase, s, hd), head_no(phase, s, hd)
                if n >= RINGS["scores"][1]:
                    before = n - RINGS["scores"][1]
                    taken = negmax_ready if PHASES[head_at[before][0]] in ("x", "self") else exp_ready
                    pe.wait_ge(taken, before + 1)
                S = bank_of(key)[:, :].rearrange("p (t k) -> p t k", t=TT)
                kind = PHASES[phase]
                if kind == "x":
                    if hd % 4 == 0:
                        wait_drained(pe, ("qproj", phase, s, hd // 4))
                        wait_drained(pe, ("kproj", phase, s, hd // 4))
                    j, r = hd // 2, slice(XD * (hd % 2), XD * (hd % 2) + XD)
                    for t in range(TT):
                        last = mm(S[:, t, :], qT[s][r, j, t * P:(t + 1) * P], kT[s][r, j, :], start=True, stop=True)
                elif kind == "self":
                    if hd == 0:
                        for u in range(8):
                            wait_drained(pe, ("stackT", phase, s, u))
                    head = head_of(phase, hd)
                    j, r = head // 2, slice(64 * (head % 2), 64 * (head % 2) + 64)
                    for t in range(TT):
                        n = (t + 1) * P
                        last = mm(S[:, t, 0:n], qs[s][r, j, t * P:(t + 1) * P], ks[s][r, j, 0:n], start=True, stop=True)
                elif kind == "cross":
                    if hd == 0:
                        for u in range(2 * TT):
                            wait_drained(pe, ("stackT", phase, s, u))
                    head = head_of(phase, hd)
                    j, r = head // 4, slice(32 * (head % 4), 32 * (head % 4) + 32)
                    for t in range(TT):
                        last = mm(S[:, t, :], qc[s][r, j, t * P:(t + 1) * P], kc[s][r, j, :], start=True, stop=True,
                                  tile_position=(32 * (head % 4), 0))
                else:
                    wait_drained(pe, ("hT", 3, s, 0))
                    wait_drained(pe, ("mem", 3, s, 0))
                    for t in range(TT):
                        for k in range(KD):
                            last = mm(S[:, t, :], hT[s][:, 0, k, t * P:(t + 1) * P], kmem[s][:, k, :],
                                      start=(k == 0), stop=(k == KD - 1))
                last.then_inc(filled[unit[key][0]], 1)

            def probs_transposed(phase, s, hd):
                key, n = ("probsT", phase, s, hd), head_no(phase, s, hd)
                wait_free(pe, key)
                pe.wait_ge(probs_ready, nth[("probs", phase, s, hd)])
                PT = bank_of(key)
                for t in range(TT):
                    for k in range(TT):
                        if PHASES[phase] == "self":
                            if k > t:
                                continue
                            at = t * P if k == 0 else 2 * P
                        else:
                            at = k * T + t * P
                        last = tr(PT[:, at:at + P], probs[:, n % PROBS, t, k * P:(k + 1) * P], ident[:, :])
                last.then_inc(filled[unit[key][0]], 1)

            def values(phase, s, b):
                kind = PHASES[phase]
                key, opens, closes = values_bank(phase, s, b)
                if opens:
                    wait_free(pe, key)
                O = bank_of(key)
                heads = [0] if kind == "mem" else [4 * b + a for a in range(4)]
                if b == 0:
                    if kind == "x":
                        for u in range(4):
                            wait_drained(pe, ("vproj", phase, s, u))
                    elif kind == "self":
                        for t in range(TT):
                            wait_drained(pe, ("v", 1, s, t))
                    elif kind == "cross":
                        wait_drained(pe, ("ckv", 2, s, 0))
                    else:
                        wait_drained(pe, ("mem", 3, s, 1))
                for hd in heads:
                    wait_drained(pe, ("probsT", phase, s, hd))
                if kind == "mem":
                    pt = probsT[:, head_no(phase, s, 0) % PTS, :].rearrange("p (k q) -> p k q", k=TT)
                    for t in range(TT):
                        for k in range(TT):
                            last = mm(O[:, t * D:(t + 1) * D], pt[:, k, t * P:(t + 1) * P], vmem[s][:, k, :],
                                      start=(k == 0), stop=(k == TT - 1))
                    last.then_inc(values_done, 1)
                    return
                for pair in ([0, 1], [2, 3]) if kind == "x" else ([0, 1, 2, 3],):
                    for k in range(TT):
                        for a in pair:
                            hd = heads[a]
                            pt = probsT[:, head_no(phase, s, hd) % PTS, :]
                            if kind == "x":
                                last = mm(O[XD * (a % 2):XD * (a % 2) + XD, T * (a // 2):T * (a // 2) + T],
                                          v[s][:, k, hd * XD:(hd + 1) * XD], pt[:, k * T:(k + 1) * T],
                                          start=(k == 0), stop=(k == TT - 1))
                            elif kind == "self":
                                first, final = b % 2 == 0 and k == 0, b % 2 == 1 and k == TT - 1
                                q0 = k * P
                                last = mm(O[32 * a:32 * a + 32, q0:T], vs[s][:, k, head_of(phase, hd), :],
                                          pt[:, k * T:k * T + T - q0], start=first, stop=final,
                                          tile_position=(0, 32 * a))
                            else:
                                first, final = b == 0 and k == 0, b == 3 and k == TT - 1
                                last = mm(O[32 * a:32 * a + 32, 0:T], vc[s][:, k, head_of(phase, hd), :],
                                          pt[:, k * T:(k + 1) * T], start=first, stop=final,
                                          tile_position=(0, 32 * a))
                last.then_inc(values_done, 1)

            def products(key, pieces):
                wait_free(pe, key)
                for cols, terms in pieces:
                    rows = terms[0][0].shape[-1]
                    for n, (stationary, moving) in enumerate(terms):
                        last = mm(bank_of(key)[0:rows, cols], stationary, moving,
                                  start=(n == 0), stop=(n == len(terms) - 1))
                last.then_inc(filled[unit[key][0]], 1)

            def turn(key, tiles):
                wait_free(pe, key)
                for n, tile in enumerate(tiles):
                    last = tr(bank_of(key)[:, n * P:(n + 1) * P], tile, ident[:, :])
                last.then_inc(filled[unit[key][0]], 1)

            tok = lambda t: slice(t * P, (t + 1) * P)
            wide = lambda t: slice(t * T, (t + 1) * T)

            with pe.Fori(0, ITERS) as it:
                for step in order:
                    kind, phase, s, i = step
                    if kind == "scores":
                        scores(phase, s, i)
                    elif kind == "probsT":
                        probs_transposed(phase, s, i)
                    elif kind == "values":
                        values(phase, s, i)
                    elif kind == "rows":
                        pe.wait_ge(setup_dve, 1)
                        pe.wait_ge(rot_tab_loaded, 16)
                        products(step, [(slice(64 * t, 64 * t + 64), [(onehot[:, k, tok(t)], rot_tab[:, k, :])
                                                                      for k in range(TT)]) for t in range(TT)])
                    elif kind == "ctxT":
                        if s == 0:
                            pe.wait_ge(ctx_loaded, it * (16 * SLOTS) + 16 * SLOTS)
                        turn(step, [ctx_in_sb[s][:, t, 0:DC] for t in range(TT)])
                    elif kind == "hT":
                        if phase == 3:
                            wait_drained(pe, ("down", 5, s, 0))
                            src = x[s]
                        else:
                            pe.wait_ge(h_ready, nth[("norm", phase, s, 0)])
                            src = h[s]
                        turn(step, [src[:, t, tok(k)] for k in range(KD) for t in range(TT)])
                    elif kind == "mctxT":
                        wait_drained(pe, ("O", 3, s, 0))
                        turn(step, [mctx[s][:, t, tok(k)] for k in range(KD) for t in range(TT)])
                    elif kind == "kproj":
                        if s == 0 and i == 0:
                            wait_drained(pe, ("ctxT", 0, SLOTS - 1, 0))
                            if phase == 0:
                                pe.wait_ge(wk_loaded, it * 16 + 16)
                            else:
                                pe.wait_ge(attn3_loaded, 16 * ATTN_DMAS)
                        products(step, [(wide(n), [(w_kv[:, tok(2 * i + n)], ctxT[s][:, :])]) for n in range(2)])
                    elif kind == "vproj":
                        t, c = i // 2, i % 2
                        if step == ("vproj", 0, 0, 0):
                            pe.wait_ge(wv_loaded, it * 16 + 16)
                        products(step, [(slice(0, 512), [(ctxT[s][:, tok(t)], w_kv[:, INNER + 512 * c:INNER + 512 * c + 512])])])
                    elif kind == "qproj":
                        if i == 0:
                            wait_drained(pe, ("hT", phase, s, 0))
                        if step == ("qproj", 0, 0, 0):
                            pe.wait_ge(wq_loaded, it * 16 + 16)
                        products(step, [(wide(n), [(w_q[:, k, tok(2 * i + n)], hT[s][:, 0, k, :]) for k in range(KD)])
                                        for n in range(2)])
                    elif kind == "out" and PHASES[phase] == "x":
                        for b in range(4):
                            wait_drained(pe, ("O", phase, s, b))
                        if step == ("out", 0, 0, 0):
                            pe.wait_ge(wo_loaded, it * 16 + 16)
                        products(step, [(wide(t), [(qT[s][:, k, tok(t)], w_o[:, k, :]) for k in range(KI)])
                                        for t in range(TT)])
                    elif kind == "ff1":
                        if i == 0:
                            wait_drained(pe, ("hT", phase, s, 0))
                            if s == 0:
                                pe.wait_ge(ff0_loaded if phase == 6 else ff3_loaded, 16 * FF_DMAS)
                        products(step, [(wide(n), [(w_1[:, k, tok(2 * i + n)], hT[s][:, 0, k, :]) for k in range(KD)])
                                        for n in range(2)])
                    elif kind == "ff2":
                        for u in range(4):
                            wait_drained(pe, ("ff1", phase, s, u))
                        products(step, [(wide(t), [(g_act[s][:, k, tok(t)], w_2[:, k, :]) for k in range(KI)])
                                        for t in range(TT)])
                    elif kind == "qk":
                        if i == 0:
                            wait_drained(pe, ("hT", 1, s, 0))
                            if s == 0:
                                pe.wait_ge(l1_loaded, 16 * L1_DMAS)
                        products(step, [(slice(0, 512), [(hT[s][:, e, k, tok(i)], w_qkv[:, e, k, 0:512])
                                                         for e in range(2) for k in range(KD)])])
                    elif kind == "v":
                        products(step, [(slice(0, 256), [(hT[s][:, e, k, tok(i)], w_qkv[:, e, k, 512:768])
                                                         for e in range(2) for k in range(KD)])])
                    elif kind == "stackT":
                        if phase == 1:
                            t, u = i // 4, i % 4
                            if u == 0:
                                pe.wait_ge(stack_ready, nth[("rotary", 1, s, t)])
                            buf = (s * TT + t) % 2
                            if u < 2:
                                tiles = [q_tmp[:, buf, 8 * u + 2 * j:8 * u + 2 * j + 2, :, :] for j in range(4)]
                            else:
                                tiles = [k_tmp[:, buf, 8 * (u - 2) + 2 * j:8 * (u - 2) + 2 * j + 2, :, :, :] for j in range(4)]
                        else:
                            t, which = i % TT, i // TT
                            if t == 0:
                                pe.wait_ge(split_ready, split_no[("ksplit", "qsplit")[which], 2, s, 0])
                            if which == 0:
                                tiles = [kc_tmp[:, s, H * t + 4 * j:H * t + 4 * j + 4, :, :, :] for j in range(4)]
                            else:
                                tiles = [qc_tmp[:, s, H * t + 4 * j:H * t + 4 * j + 4, :, :] for j in range(4)]
                        turn(step, tiles)
                    elif kind == "out" and phase == 1:
                        for g in range(2):
                            wait_drained(pe, ("O", 1, s, g))
                        products(step, [(wide(t), [(hT[s][:, e, g, tok(t)], w_dense[:, e, g, :])
                                                   for e in range(2) for g in range(2)]) for t in range(TT)])
                    elif kind == "ckv":
                        if s == 0:
                            pe.wait_ge(ckv_loaded, 16)
                        products(step, [(wide(t), [(ctxT[s][:, tok(t)], w_ckv[:, :])]) for t in range(TT)])
                    elif kind == "cq":
                        wait_drained(pe, ("hT", 2, s, 0))
                        products(step, [(tok(t), [(hT[s][:, 0, k, tok(t)], w_cq[:, k, :]) for k in range(KD)])
                                        for t in range(TT)])
                    elif kind == "out" and phase == 2:
                        wait_drained(pe, ("O", 2, s, 0))
                        products(step, [(wide(t), [(hT[s][:, 1, 0, tok(t)], w_cdense[:, :])]) for t in range(TT)])
                    elif kind == "gateup":
                        if i == 0:
                            wait_drained(pe, ("hT", 5, s, 0))
                            if s == 0:
                                pe.wait_ge(mlp_loaded, 16 * MLP_DMAS)
                        cols = slice(i * P, min(MLP, (i + 1) * P))
                        products(step, [(wide(n), [(w_gu[:, 2 * n + e, k, cols], hT[s][:, e, k, :])
                                                   for e in range(2) for k in range(KD)]) for n in range(2)])
                    elif kind == "down":
                        pe.wait_ge(acts_ready, nth[("gateup", 5, s, MT - 1)])
                        rows = [slice(0, P if m < MT - 1 else MLAST) for m in range(MT)]
                        products(step, [(wide(t), [(acts[s][rows[m], e, m, tok(t)], w_down[rows[m], e, m, :])
                                                   for m in range(MT) for e in range(2)]) for t in range(TT)])
                    elif kind == "mem":
                        if i == 0:
                            if s == 0:
                                pe.wait_ge(late_loaded, 16 * LATE_DMAS)
                            products(step, [(wide(k), [(w_memT[:, tok(k)], ctxT[s][:, :])]) for k in range(KD)])
                        else:
                            products(step, [(wide(t), [(ctxT[s][:, tok(t)], w_memT[:, :])]) for t in range(TT)])
                    elif kind == "mgate":
                        wait_drained(pe, ("mctxT", 3, s, 0))
                        products(step, [(wide(t), [(hT[s][:, e, k, tok(t)], w_gate[:, 2 * e + k, :])
                                                   for e in range(2) for k in range(KD)]) for t in range(TT)])
                pe.drain().then_inc(engines_done, 1)
                pe.wait_ge(iteration_open, it + 1)

        @block.scalar
        def _(act):
            def copy(dst, src, scale=1.0):
                return nc.scalar.activation(dst, src, ACT.Copy, scale=scale)

            def by_k(w):
                return w.rearrange("(k p) n -> p k n", p=P)

            act.dma_start(w_kv[:, 0:INNER], xw[0]["Wkv"][:, 0:INNER]).then_inc(wk_loaded, 16)
            act.dma_start(w_kv[:, INNER:], xw[0]["Wkv"][:, INNER:]).then_inc(wv_loaded, 16)
            act.dma_start(w_q[:, :, :], by_k(xw[0]["Wq"])).then_inc(wq_loaded, 16)
            act.dma_start(w_o[:, :, :], by_k(xw[0]["Wo"])).then_inc(wo_loaded, 16)
            act.dma_start(w_ckv[:, :], l1["ckv_w"]).then_inc(ckv_loaded, 16)
            act.dma_start(rot_tab[:, :, :], by_k(consts["rot"])).then_inc(rot_tab_loaded, 16)
            act.wait_ge(gates_loaded, 16)
            nc.scalar.activation(gates[:, :], gates_raw[:, :], ACT.Tanh).then_inc(setup_act, 1)

            with act.Fori(0, ITERS) as it:
                for step in order:
                    kind, phase, s, i = step
                    if kind in unit_kinds_act or (kind == "hT" and phase not in (1, 5)):
                        wait_filled(act, step)
                        src = bank_of(step)
                        free = drained[unit[step][0]]
                    if kind == "ctxT":
                        copy(ctxT[s][:, :], src[:, 0:T]).then_inc(free, 1)
                    elif kind == "hT" and phase == 3:
                        copy(hT[s][:, 0, :, :], src[:, :].rearrange("p (k t) -> p k t", k=KD)).then_inc(free, 1)
                    elif kind == "hT" and phase not in (1, 5):
                        if phase == 0:
                            act.wait_ge(gains_loaded, 16)
                        for k in range(KD):
                            c, cols = GAIN[phase] + k, slice(k * T, (k + 1) * T)
                            bias = 0.0 if phase == 2 else gains[:, c + KD:c + KD + 1]
                            last = nc.scalar.activation(hT[s][:, 0, k, :], src[:, cols], ACT.Identity,
                                                        bias=bias, scale=gains[:, c:c + 1])
                        last.then_inc(free, 1)
                    elif kind == "vproj":
                        t, c = i // 2, i % 2
                        copy(v[s][:, t, 512 * c:512 * c + 512], src[:, :]).then_inc(free, 1)
                    elif kind == "mctxT":
                        copy(hT[s][:, 1, :, :], src[:, :].rearrange("p (k t) -> p k t", k=KD)).then_inc(free, 1)
                    elif kind == "kproj":
                        copy(kT[s][:, 2 * i:2 * i + 2, :], src[:, :].rearrange("p (k t) -> p k t", k=2)).then_inc(free, 1)
                    elif kind == "qproj":
                        copy(qT[s][:, 2 * i:2 * i + 2, :], src[:, :].rearrange("p (k t) -> p k t", k=2),
                             -float(XD) ** -0.5).then_inc(free, 1)
                    elif kind == "ff1":
                        nc.scalar.activation(g_act[s][:, 2 * i:2 * i + 2, :], src[:, :].rearrange("p (k t) -> p k t", k=2),
                                             ACT.Gelu).then_inc(free, 1)
                    elif kind == "v":
                        if i == 0:
                            act.wait_ge(vs_zeroed, s + 1)
                        pairs = vs[s][:, i, :, :].rearrange("p (j c) d -> p j (c d)", c=2)
                        halves = src[:, 0:D].rearrange("p (j c d) -> p j c d", c=2, d=SD)
                        copy(pairs[:, :, 0:SD], halves[:, :, 0, :])
                        copy(pairs[:, :, 3 * SD:4 * SD], halves[:, :, 1, :]).then_inc(free, 1)
                    elif kind == "stackT":
                        block4 = src[:, :].rearrange("p (j q) -> p j q", j=4)
                        if phase == 1:
                            t, u = i // 4, i % 4
                            dst = (qs if u < 2 else ks)[s][:, 4 * (u % 2):4 * (u % 2) + 4, t * P:(t + 1) * P]
                        else:
                            t = i % TT
                            dst = (kc if i < TT else qc)[s][:, :, t * P:(t + 1) * P]
                        copy(dst, block4).then_inc(free, 1)
                    elif kind == "mem":
                        copy((kmem, vmem)[i][s][:, :, :], src[:, :].rearrange("p (k t) -> p k t", k=2),
                             (float(D) ** -0.5, 1.0)[i]).then_inc(free, 1)
                    elif kind == "gateup":
                        rows = slice(0, P if i < MT - 1 else MLAST)
                        nc.scalar.activation(sg[s][rows, i, :], src[rows, 0:T], ACT.Silu).then_inc(silu_ready, 1)
                    elif kind == "probs":
                        what, n = PHASES[phase], head_no(phase, s, i)
                        key = ("scores", phase, s, i)
                        act.wait_ge(negmax_ready, n + 1)
                        if n >= PROBS:
                            wait_filled(act, ("probsT", *head_at[n - PROBS]))
                        if n >= SMALL:
                            act.wait_ge(probs_ready, n - SMALL + 1)
                        for t in range(TT):
                            cols = (t + 1) * P if what == "self" else T
                            if what in ("x", "self"):
                                scores, sign = masked[:, n % MASKED, t, 0:cols], -1.0
                            else:
                                scores, sign = bank_of(key)[:, t * T:t * T + cols], 1.0
                            last = nc.scalar.activation(probs[:, n % PROBS, t, 0:cols], scores, ACT.Exp,
                                                        bias=negmax[:, n % SMALL, t:t + 1], scale=sign,
                                                        accum_out=sums[:, n % SMALL, t:t + 1])
                        last.then_inc(exp_ready, 1)
                    elif kind == "probsT":
                        n, cols = head_no(phase, s, i), 3 * P if PHASES[phase] == "self" else 2 * T
                        if n >= PTS:
                            p_, s_, i_ = head_at[n - PTS]
                            act.wait_ge(values_done, nth[("values", p_, s_, i_ // min(4, heads_of(p_)))])
                        wait_filled(act, step)
                        copy(probsT[:, n % PTS, 0:cols], bank_of(step)[:, 0:cols]).then_inc(drained[unit[step][0]], 1)
                    elif kind == "mgate":
                        wait_drained(act, step)
                        nc.scalar.activation(mg[s][:, :, :], mz[s][:, :, :], ACT.Sigmoid).then_inc(mgate_ready, 1)
                act.drain().then_inc(engines_done, 1)
                act.wait_ge(iteration_open, it + 1)

        @block.gpsimd
        def _(pool):
            def by_k(w):
                return w.rearrange("(k p) n -> p k n", p=P)

            pool.wait_ge(wq_loaded, 16)
            pool.dma_start(causal[:, :], consts["causal"]).then_inc(late_loaded, 16)
            pool.dma_start(w_memT[:, :], l2["W_mem"]).then_inc(late_loaded, 16)
            pool.dma_start(w_gate[:, :, :], by_k(l2["W_gate"])).then_inc(late_loaded, 16)
            pool.dma_start(fusion_rows[:, :, :], fusion_rows_in.partition_broadcast(P)).then_inc(late_loaded, 16)
            for e, w in enumerate(("v_qkv", "l_qkv")):
                pool.dma_start(w_qkv[:, e, :, :], by_k(l1[w])).then_inc(l1_loaded, 16)
            for e, w in enumerate(("v_dense", "l_dense")):
                pool.dma_start(w_dense[:, e, :, :], by_k(l1[w])).then_inc(l1_loaded, 16)
            pool.dma_start(w_cq[:, :, :], by_k(l1["cq_w"])).then_inc(l1_loaded, 16)
            pool.dma_start(w_cdense[:, :], l1["cdense_w"]).then_inc(l1_loaded, 16)
            nc.gpsimd.memset(half[:, :], -0.5).then_inc(setup_pool, 1)
            pool.wait_ge(setup_pool, 1)
            with pool.Fori(0, ITERS) as it:
                for step in order:
                    kind, phase, s, i = step
                    if kind in ("norm", "fuse"):
                        pool.wait_ge(var_ready, root_no[step])
                        nc.gpsimd.tensor_tensor(rstd[:, s, :], ms[:, s, :], half[:, :], ALU.pow).then_inc(rstd_ready, 1)
                    elif kind == "values" and phase == 0 and i == 3:
                        pool.wait_ge(values_done, nth[step])
                        nc.gpsimd.memset(vc[s][:, :, :, :], 0.0).then_inc(vc_zeroed, 1)
                        nc.gpsimd.memset(vs[s][:, :, :, :], 0.0).then_inc(vs_zeroed, 1)
                pool.drain().then_inc(engines_done, 1)
                pool.wait_ge(iteration_open, it + 1)

        @block.vector
        def _(dve):
            steps = [0]

            def then(ins):
                steps[0] += 1
                ins.then_inc(dve_step, 1)
                dve.wait_ge(dve_step, steps[0])

            def setup_then(ins):
                setup[0] += 1
                ins.then_inc(setup_step, 1)
                dve.wait_ge(setup_step, setup[0])

            ts, tt, copy = nc.vector.tensor_scalar, nc.vector.tensor_tensor, nc.vector.tensor_copy
            stt = nc.vector.scalar_tensor_tensor
            setup = [0]

            dve.wait_ge(pos_loaded, 16 * 2)
            setup_then(copy(pos_f[:, :], pos_raw[:, :]))
            setup_then(ts(pos_n[:, :], pos_f[:, :], 0.0, float(T), ALU.is_lt, ALU.mult))
            setup_then(tt(pos_f[:, :], pos_f[:, :], pos_n[:, :], ALU.add))
            setup_then(ts(pos_n[:, :], pos_f[:, :], 0.0, float(T - 1), ALU.max, ALU.min))
            for k in range(TT):
                last = ts(onehot[:, k, :], pos_n[:, :], iota[:, k:k + 1], None, ALU.is_equal)
            last.then_inc(setup_dve, 1)
            dve.wait_ge(setup_dve, 1)

            def root(s, step, mean_square):
                for t in range(TT):
                    last = nc.vector.bn_aggr(mv[:, s, t, :], stats[:, s, t, :])
                then(last)
                if mean_square:
                    then(tt(ms[:, s, :], mv[:, s, :, 0], mv[:, s, :, 0], ALU.mult))
                    stt(out=ms[:, s, :], in0=ms[:, s, :], scalar=RMS_EPS, in1=mv[:, s, :, 1],
                        op0=ALU.add, op1=ALU.add).then_inc(var_ready, 1)
                else:
                    ts(ms[:, s, :], mv[:, s, :, 1], LN_EPS, None, ALU.add).then_inc(var_ready, 1)
                dve.wait_ge(rstd_ready, root_no[step])

            def statistics(s, src):
                for t in range(TT):
                    last = nc.vector.bn_stats(stats[:, s, t, :], src[:, t, :])
                then(last)

            BEFORE_NORM = {1: ("ff2", 6), 2: ("out", 1), 5: ("out", 2), 6: ("out", 0), 10: ("out", 4)}

            with dve.Fori(0, ITERS) as it:
                dve.wait_ge(masks_loaded, it * (32 * SLOTS) + 32 * SLOTS)
                ts(media[:, :, :], media_raw[:, :, :], 0.0, NEG, ALU.is_equal, ALU.mult)
                eq = masked[:, 0, :, :]
                then(ts(eq, expert_raw[:, :, :], 1.0, None, ALU.is_equal))
                tt(expert[:, :, 0, 0:T - 1], eq[:, :, 0:T - 1], eq[:, :, 1:T], ALU.mult)
                then(nc.vector.memset(expert[:, :, 0, T - 1:T], 0.0))
                then(ts(expert[:, :, 1, :], expert[:, :, 0, :], -1.0, 1.0, ALU.mult, ALU.add))
                for step in order:
                    kind, phase, s, i = step
                    what = PHASES.get(phase)
                    if kind in ("out", "rows", "vproj", "hT", "qk", "ff2", "gateup", "down", "ckv", "cq", "mgate") and phase != 3 or kind == "mgate":
                        src = bank_of(step)
                        free = drained[unit[step][0]]
                    if kind == "qk" and s == 0 and i == 0:
                        dve.wait_ge(gains_loaded, 16)
                        dve.wait_ge(late_loaded, 16 * LATE_DMAS)
                    if kind == "norm":
                        if phase == 0:
                            if s == 0:
                                dve.wait_ge(x_loaded, it * (16 * SLOTS) + 16 * SLOTS)
                            wait_drained(dve, ("ctxT", 0, s, 0))
                        elif phase in BEFORE_NORM:
                            wait_drained(dve, (*BEFORE_NORM[phase], s, 0))
                        rms = phase in (1, 2, 5)
                        statistics(s, x[s])
                        root(s, step, rms)
                        for t in range(TT):
                            if rms:
                                last = ts(h[s][:, t, :], x[s][:, t, :], rstd[:, s, t:t + 1], None, ALU.mult)
                            else:
                                last = ts(h[s][:, t, :], x[s][:, t, :], mv[:, s, t, 0:1], rstd[:, s, t:t + 1],
                                          ALU.subtract, ALU.mult)
                        last.then_inc(h_ready, 1)
                    elif kind == "hT" and phase in (1, 5):
                        wait_filled(dve, step)
                        for k in range(KD):
                            c, cols = GAIN[phase] + k, slice(k * T, (k + 1) * T)
                            for e in range(2):
                                last = stt(out=hT[s][:, e, k, :], in0=src[:, cols], scalar=gains[:, c:c + 1],
                                           in1=expert[:, s, e, :], op0=ALU.mult, op1=ALU.mult)
                        last.then_inc(free, 1)
                    elif kind == "scores":
                        n = head_no(phase, s, i)
                        wait_filled(dve, step)
                        if n >= SMALL:
                            dve.wait_ge(exp_ready, n - SMALL + 1)
                        if what in ("x", "self"):
                            if n >= MASKED:
                                dve.wait_ge(exp_ready, n - MASKED + 1)
                            for t in range(TT):
                                if what == "x":
                                    cols, mask = T, media[:, s, :]
                                else:
                                    cols, mask = (t + 1) * P, causal[:, (TT - 1 - t) * P:TT * P]
                                last = nc.vector.tensor_tensor_reduce(
                                    out=masked[:, n % MASKED, t, 0:cols], in0=bank_of(step)[:, t * T:t * T + cols],
                                    in1=mask, scale=1.0, scalar=BIG, op0=ALU.add, op1=ALU.min,
                                    accum_out=negmax[:, n % SMALL, t:t + 1])
                            last.then_inc(negmax_ready, 1)
                        else:
                            nc.vector.tensor_reduce(negmax[:, n % SMALL, :],
                                                    bank_of(step)[:, :].rearrange("p (t k) -> p t k", t=TT),
                                                    AX_X, ALU.max, negate=True).then_inc(negmax_ready, 1)
                    elif kind == "probs":
                        n = head_no(phase, s, i)
                        dve.wait_ge(exp_ready, n + 1)
                        recip = nc.vector.reciprocal(rsum[:, n % SMALL, :], sums[:, n % SMALL, :])
                        if what == "mem":
                            recip.then_inc(probs_ready, 1)
                            continue
                        then(recip)
                        for t in range(TT):
                            cols = (t + 1) * P if what == "self" else T
                            p_t = probs[:, n % PROBS, t, 0:cols]
                            last = ts(p_t, p_t, rsum[:, n % SMALL, t:t + 1], None, ALU.mult)
                        last.then_inc(probs_ready, 1)
                    elif kind == "values":
                        key, _, closes = values_bank(phase, s, i)
                        if not closes:
                            continue
                        dve.wait_ge(values_done, nth[step])
                        O = bank_of(key)
                        if what == "x":
                            last = copy(qT[s][:, 2 * i:2 * i + 2, :], O[:, :].rearrange("p (k t) -> p k t", k=2))
                        elif what == "self":
                            for e in range(2):
                                last = tt(hT[s][:, e, i // 2, :], O[:, 0:T], expert[:, s, e, :], ALU.mult)
                        elif what == "cross":
                            last = copy(hT[s][:, 1, 0, :], O[:, 0:T])
                        else:
                            n = head_no(phase, s, 0)
                            dve.wait_ge(probs_ready, n + 1)
                            for t in range(TT):
                                last = ts(mctx[s][:, t, :], O[:, t * D:(t + 1) * D], rsum[:, n % SMALL, t:t + 1],
                                          None, ALU.mult)
                        last.then_inc(drained[unit[key][0]], 1)
                    elif kind == "rows":
                        wait_filled(dve, step)
                        copy(rot[:, :, :, :, :].rearrange("p t a b d -> p (t a b d)"),
                             src[:, 0:128]).then_inc(free, 1)
                    elif kind in ("out", "ff2", "down"):
                        wait_filled(dve, step)
                        if step == ("out", 0, 0, 0):
                            dve.wait_ge(setup_act, 1)
                        delta = src[:, :].rearrange("p (t d) -> p t d", t=TT)
                        if kind == "ff2" or what == "x":
                            g = {0: 0, 6: 1, 4: 2, 10: 3}[phase]
                            stt(out=x[s][:, :, :], in0=delta, scalar=gates[:, g:g + 1], in1=x[s][:, :, :],
                                op0=ALU.mult, op1=ALU.add).then_inc(free, 1)
                        else:
                            tt(x[s][:, :, :], delta, x[s][:, :, :], ALU.add).then_inc(free, 1)
                    elif kind == "rotary":
                        qk = ("qk", 1, s, i)
                        wait_filled(dve, qk)
                        src = bank_of(qk)[:, :].rearrange("p (w h d) -> p w h d", w=2, h=H)
                        n = s * TT + i
                        buf, half_d = n % 2, SD // 2
                        if n >= 2:
                            wait_filled(dve, ("stackT", 1, (n - 2) // TT, 4 * ((n - 2) % TT) + 3))
                        if n:
                            dve.wait_ge(stack_ready, n)
                        cos = rot[:, i, :, 0, :].unsqueeze(2)
                        sin = rot[:, i, :, 1, :].unsqueeze(2)
                        tt(rot_a, src, cos.to_broadcast([P, 2, H, SD]), ALU.mult)
                        tt(rot_b[:, :, :, 0:half_d], src[:, :, :, half_d:SD],
                           sin[:, :, :, 0:half_d].to_broadcast([P, 2, H, half_d]), ALU.mult)
                        ins = tt(rot_b[:, :, :, half_d:SD], src[:, :, :, 0:half_d],
                                 sin[:, :, :, half_d:SD].to_broadcast([P, 2, H, half_d]), ALU.mult)
                        ins.then_inc(drained[unit[qk][0]], 1)
                        wait_drained(dve, qk)
                        then(tt(rot_a, rot_a, rot_b, ALU.add))
                        q, k = rot_a[:, 0, :, :], rot_a[:, 1, :, :]
                        q2 = q.unsqueeze(2).to_broadcast([P, H, 2, SD])
                        copy(q_tmp[:, buf, :, 0:2, :].bitcast(F32R), q2)
                        k2 = k.unsqueeze(2).to_broadcast([P, H, 2, SD])
                        then(copy(k_tmp[:, buf, :, :, 0, :].bitcast(F32R), k2))
                        tt(q_tmp[:, buf, :, 2:4, :], q2, q_tmp[:, buf, :, 0:2, :], ALU.subtract)
                        tt(k_tmp[:, buf, :, :, 1, :], k2, k_tmp[:, buf, :, :, 0, :], ALU.subtract).then_inc(stack_ready, 1)
                    elif kind == "ksplit":
                        ckv = ("ckv", 2, s, 0)
                        wait_filled(dve, ckv)
                        both = bank_of(ckv)[:, :].rearrange("p (t w h d) -> p t w h d", t=TT, w=2, h=H)
                        for t in range(TT):
                            k2 = both[:, t, 0, :, :].unsqueeze(2).to_broadcast([P, H, 2, CD])
                            last = copy(kc_tmp[:, s, H * t:H * t + H, :, 0, :].bitcast(F32R), k2)
                        then(last)
                        for t in range(TT):
                            k2 = both[:, t, 0, :, :].unsqueeze(2).to_broadcast([P, H, 2, CD])
                            last = tt(kc_tmp[:, s, H * t:H * t + H, :, 1, :], k2,
                                      kc_tmp[:, s, H * t:H * t + H, :, 0, :], ALU.subtract)
                        last.then_inc(split_ready, 1)
                        dve.wait_ge(vc_zeroed, s + 1)
                        for c in range(4):
                            for t in range(TT):
                                heads = vc[s][:, t, :, :].rearrange("p (a c) d -> p a c d", c=4)
                                vals = both[:, t, 1, :, :].rearrange("p (a c) d -> p a c d", c=4)
                                last = copy(heads[:, :, c, CD * c:CD * c + CD], vals[:, :, c, :])
                        last.then_inc(drained[unit[ckv][0]], 1)
                    elif kind == "qsplit":
                        cq = ("cq", 2, s, 0)
                        wait_filled(dve, cq)
                        flat = bank_of(cq)[:, 0:TT * DC].rearrange("p (h d) -> p h d", d=CD)
                        ins = ts(qc_raw[:, s, :, :], flat, float(CD) ** -0.5, None, ALU.mult)
                        ins.then_inc(drained[unit[cq][0]], 1)
                        wait_drained(dve, cq)
                        q2 = qc_raw[:, s, :, :].unsqueeze(2).to_broadcast([P, TT * H, 2, CD])
                        then(copy(qc_tmp[:, s, :, 0:2, :].bitcast(F32R), q2))
                        tt(qc_tmp[:, s, :, 2:4, :], q2, qc_tmp[:, s, :, 0:2, :], ALU.subtract).then_inc(split_ready, 1)
                    elif kind == "gateup":
                        rows = slice(0, P if i < MT - 1 else MLAST)
                        dve.wait_ge(silu_ready, nth[step])
                        ins = tt(sg[s][rows, i, :], src[rows, T:2 * T], sg[s][rows, i, :], ALU.mult)
                        ins.then_inc(free, 1)
                        wait_drained(dve, step)
                        for e in range(2):
                            last = tt(acts[s][rows, e, i, :], sg[s][rows, i, :], expert[rows, s, e, :], ALU.mult)
                        last.then_inc(acts_ready, 1)
                    elif kind == "mgate":
                        wait_filled(dve, step)
                        tt(mz[s][:, :, :], src[:, :].rearrange("p (t d) -> p t d", t=TT),
                           fusion_rows[:, 0:1, :].to_broadcast([P, TT, D]), ALU.add).then_inc(free, 1)
                    elif kind == "fuse":
                        dve.wait_ge(mgate_ready, s + 1)
                        then(tt(mg[s], mg[s], mctx[s], ALU.mult))
                        then(tt(x[s], x[s], mg[s], ALU.add))
                        statistics(s, x[s])
                        root(s, step, True)
                        for t in range(TT):
                            last = stt(out=x[s][:, t, :], in0=x[s][:, t, :], scalar=rstd[:, s, t:t + 1],
                                       in1=fusion_rows[:, 1, :], op0=ALU.mult, op1=ALU.mult)
                        then(last)
                dve.drain().then_inc(engines_done, 1)
                dve.wait_ge(iteration_open, it + 1)


_X = ["Wq", "Wkv", "Wo", "W1", "W2"]
_L1 = ["v_qkv", "l_qkv", "v_dense", "l_dense", "cq_w", "ckv_w", "cdense_w", "v_gate", "v_up", "v_down", "l_gate",
       "l_up", "l_down"]
_GAINS = [f"L{n}_xattn_{g}" for n in (0, 3) for g in ("ln_q_g", "ln_q_b", "ln_ff_g", "ln_ff_b")]
_GAINS += [f"L1_xattn_{g}" for g in ("ln_in_w", "ln_post_attn_w", "ln_post_cross_w")]
_GATES = [f"L{n}_xattn_{g}" for n in (0, 3) for g in ("attn_gate", "ff_gate")]


def _constants():
    f = np.float32
    causal = np.zeros((P, 2 * P), f)
    causal[:, P:] = np.triu(np.full((P, P), NEG, f), 1)
    inv = f(1.0) / np.power(f(10000.0), np.arange(0, SD, 2, dtype=f) / f(SD), dtype=f)
    angle = np.outer(np.arange(T, dtype=f), inv)
    cos, sin = np.cos(angle), np.sin(angle)
    rows = np.concatenate([cos, cos, -sin, sin], -1)
    rot = np.concatenate([rows * f(-float(SD) ** -0.5), rows], -1).astype(f)
    iota = np.arange(T, dtype=f).reshape(TT, P).T.copy()
    return {"ident": np.eye(P, dtype=f), "causal": causal, "iota": iota, "rot": rot}


def kernel(**inputs):
    import concourse.bacc as _bacc
    from concourse.bass_utils import run_bass_kernel_spmd as _run

    nc = _bacc.Bacc("TRN2", target_bir_lowering=False, num_devices=1)
    arrays = {}

    def feed(name, a):
        a = np.ascontiguousarray(a)
        arrays[name] = a
        return nc.dram_tensor(name, a.shape, mybir.dt.from_np(a.dtype), kind="ExternalInput").ap()

    x = feed("x", inputs["x"])
    ctx = feed("ctx", inputs["ctx_1024"])
    pos = feed("pos", inputs["pos_1xS"])
    media = feed("media_mask", inputs["mask_BxS2_bk0"])
    expert = feed("expert_mask", inputs["mask_BxS_ik0"])
    xw = {n: {k: feed(f"L{n}_{k}", inputs[f"L{n}_xattn_{k}"]) for k in _X} for n in (0, 3)}
    l1 = {k: feed(f"L1_{k}", inputs[f"L1_xattn_{k}"]) for k in _L1}
    l2 = {k: feed(f"L2_{k}", np.asarray(inputs[f"L2_xattn_{k}"]).T) for k in ("W_mem", "W_gate")}
    columns = [np.asarray(inputs[k]).reshape(KD, P).T for k in _GAINS]
    gains = feed("gains", np.concatenate(columns, axis=1))
    gates = feed("gates", np.concatenate([np.asarray(inputs[k]) for k in _GATES]))
    fusion_rows = feed("fusion_rows", np.stack([np.asarray(inputs["L2_xattn_b_gate"]), np.asarray(inputs["L2_xattn_norm_w"])]))
    consts = {k: feed(f"const_{k}", a) for k, a in _constants().items()}
    out = nc.dram_tensor("out", (B, T, D), F32, kind="ExternalOutput").ap()
    fused_layers(nc, x, ctx, pos, media, expert, gains, gates, fusion_rows, xw, l1, l2, consts, out)
    r = _run(nc, [arrays], core_ids=[0])
    return r.results[0]["out"]
```

```python
from contextlib import ExitStack

import numpy as np
import concourse.bass as bass
from concourse import mybir

F32 = mybir.dt.float32
F32R = mybir.dt.float32r
I32 = mybir.dt.int32
U8 = mybir.dt.uint8
ALU = mybir.AluOpType
ACT = mybir.ActivationFunctionType
AX_X = mybir.AxisListType.X

P = 128
B, T, D = 4, 256, 256
TT, KD = T // P, D // P
DC = 128
SLOTS = 2
ITERS = B // SLOTS
H = 16
XD, INNER = 64, 1024
KI = INNER // P
FF = 1024
SD = D // H
CD = DC // H
MLP = 688
MT = -(-MLP // P)
MLAST = MLP - (MT - 1) * P
NEG = 1.0e30
BIG = 3.0e38
LN_EPS, RMS_EPS = 1e-5, 1e-6

BANKS = 8
RINGS = {"scores": (0, 4), "probsT": (4, 3), "values": (7, 1), "others": (4, 4)}
PROBS, PTS, SMALL, MASKED = 5, 8, 8, 2
DVE_MOVES = (1, 4)
LAG_T, LAG_O = 4, 7
PHASES = {0: "x", 1: "self", 2: "cross", 3: "mem", 4: "x"}


def schedule():
    matrix, vector = [], []

    def step(kind, phase, s, i=0):
        if kind not in NO_BANK:
            matrix.append((kind, phase, s, i))
        if kind in ("out", "ff2"):
            matrix.append((kind + "_rest", phase, s, i))
        vector.append((kind, phase, s, i))

    def run(kind, phase, s, n, first=0):
        for i in range(first, n):
            step(kind, phase, s, i)

    def each(kind, phase, n=1):
        for s in range(SLOTS):
            run(kind, phase, s, n)

    def attention(phase, heads, filler=()):
        items = [(phase, s, h) for s in range(SLOTS) for h in range(heads)]
        batch = min(4, heads)
        for i in range(len(items) + LAG_O):
            if i == len(items):
                for f in filler:
                    step(*f)
            if i < len(items):
                step("scores", *items[i])
            if 0 <= i - 1 < len(items):
                step("probs", *items[i - 1])
            if 0 <= i - LAG_T < len(items):
                step("probsT", *items[i - LAG_T])
            o = i - LAG_O
            if 0 <= o < len(items) and o % batch == batch - 1:
                phase, s, h = items[o]
                step("values", phase, s, h // batch)

    def norm(phase, s):
        step("stats", phase, s)
        step("norm", phase, s)

    def onward(last, last_phase, phase, filler=()):
        step(last, last_phase, 0)
        norm(phase, 0)
        late = phase in (6, 10, 1)
        if late:
            matrix.append((last, last_phase, 1, 0))
        else:
            step(last, last_phase, 1)
        for f in filler:
            step(*f)
        step("hT", phase, 0)
        if late:
            matrix.append((last + "_rest", last_phase, 1, 0))
            vector.append((last, last_phase, 1, 0))
        norm(phase, 1)

    def feed_forward(phase, filler=()):
        run("ff1", phase, 0, 2)
        step("hT", phase, 1)
        run("ff1", phase, 0, 4, 2)
        for f in filler:
            step(*f)
        run("ff1", phase, 1, 4)

    each("ctxT", 0)
    for s in range(SLOTS):
        norm(0, s)
    for s in range(SLOTS):
        run("kproj", 0, s, 4)
        run("vproj", 0, s, 4 - s)
    step("hT", 0, 0)
    step("vproj", 0, 1, 3)
    run("qproj", 0, 0, 2)
    step("hT", 0, 1)
    run("qproj", 0, 0, 4, 2)
    run("qproj", 0, 1, 4)
    attention(0, H)
    onward("out", 0, 6)
    feed_forward(6, [(kind, 2, s) for kind in ("ckv", "ksplit") for s in range(SLOTS)])
    for s in range(SLOTS):
        run("stackT", 2, s, TT)
    onward("ff2", 6, 1)
    tiles = [(s, t) for s in range(SLOTS) for t in range(TT)]
    for n in range(len(tiles) + 1):
        if n == 1:
            step("hT", 1, 1)
        if n < len(tiles):
            for kind in ("qk", "v", "rotary"):
                step(kind, 1, *tiles[n])
        if n:
            s, t = tiles[n - 1]
            run("stackT", 1, s, 4 * t + 4, 4 * t)
    attention(1, H)
    onward("out", 1, 2)
    step("cq", 2, 0)
    step("qsplit", 2, 0)
    step("hT", 2, 1)
    step("cq", 2, 1)
    step("qsplit", 2, 1)
    for s in range(SLOTS):
        run("stackT", 2, s, 2 * TT, TT)
    attention(2, H)
    onward("out", 2, 5, [("mem", 3, s, i) for s in range(SLOTS) for i in range(2)])
    run("gateup", 5, 0, 2)
    step("hT", 5, 1)
    run("gateup", 5, 0, MT, 2)
    run("gateup", 5, 1, MT)
    each("down", 5)
    each("hT", 3)
    attention(3, 1, [("kproj", 4, 0, i) for i in range(4)])
    each("mctxT", 3)
    step("mgate", 3, 0)
    run("vproj", 4, 0, 2)
    step("mgate", 3, 1)
    run("vproj", 4, 0, 4, 2)
    step("fuse", 3, 0)
    norm(4, 0)
    run("kproj", 4, 1, 4)
    step("fuse", 3, 1)
    norm(4, 1)
    run("vproj", 4, 1, 4)
    for s in range(SLOTS):
        step("hT", 4, s)
        run("qproj", 4, s, 4)
    attention(4, H)
    onward("out", 4, 10)
    feed_forward(10)
    each("ff2", 10)
    return matrix, vector


NO_BANK = {"stats", "norm", "rotary", "ksplit", "qsplit", "probs", "fuse", "out_rest", "ff2_rest"}


def head_of(phase, i):
    kind = PHASES[phase]
    if kind == "self":
        return 8 * (i // 8) + 2 * (i % 4) + i % 8 // 4
    if kind == "cross":
        return 4 * (i % 4) + i // 4
    return i


def values_bank(phase, s, b):
    per = {"x": 1, "self": 2, "cross": 4, "mem": 1}[PHASES[phase]]
    return ("O", phase, s, b // per), b % per == 0, b % per == per - 1


def fused_layers(
    nc, x_in, ctx_in, pos_in, media_mask_in, expert_mask_in, gains_in, gates_in, fusion_rows_in, xw, l1, l2, consts, out,
):
    matrix_order, vector_order = schedule()

    unit, fills = {}, {}
    turns, uses, filled_before = {r: 0 for r in RINGS}, [0] * BANKS, [0] * BANKS
    for kind, phase, s, i in matrix_order:
        if kind in NO_BANK:
            continue
        key = (kind, phase, s, i)
        ring = kind if kind in RINGS else "others"
        if kind == "values":
            key, opens, _ = values_bank(phase, s, i)
            if not opens:
                continue
        first, banks = RINGS[ring]
        b = first + turns[ring] % banks
        turns[ring] += 1
        unit[key] = (b, uses[b])
        uses[b] += 1
        if kind != "values":
            filled_before[b] += 1
            fills[key] = filled_before[b]

    nth = {}
    for order in (matrix_order, vector_order):
        seen = {}
        for step in order:
            seen[step[0]] = seen.get(step[0], 0) + 1
            assert nth.setdefault(step, seen[step[0]]) == seen[step[0]]

    with ExitStack() as ctx:
        top = [-(-nc.sbuf_base // 64) * 64]

        def place(name, shape, dtype=F32, at=None):
            size = int(np.prod(shape[1:])) * (1 if dtype == U8 else 4)
            offset = top[0] if at is None else at
            if at is None:
                top[0] += -(-size // 64) * 64
                assert top[0] <= nc.sbuf_usable_end, (name, top[0])
            tensor = nc.alloc_sbuf_tensor_at(name, list(shape), dtype, offset=offset)
            return tensor.ap() if hasattr(tensor, "ap") else tensor

        def region(size):
            at = top[0]
            top[0] += size
            assert top[0] <= nc.sbuf_usable_end, top[0]
            return at

        KB = 1024
        w_q = place("w_q", [P, KD, INNER])
        w_kv = place("w_kv", [P, 2 * INNER])
        w_o = place("w_o", [P, KI, D])
        w_ff = region((4 * KD * MLP + 2 * MT * D) * 4)
        w_1 = place("w_1", [P, KD, FF], at=w_ff)
        w_2 = place("w_2", [P, KI, D], at=w_ff + KD * FF * 4)
        w_gu = place("w_gu", [P, 4, KD, MLP], at=w_ff)
        w_down = place("w_down", [P, 2, MT, D], at=w_ff + 4 * KD * MLP * 4)
        w_qkv = place("w_qkv", [P, 2, KD, 3 * D])
        w_dense = place("w_dense", [P, 2, 2, D])
        w_cq = place("w_cq", [P, KD, DC])
        w_ckv = place("w_ckv", [P, 2 * DC])
        w_cdense = place("w_cdense", [P, D])
        w_gate = place("w_gate", [P, 2 * KD, D])
        w_memT = place("w_memT", [P, D])
        ident = place("ident", [P, P])
        causal = place("causal", [P, 2 * P])
        iota = place("iota", [P, TT])
        gains = place("gains", [P, 22])
        rot = place("rot", [P, TT, 2, 2, SD])
        half = place("half", [P, TT])
        ones = place("ones", [P, 6, 32])
        gates = place("gates", [P, 4])
        gates_raw = place("gates_raw", [P, 4])
        fusion_rows = place("fusion_rows", [P, 2, D])
        expert = place("expert", [P, SLOTS, 2, T])
        media = place("media", [P, SLOTS, T])
        media_raw = place("media_raw", [P, SLOTS, T], U8)
        x, h, hT, ctxT, kmem, vmem = [], [], [], [], [], []
        qT, kT, v, g_act, qs, ks, qc, kc, vs, vc, sg, acts, slot_at = ([] for _ in range(13))
        for s in range(SLOTS):
            x.append(place(f"x{s}", [P, TT, D]))
            h.append(place(f"h{s}", [P, TT, D]))
            hT.append(place(f"hT{s}", [P, 2, KD, T]))
            ctxT.append(place(f"ctxT{s}", [P, T]))
            kmem.append(place(f"kmem{s}", [P, KD, T]))
            vmem.append(place(f"vmem{s}", [P, TT, D]))
            big = region(24 * KB)
            slot_at.append(big)
            qT.append(place(f"qT{s}", [P, KI, T], at=big))
            kT.append(place(f"kT{s}", [P, KI, T], at=big + 8 * KB))
            v.append(place(f"v{s}", [P, TT, INNER], at=big + 16 * KB))
            g_act.append(place(f"g_act{s}", [P, KI, T], at=big))
            qs.append(place(f"qs{s}", [P, 8, T], F32R, at=big))
            ks.append(place(f"ks{s}", [P, 8, T], F32R, at=big + 8 * KB))
            qc.append(place(f"qc{s}", [P, 4, T], F32R, at=big))
            kc.append(place(f"kc{s}", [P, 4, T], F32R))
            vs.append(place(f"vs{s}", [P, TT, H, 32], at=big + 16 * KB))
            vc.append(place(f"vc{s}", [P, TT, H, 32], at=big + 20 * KB))
            sg.append(place(f"sg{s}", [P, MT, T], at=big))
            acts.append(place(f"acts{s}", [P, 2, MT, T], at=big + 6 * KB))
        ctx_in_sb = [h[s] for s in range(SLOTS)]
        masked = place("masked", [P, MASKED, TT, T])
        probs_at = region(PROBS * TT * T * 4)
        probs = place("probs", [P, PROBS, TT, T], at=probs_at)
        probsT_at = region(PTS * 2 * T * 4)
        probsT = place("probsT", [P, PTS, 2 * T], at=probsT_at)
        negmax = place("negmax", [P, SMALL, TT])
        sums = place("sums", [P, SMALL, TT])
        rsum = place("rsum", [P, SMALL, TT])
        stats = place("stats", [P, SLOTS, TT, 6])
        mv = place("mv", [P, SLOTS, TT, 2])
        ms = place("ms", [P, SLOTS, TT])
        rstd = place("rstd", [P, SLOTS, TT])
        q_tmp = place("q_tmp", [P, 2, H, 4, SD], at=probsT_at)
        k_tmp = place("k_tmp", [P, 2, H, 2, 2, SD], at=probsT_at + 8 * KB)
        rot_a = place("rot_a", [P, 2, H, SD], at=probs_at)
        rot_b = place("rot_b", [P, 2, H, SD], at=probs_at + 2 * KB)
        kc_tmp = place("kc_tmp", [P, SLOTS, TT * H, 2, 2, CD], at=probsT_at + 8 * KB)
        qc_tmp = [place(f"qc_tmp{s}", [P, TT * H, 4, CD], at=slot_at[s] + 8 * KB) for s in range(SLOTS)]
        qc_raw = [place(f"qc_raw{s}", [P, TT * H, CD], at=slot_at[s] + 12 * KB) for s in range(SLOTS)]
        pos_raw = place("pos_raw", [P, T], I32, at=probsT_at)
        pos_f = place("pos_f", [P, T], at=probsT_at + KB)
        pos_n = place("pos_n", [P, T], at=probsT_at + 2 * KB)
        onehot = place("onehot", [P, TT, T], at=probsT_at + 3 * KB)
        rot_tab = place("rot_tab", [P, TT, 64], at=probsT_at + 5 * KB)
        expert_raw = place("expert_raw", [P, SLOTS, T], I32)
        qT_at = [slot_at[s] for s in range(SLOTS)]
        mctx = [place(f"mctx{s}", [P, TT, D], at=qT_at[s]) for s in range(SLOTS)]
        mz = [place(f"mz{s}", [P, TT, D], at=qT_at[s] + 2 * KB) for s in range(SLOTS)]
        mg = [place(f"mg{s}", [P, TT, D], at=qT_at[s] + 4 * KB) for s in range(SLOTS)]

        bank = [ctx.enter_context(nc.psum_tensor(f"bank{i}", [P, 512], F32)) for i in range(8)]

        def sem(name):
            return ctx.enter_context(nc.semaphore(name))

        filled = [sem(f"bank{i}_filled") for i in range(8)]
        drained = [sem(f"bank{i}_drained") for i in range(8)]
        negmax_ready = sem("negmax_ready")
        exp_ready = sem("exp_ready")
        probs_ready = sem("probs_ready")
        values_done = sem("values_done")
        h_ready = sem("h_ready")
        var_ready = sem("var_ready")
        rstd_ready = sem("rstd_ready")
        stack_ready = sem("stack_ready")
        split_ready = sem("split_ready")
        silu_ready = sem("silu_ready")
        acts_ready = sem("acts_ready")
        mgate_ready = sem("mgate_ready")
        vs_zeroed = sem("vs_zeroed")
        vc_zeroed = sem("vc_zeroed")
        dve_step = sem("dve_step")
        ff0_loaded = sem("ff0_loaded")
        attn3_loaded = sem("attn3_loaded")
        mlp_loaded = sem("mlp_loaded")
        ff3_loaded = sem("ff3_loaded")
        engines_done = sem("engines_done")
        per_iteration = [s.num for s in (
            *filled, *drained, negmax_ready, exp_ready, probs_ready, values_done, h_ready, var_ready,
            rstd_ready, stack_ready, split_ready, silu_ready, acts_ready, mgate_ready, vs_zeroed, vc_zeroed, dve_step,
            ff0_loaded, attn3_loaded, mlp_loaded, ff3_loaded, engines_done)]
        assert per_iteration == list(range(per_iteration[0], per_iteration[0] + len(per_iteration)))
        iteration_open = sem("iteration_open")
        ident_loaded = sem("ident_loaded")
        ctx_loaded = sem("ctx_loaded")
        x_loaded = sem("x_loaded")
        masks_loaded = sem("masks_loaded")
        wk_loaded, wv_loaded, wq_loaded, wo_loaded = (sem(f"layer0_w{n}_loaded") for n in "kvqo")
        x_free = sem("x_free")
        pos_loaded = sem("pos_loaded")
        ckv_loaded = sem("ckv_loaded")
        l1_loaded = sem("l1_loaded")
        gates_loaded = sem("gates_loaded")
        gains_loaded = sem("gains_loaded")
        rot_tab_loaded = sem("rot_tab_loaded")
        late_loaded = sem("late_loaded")
        setup_pe = sem("setup_pe")
        setup_dve = sem("setup_dve")
        setup_act = sem("setup_act")
        setup_pool = sem("setup_pool")
        setup_step = sem("setup_step")

        ATTN_DMAS, FF_DMAS, MLP_DMAS, L1_DMAS, LATE_DMAS = 4, 2, 4 + 2 * 2, 6, 5

        GAIN = {0: 0, 6: 4, 4: 8, 10: 12, 1: 16, 5: 18, 2: 20}

        def bank_of(key):
            return bank[unit[key][0]]

        def wait_filled(eng, key):
            eng.wait_ge(filled[unit[key][0]], fills[key])

        def wait_drained(eng, key):
            b, n = unit[key]
            eng.wait_ge(drained[b], n + 1)

        def wait_free(pe, key):
            b, n = unit[key]
            if n:
                pe.wait_ge(drained[b], n)

        unit_kinds_act = {"ctxT", "kproj", "vproj", "qproj", "ff1", "v", "stackT", "mem", "gateup", "mctxT"}

        def heads_of(phase):
            return 1 if PHASES[phase] == "mem" else H

        def head_no(phase, s, hd):
            return nth[("scores", phase, s, hd)] - 1

        def by_no():
            return {head_no(p_, s_, i_): (p_, s_, i_) for k_, p_, s_, i_ in vector_order if k_ == "scores"}

        head_at = by_no()

        narrow = [PHASES[head_at[n][0]] in ("self", "cross") for n in range(len(head_at))]

        by_dve = [narrow[n] and n % 8 in DVE_MOVES for n in range(len(head_at))]

        def divided_no(n):
            return n + 1 - sum(narrow[:n + 1])

        def readers_no(n):
            phase, s, i = head_at[n]
            return nth[("values", phase, s, i // min(4, heads_of(phase)))]

        split_no = {step: n + 1 for n, step in enumerate(st for st in vector_order if st[0] in ("ksplit", "qsplit"))}
        root_no = {step: n + 1 for n, step in enumerate(st for st in vector_order if st[0] in ("stats", "fuse"))}

        block = ctx.enter_context(nc.Block())

        @block.sync
        def _(sp):
            def load_attention(layer, done):
                sp.dma_start(w_kv[:, 0:INNER], xw[layer]["Wkv"][:, 0:INNER]).then_inc(done[0], 16)
                sp.dma_start(w_kv[:, INNER:], xw[layer]["Wkv"][:, INNER:]).then_inc(done[1], 16)
                sp.dma_start(w_q[:, :, :], xw[layer]["Wq"].rearrange("(k p) n -> p k n", p=P)).then_inc(done[2], 16)
                sp.dma_start(w_o[:, :, :], xw[layer]["Wo"].rearrange("(k p) n -> p k n", p=P)).then_inc(done[3], 16)

            def load_ff(layer, done):
                sp.dma_start(w_1[:, :, :], xw[layer]["W1"].rearrange("(k p) n -> p k n", p=P)).then_inc(done, 16)
                sp.dma_start(w_2[:, :, :], xw[layer]["W2"].rearrange("(k p) n -> p k n", p=P)).then_inc(done, 16)

            def load_mlp(done):
                for n, w in enumerate(("v_gate", "l_gate", "v_up", "l_up")):
                    sp.dma_start(w_gu[:, n, :, :], l1[w].rearrange("(k p) n -> p k n", p=P)).then_inc(done, 16)
                for n, w in enumerate(("v_down", "l_down")):
                    full = (MT - 1) * P
                    sp.dma_start(w_down[:, n, 0:MT - 1, :],
                                 l1[w][0:full, :].rearrange("(k p) n -> p k n", p=P)).then_inc(done, 16)
                    sp.dma_start(w_down[0:MLAST, n, MT - 1, :], l1[w][full:MLP, :]).then_inc(done, 16)

            def load_ctx(first):
                for s in range(SLOTS):
                    sp.dma_start(ctx_in_sb[s][:, :, 0:DC],
                                 ctx_in[first + s].rearrange("(t p) d -> p t d", p=P)).then_inc(ctx_loaded, 16)

            def load_x(first):
                for s in range(SLOTS):
                    sp.dma_start(x[s][:, :, :], x_in[first + s].rearrange("(t p) d -> p t d", p=P)).then_inc(x_loaded, 16)
                for s in range(SLOTS):
                    sp.dma_start(media_raw[:, s, :], media_mask_in[first + s].partition_broadcast(P)).then_inc(masks_loaded, 16)
                    sp.dma_start(expert_raw[:, s, :], expert_mask_in[first + s].partition_broadcast(P)).then_inc(masks_loaded, 16)

            load_ctx(0)
            sp.dma_start(ident[:, :], consts["ident"]).then_inc(ident_loaded, 16)
            sp.dma_start(pos_raw[:, :], pos_in.partition_broadcast(P).rearrange("p a t -> p (a t)")).then_inc(pos_loaded, 16)
            sp.dma_start(iota[:, :], consts["iota"]).then_inc(pos_loaded, 16)
            sp.dma_start(rot_tab[:, :, :], consts["rot"].rearrange("(k p) n -> p k n", p=P)).then_inc(rot_tab_loaded, 16)
            sp.dma_start(gates_raw[:, :], gates_in.partition_broadcast(P)).then_inc(gates_loaded, 16)
            sp.dma_start(gains[:, :], gains_in).then_inc(gains_loaded, 16)
            sp.sem_inc(x_free, 16 * SLOTS)

            with sp.Fori(0, ITERS) as it:
                sp.wait_ge(x_free, it * (16 * SLOTS) + 16 * SLOTS)
                load_x(it * SLOTS)
                wait_filled(sp, ("qproj", 0, SLOTS - 1, 3))
                load_ff(0, ff0_loaded)
                wait_filled(sp, ("out", 0, SLOTS - 1, 0))
                load_attention(3, [attn3_loaded] * 4)
                wait_filled(sp, ("ff2", 6, SLOTS - 1, 0))
                load_mlp(mlp_loaded)
                wait_filled(sp, ("down", 5, SLOTS - 1, 0))
                load_ff(3, ff3_loaded)
                wait_filled(sp, ("out", 4, SLOTS - 1, 0))
                load_attention(0, [wk_loaded, wv_loaded, wq_loaded, wo_loaded])
                wait_filled(sp, ("ff2", 10, SLOTS - 1, 0))
                load_ctx(it * -SLOTS + (ITERS - 1) * SLOTS)
                for s in range(SLOTS):
                    wait_drained(sp, ("ff2", 10, s, 0))
                    sp.dma_start(out[it * SLOTS + s].rearrange("(t p) d -> p t d", p=P), x[s][:, :, :]).then_inc(x_free, 16)
                sp.wait_ge(engines_done, 4)
                sp.sem_clear(range(per_iteration[0], per_iteration[-1] + 1))
                sp.sem_inc(iteration_open, 1)
            sp.wait_ge(x_free, 16 * SLOTS * (ITERS + 1))
            for loaded in (wk_loaded, wv_loaded, wq_loaded, wo_loaded):
                sp.wait_ge(loaded, 16 * (ITERS + 1))
            sp.wait_ge(ctx_loaded, 16 * SLOTS * (ITERS + 1))

        @block.tensor
        def _(pe):
            mm, tr = nc.tensor.matmul, nc.tensor.transpose

            pe.wait_ge(rot_tab_loaded, 16)
            pe.wait_ge(setup_dve, 1)
            for t in range(TT):
                for k in range(TT):
                    last = mm(bank[0][:, 64 * t:64 * t + 64], onehot[:, k, t * P:(t + 1) * P], rot_tab[:, k, :],
                              start=(k == 0), stop=(k == TT - 1))
            last.then_inc(setup_pe, 1)
            pe.wait_ge(ident_loaded, 16)
            pe.wait_ge(setup_dve, 2)

            tok = lambda t: slice(t * P, (t + 1) * P)
            wide = lambda t: slice(t * T, (t + 1) * T)

            def wait_scores_bank(n):
                before = n - RINGS["scores"][1]
                if before >= 0:
                    taken = negmax_ready if PHASES[head_at[before][0]] in ("x", "self") else exp_ready
                    pe.wait_ge(taken, before + 1)

            def paired_scores(phase, s, hd):
                for a in range(2):
                    wait_scores_bank(head_no(phase, s, hd + a))
                if hd % 4 == 0:
                    wait_drained(pe, ("qproj", phase, s, hd // 4))
                    wait_drained(pe, ("kproj", phase, s, hd // 4))
                for t in range(TT):
                    for a in range(2):
                        key, r = ("scores", phase, s, hd + a), slice(XD * a, XD * a + XD)
                        last = mm(bank_of(key)[:, wide(t)], qT[s][r, hd // 2, tok(t)], kT[s][r, hd // 2, :],
                                  start=True, stop=True, tile_position=(XD * a, 0))
                        if t == TT - 1:
                            last.then_inc(filled[unit[key][0]], 1)

            def scores(phase, s, hd):
                kind = PHASES[phase]
                if kind == "x":
                    if hd % 2 == 0:
                        paired_scores(phase, s, hd)
                    return
                key, n = ("scores", phase, s, hd), head_no(phase, s, hd)
                wait_scores_bank(n)
                S = bank_of(key)[:, :].rearrange("p (t k) -> p t k", t=TT)
                if kind == "self":
                    if hd == 0:
                        for u in range(8):
                            wait_drained(pe, ("stackT", phase, s, u))
                    head = head_of(phase, hd)
                    j, r = head // 2, slice(64 * (head % 2), 64 * (head % 2) + 64)
                    for t in range(TT):
                        n = (t + 1) * P
                        last = mm(S[:, t, 0:n], qs[s][r, j, t * P:(t + 1) * P], ks[s][r, j, 0:n], start=True, stop=True)
                elif kind == "cross":
                    if hd == 0:
                        for u in range(2 * TT):
                            wait_drained(pe, ("stackT", phase, s, u))
                    head = head_of(phase, hd)
                    j, r = head // 4, slice(32 * (head % 4), 32 * (head % 4) + 32)
                    for t in range(TT):
                        last = mm(S[:, t, :], qc[s][r, j, t * P:(t + 1) * P], kc[s][r, j, :], start=True, stop=True,
                                  tile_position=(32 * (head % 4), 0))
                else:
                    wait_drained(pe, ("hT", 3, s, 0))
                    wait_drained(pe, ("mem", 3, s, 0))
                    for t in range(TT):
                        for k in range(KD):
                            last = mm(S[:, t, :], hT[s][:, 0, k, t * P:(t + 1) * P], kmem[s][:, k, :],
                                      start=(k == 0), stop=(k == KD - 1))
                last.then_inc(filled[unit[key][0]], 1)

            def probs_transposed(phase, s, hd):
                key, n = ("probsT", phase, s, hd), head_no(phase, s, hd)
                wait_free(pe, key)
                if narrow[n]:
                    pe.wait_ge(exp_ready, n + 1)
                else:
                    pe.wait_ge(probs_ready, divided_no(n))
                PT = bank_of(key)
                for t in range(TT):
                    for k in range(TT):
                        if PHASES[phase] == "self":
                            if k > t:
                                continue
                            at = t * P if k == 0 else 2 * P
                        else:
                            at = k * T + t * P
                        last = tr(PT[:, at:at + P], probs[:, n % PROBS, t, k * P:(k + 1) * P], ident[:, :])
                last.then_inc(filled[unit[key][0]], 1)

            def values(phase, s, b):
                kind = PHASES[phase]
                key, opens, closes = values_bank(phase, s, b)
                if opens:
                    wait_free(pe, key)
                O = bank_of(key)
                heads = [0] if kind == "mem" else [4 * b + a for a in range(4)]
                if b == 0:
                    if kind == "x":
                        for u in range(4):
                            wait_drained(pe, ("vproj", phase, s, u))
                    elif kind == "self":
                        for t in range(TT):
                            wait_drained(pe, ("v", 1, s, t))
                    elif kind == "cross":
                        wait_drained(pe, ("ckv", 2, s, 0))
                    else:
                        wait_drained(pe, ("mem", 3, s, 1))
                for hd in heads:
                    wait_drained(pe, ("probsT", phase, s, hd))
                if kind == "mem":
                    pt = probsT[:, head_no(phase, s, 0) % PTS, :].rearrange("p (k q) -> p k q", k=TT)
                    for t in range(TT):
                        for k in range(TT):
                            last = mm(O[:, t * D:(t + 1) * D], pt[:, k, t * P:(t + 1) * P], vmem[s][:, k, :],
                                      start=(k == 0), stop=(k == TT - 1))
                    last.then_inc(values_done, 1)
                    return
                for pair in ([0, 1], [2, 3]) if kind == "x" else ([0, 1, 2, 3],):
                    for k in range(TT):
                        for a in pair:
                            hd = heads[a]
                            pt = probsT[:, head_no(phase, s, hd) % PTS, :]
                            if kind == "x":
                                last = mm(O[XD * (a % 2):XD * (a % 2) + XD, T * (a // 2):T * (a // 2) + T],
                                          v[s][:, k, hd * XD:(hd + 1) * XD], pt[:, k * T:(k + 1) * T],
                                          start=(k == 0), stop=(k == TT - 1))
                            elif kind == "self":
                                first, final = b % 2 == 0 and k == 0, b % 2 == 1 and k == TT - 1
                                q0 = k * P
                                for at, columns in ((0, vs[s][:, k, head_of(phase, hd), :]), (T, ones[:, b % 2, :])):
                                    last = mm(O[32 * a:32 * a + 32, at + q0:at + T], columns,
                                              pt[:, k * T:k * T + T - q0], start=first and at == 0, stop=final and at == T,
                                              tile_position=(0, 32 * a))
                            else:
                                first, final = b == 0 and k == 0, b == 3 and k == TT - 1
                                for at, columns in ((0, vc[s][:, k, head_of(phase, hd), :]), (T, ones[:, 2 + b, :])):
                                    last = mm(O[32 * a:32 * a + 32, at:at + T], columns,
                                              pt[:, k * T:(k + 1) * T], start=first and at == 0, stop=final and at == T,
                                              tile_position=(0, 32 * a))
                last.then_inc(values_done, 1)

            def products(key, pieces):
                wait_free(pe, key)
                for cols, terms in pieces:
                    rows = terms[0][0].shape[-1]
                    for n, (stationary, moving) in enumerate(terms):
                        last = mm(bank_of(key)[0:rows, cols], stationary, moving,
                                  start=(n == 0), stop=(n == len(terms) - 1))
                last.then_inc(filled[unit[key][0]], 1)

            def most_and_rest(step, terms):
                kind, phase, s, _ = step
                rest = kind.endswith("_rest")
                key = (kind.removesuffix("_rest"), phase, s, 0)
                if not rest:
                    wait_free(pe, key)
                todo = [(t, n) for t in range(TT) for n in range(len(terms))]
                split = len(todo) - max(1, len(todo) // 4)
                for t, n in todo[split:] if rest else todo[:split]:
                    tiles, weights, k = terms[n]
                    last = mm(bank_of(key)[:, wide(t)], tiles[:, k, tok(t)], weights,
                              start=(n == 0), stop=(n == len(terms) - 1))
                if rest:
                    last.then_inc(filled[unit[key][0]], 1)

            def turn(key, tiles):
                wait_free(pe, key)
                for n, tile in enumerate(tiles):
                    last = tr(bank_of(key)[:, n * P:(n + 1) * P], tile, ident[:, :])
                last.then_inc(filled[unit[key][0]], 1)

            with pe.Fori(0, ITERS) as it:
                for step in matrix_order:
                    kind, phase, s, i = step
                    if kind == "scores":
                        if step == ("scores", 1, 0, 0):
                            pe.wait_ge(late_loaded, 16 * LATE_DMAS)
                        scores(phase, s, i)
                    elif kind == "probsT":
                        probs_transposed(phase, s, i)
                    elif kind == "values":
                        values(phase, s, i)
                    elif kind == "ctxT":
                        if s == 0:
                            pe.wait_ge(ctx_loaded, it * (16 * SLOTS) + 16 * SLOTS)
                        turn(step, [ctx_in_sb[s][:, t, 0:DC] for t in range(TT)])
                    elif kind == "hT":
                        if phase == 3:
                            wait_drained(pe, ("down", 5, s, 0))
                            src = x[s]
                        else:
                            pe.wait_ge(h_ready, nth[("norm", phase, s, 0)])
                            src = h[s]
                        turn(step, [src[:, t, tok(k)] for k in range(KD) for t in range(TT)])
                    elif kind == "mctxT":
                        wait_drained(pe, ("O", 3, s, 0))
                        turn(step, [mctx[s][:, t, tok(k)] for k in range(KD) for t in range(TT)])
                    elif kind == "kproj":
                        if s == 0 and i == 0:
                            wait_drained(pe, ("ctxT", 0, SLOTS - 1, 0))
                            if phase == 0:
                                pe.wait_ge(wk_loaded, it * 16 + 16)
                            else:
                                pe.wait_ge(attn3_loaded, 16 * ATTN_DMAS)
                        products(step, [(wide(n), [(w_kv[:, tok(2 * i + n)], ctxT[s][:, :])]) for n in range(2)])
                    elif kind == "vproj":
                        t, c = i // 2, i % 2
                        if step == ("vproj", 0, 0, 0):
                            pe.wait_ge(wv_loaded, it * 16 + 16)
                        products(step, [(slice(0, 512), [(ctxT[s][:, tok(t)], w_kv[:, INNER + 512 * c:INNER + 512 * c + 512])])])
                    elif kind == "qproj":
                        if i == 0:
                            wait_drained(pe, ("hT", phase, s, 0))
                        if step == ("qproj", 0, 0, 0):
                            pe.wait_ge(wq_loaded, it * 16 + 16)
                        products(step, [(wide(n), [(w_q[:, k, tok(2 * i + n)], hT[s][:, 0, k, :]) for k in range(KD)])
                                        for n in range(2)])
                    elif kind in ("out", "out_rest") and PHASES[phase] == "x":
                        if kind == "out":
                            for b in range(4):
                                wait_drained(pe, ("O", phase, s, b))
                        if step == ("out", 0, 0, 0):
                            pe.wait_ge(wo_loaded, it * 16 + 16)
                        most_and_rest(step, [(qT[s], w_o[:, k, :], k) for k in range(KI)])
                    elif kind == "ff1":
                        if i == 0:
                            wait_drained(pe, ("hT", phase, s, 0))
                            if s == 0:
                                pe.wait_ge(ff0_loaded if phase == 6 else ff3_loaded, 16 * FF_DMAS)
                        products(step, [(wide(n), [(w_1[:, k, tok(2 * i + n)], hT[s][:, 0, k, :]) for k in range(KD)])
                                        for n in range(2)])
                    elif kind in ("ff2", "ff2_rest"):
                        if kind == "ff2":
                            for u in range(4):
                                wait_drained(pe, ("ff1", phase, s, u))
                        most_and_rest(step, [(g_act[s], w_2[:, k, :], k) for k in range(KI)])
                    elif kind == "qk":
                        if i == 0:
                            wait_drained(pe, ("hT", 1, s, 0))
                            if s == 0:
                                pe.wait_ge(l1_loaded, 16 * L1_DMAS)
                        products(step, [(slice(0, 512), [(hT[s][:, e, k, tok(i)], w_qkv[:, e, k, 0:512])
                                                         for e in range(2) for k in range(KD)])])
                    elif kind == "v":
                        products(step, [(slice(0, 256), [(hT[s][:, e, k, tok(i)], w_qkv[:, e, k, 512:768])
                                                         for e in range(2) for k in range(KD)])])
                    elif kind == "stackT":
                        if phase == 1:
                            t, u = i // 4, i % 4
                            if u == 0:
                                pe.wait_ge(stack_ready, nth[("rotary", 1, s, t)])
                            buf = (s * TT + t) % 2
                            if u < 2:
                                tiles = [q_tmp[:, buf, 8 * u + 2 * j:8 * u + 2 * j + 2, :, :] for j in range(4)]
                            else:
                                tiles = [k_tmp[:, buf, 8 * (u - 2) + 2 * j:8 * (u - 2) + 2 * j + 2, :, :, :] for j in range(4)]
                        else:
                            t, which = i % TT, i // TT
                            if t == 0:
                                pe.wait_ge(split_ready, split_no[("ksplit", "qsplit")[which], 2, s, 0])
                            if which == 0:
                                tiles = [kc_tmp[:, s, H * t + 4 * j:H * t + 4 * j + 4, :, :, :] for j in range(4)]
                            else:
                                tiles = [qc_tmp[s][:, H * t + 4 * j:H * t + 4 * j + 4, :, :] for j in range(4)]
                        turn(step, tiles)
                    elif kind in ("out", "out_rest") and phase == 1:
                        if kind == "out":
                            for g in range(2):
                                wait_drained(pe, ("O", 1, s, g))
                        most_and_rest(step, [(hT[s][:, e, :, :], w_dense[:, e, g, :], g)
                                             for e in range(2) for g in range(2)])
                    elif kind == "ckv":
                        if s == 0:
                            pe.wait_ge(ckv_loaded, 16)
                        products(step, [(wide(t), [(ctxT[s][:, tok(t)], w_ckv[:, :])]) for t in range(TT)])
                    elif kind == "cq":
                        wait_drained(pe, ("hT", 2, s, 0))
                        products(step, [(tok(t), [(hT[s][:, 0, k, tok(t)], w_cq[:, k, :]) for k in range(KD)])
                                        for t in range(TT)])
                    elif kind in ("out", "out_rest") and phase == 2:
                        if kind == "out":
                            wait_drained(pe, ("O", 2, s, 0))
                        most_and_rest(step, [(hT[s][:, 1, :, :], w_cdense[:, :], 0)])
                    elif kind == "gateup":
                        if i == 0:
                            wait_drained(pe, ("hT", 5, s, 0))
                            if s == 0:
                                pe.wait_ge(mlp_loaded, 16 * MLP_DMAS)
                        cols = slice(i * P, min(MLP, (i + 1) * P))
                        products(step, [(wide(n), [(w_gu[:, 2 * n + e, k, cols], hT[s][:, e, k, :])
                                                   for e in range(2) for k in range(KD)]) for n in range(2)])
                    elif kind == "down":
                        pe.wait_ge(acts_ready, nth[("gateup", 5, s, MT - 1)])
                        rows = [slice(0, P if m < MT - 1 else MLAST) for m in range(MT)]
                        products(step, [(wide(t), [(acts[s][rows[m], e, m, tok(t)], w_down[rows[m], e, m, :])
                                                   for m in range(MT) for e in range(2)]) for t in range(TT)])
                    elif kind == "mem":
                        if i == 0:
                            if s == 0:
                                pe.wait_ge(late_loaded, 16 * LATE_DMAS)
                            products(step, [(wide(k), [(w_memT[:, tok(k)], ctxT[s][:, :])]) for k in range(KD)])
                        else:
                            products(step, [(wide(t), [(ctxT[s][:, tok(t)], w_memT[:, :])]) for t in range(TT)])
                    elif kind == "mgate":
                        wait_drained(pe, ("mctxT", 3, s, 0))
                        products(step, [(wide(t), [(hT[s][:, e, k, tok(t)], w_gate[:, 2 * e + k, :])
                                                   for e in range(2) for k in range(KD)]) for t in range(TT)])
                pe.drain().then_inc(engines_done, 1)
                pe.wait_ge(iteration_open, it + 1)

        @block.scalar
        def _(act):
            def copy(dst, src, scale=1.0):
                return nc.scalar.activation(dst, src, ACT.Copy, scale=scale)

            def by_k(w):
                return w.rearrange("(k p) n -> p k n", p=P)

            act.dma_start(w_kv[:, 0:INNER], xw[0]["Wkv"][:, 0:INNER]).then_inc(wk_loaded, 16)
            act.wait_ge(rot_tab_loaded, 16)
            act.dma_start(w_kv[:, INNER:], xw[0]["Wkv"][:, INNER:]).then_inc(wv_loaded, 16)
            act.dma_start(w_q[:, :, :], by_k(xw[0]["Wq"])).then_inc(wq_loaded, 16)
            act.dma_start(w_o[:, :, :], by_k(xw[0]["Wo"])).then_inc(wo_loaded, 16)
            act.dma_start(w_ckv[:, :], l1["ckv_w"]).then_inc(ckv_loaded, 16)
            act.wait_ge(gates_loaded, 16)
            nc.scalar.activation(gates[:, :], gates_raw[:, :], ACT.Tanh).then_inc(setup_act, 1)

            with act.Fori(0, ITERS) as it:
                for step in vector_order:
                    kind, phase, s, i = step
                    if kind in unit_kinds_act or (kind == "hT" and phase not in (1, 5)):
                        wait_filled(act, step)
                        src = bank_of(step)
                        free = drained[unit[step][0]]
                    if kind == "ctxT":
                        copy(ctxT[s][:, :], src[:, 0:T]).then_inc(free, 1)
                    elif kind == "hT" and phase == 3:
                        copy(hT[s][:, 0, :, :], src[:, :].rearrange("p (k t) -> p k t", k=KD)).then_inc(free, 1)
                    elif kind == "hT" and phase not in (1, 5):
                        if phase == 0:
                            act.wait_ge(gains_loaded, 16)
                        for k in range(KD):
                            c, cols = GAIN[phase] + k, slice(k * T, (k + 1) * T)
                            bias = 0.0 if phase == 2 else gains[:, c + KD:c + KD + 1]
                            last = nc.scalar.activation(hT[s][:, 0, k, :], src[:, cols], ACT.Identity,
                                                        bias=bias, scale=gains[:, c:c + 1])
                        last.then_inc(free, 1)
                    elif kind == "vproj":
                        t, c = i // 2, i % 2
                        copy(v[s][:, t, 512 * c:512 * c + 512], src[:, :]).then_inc(free, 1)
                    elif kind == "mctxT":
                        copy(hT[s][:, 1, :, :], src[:, :].rearrange("p (k t) -> p k t", k=KD)).then_inc(free, 1)
                    elif kind == "kproj":
                        copy(kT[s][:, 2 * i:2 * i + 2, :], src[:, :].rearrange("p (k t) -> p k t", k=2)).then_inc(free, 1)
                    elif kind == "qproj":
                        copy(qT[s][:, 2 * i:2 * i + 2, :], src[:, :].rearrange("p (k t) -> p k t", k=2),
                             -float(XD) ** -0.5).then_inc(free, 1)
                    elif kind == "ff1":
                        nc.scalar.activation(g_act[s][:, 2 * i:2 * i + 2, :], src[:, :].rearrange("p (k t) -> p k t", k=2),
                                             ACT.Gelu).then_inc(free, 1)
                    elif kind == "v":
                        if i == 0:
                            act.wait_ge(vs_zeroed, s + 1)
                        pairs = vs[s][:, i, :, :].rearrange("p (j c) d -> p j (c d)", c=2)
                        halves = src[:, 0:D].rearrange("p (j c d) -> p j c d", c=2, d=SD)
                        copy(pairs[:, :, 0:SD], halves[:, :, 0, :])
                        copy(pairs[:, :, 3 * SD:4 * SD], halves[:, :, 1, :]).then_inc(free, 1)
                    elif kind == "stackT":
                        block4 = src[:, :].rearrange("p (j q) -> p j q", j=4)
                        if phase == 1:
                            t, u = i // 4, i % 4
                            dst = (qs if u < 2 else ks)[s][:, 4 * (u % 2):4 * (u % 2) + 4, t * P:(t + 1) * P]
                        else:
                            t = i % TT
                            dst = (kc if i < TT else qc)[s][:, :, t * P:(t + 1) * P]
                        copy(dst, block4).then_inc(free, 1)
                    elif kind == "mem":
                        copy((kmem, vmem)[i][s][:, :, :], src[:, :].rearrange("p (k t) -> p k t", k=2),
                             (float(D) ** -0.5, 1.0)[i]).then_inc(free, 1)
                    elif kind == "gateup":
                        rows = slice(0, P if i < MT - 1 else MLAST)
                        nc.scalar.activation(sg[s][rows, i, :], src[rows, 0:T], ACT.Silu).then_inc(silu_ready, 1)
                    elif kind == "probs":
                        what, n = PHASES[phase], head_no(phase, s, i)
                        key = ("scores", phase, s, i)
                        act.wait_ge(negmax_ready, n + 1)
                        if n >= PROBS:
                            wait_filled(act, ("probsT", *head_at[n - PROBS]))
                        if n >= SMALL and not narrow[n] and not narrow[n - SMALL]:
                            act.wait_ge(probs_ready, divided_no(n - SMALL))
                        for t in range(TT):
                            cols = (t + 1) * P if what == "self" else T
                            if what in ("x", "self"):
                                scores, sign = masked[:, n % MASKED, t, 0:cols], -1.0
                            else:
                                scores, sign = bank_of(key)[:, t * T:t * T + cols], 1.0
                            summed = {} if narrow[n] else {"accum_out": sums[:, n % SMALL, t:t + 1]}
                            last = nc.scalar.activation(probs[:, n % PROBS, t, 0:cols], scores, ACT.Exp,
                                                        bias=negmax[:, n % SMALL, t:t + 1], scale=sign, **summed)
                        last.then_inc(exp_ready, 1)
                    elif kind == "probsT" and not by_dve[head_no(phase, s, i)]:
                        n, cols = head_no(phase, s, i), 3 * P if PHASES[phase] == "self" else 2 * T
                        if n >= PTS:
                            act.wait_ge(values_done, readers_no(n - PTS))
                        wait_filled(act, step)
                        copy(probsT[:, n % PTS, 0:cols], bank_of(step)[:, 0:cols]).then_inc(drained[unit[step][0]], 1)
                    elif kind == "mgate":
                        wait_drained(act, step)
                        nc.scalar.activation(mg[s][:, :, :], mz[s][:, :, :], ACT.Sigmoid).then_inc(mgate_ready, 1)
                act.drain().then_inc(engines_done, 1)
                act.wait_ge(iteration_open, it + 1)

        @block.gpsimd
        def _(pool):
            def by_k(w):
                return w.rearrange("(k p) n -> p k n", p=P)

            pool.wait_ge(wq_loaded, 16)
            pool.dma_start(ones[:, :, :], consts["ones"].rearrange("p (n c) -> p n c", c=32)).then_inc(late_loaded, 16)
            pool.dma_start(causal[:, :], consts["causal"]).then_inc(late_loaded, 16)
            pool.dma_start(w_memT[:, :], l2["W_mem"]).then_inc(late_loaded, 16)
            pool.dma_start(w_gate[:, :, :], by_k(l2["W_gate"])).then_inc(late_loaded, 16)
            pool.dma_start(fusion_rows[:, :, :], fusion_rows_in.partition_broadcast(P)).then_inc(late_loaded, 16)
            for e, w in enumerate(("v_qkv", "l_qkv")):
                pool.dma_start(w_qkv[:, e, :, :], by_k(l1[w])).then_inc(l1_loaded, 16)
            for e, w in enumerate(("v_dense", "l_dense")):
                pool.dma_start(w_dense[:, e, :, :], by_k(l1[w])).then_inc(l1_loaded, 16)
            pool.dma_start(w_cq[:, :, :], by_k(l1["cq_w"])).then_inc(l1_loaded, 16)
            pool.dma_start(w_cdense[:, :], l1["cdense_w"]).then_inc(l1_loaded, 16)
            nc.gpsimd.memset(half[:, :], -0.5).then_inc(setup_pool, 1)
            pool.wait_ge(setup_pool, 1)
            with pool.Fori(0, ITERS) as it:
                for step in vector_order:
                    kind, phase, s, i = step
                    if kind in ("stats", "fuse"):
                        pool.wait_ge(var_ready, root_no[step])
                        nc.gpsimd.tensor_tensor(rstd[:, s, :], ms[:, s, :], half[:, :], ALU.pow).then_inc(rstd_ready, 1)
                    elif kind == "values" and phase == 0 and i == 3:
                        pool.wait_ge(values_done, nth[step])
                        nc.gpsimd.memset(vc[s][:, :, :, :], 0.0).then_inc(vc_zeroed, 1)
                        nc.gpsimd.memset(vs[s][:, :, :, :], 0.0).then_inc(vs_zeroed, 1)
                pool.drain().then_inc(engines_done, 1)
                pool.wait_ge(iteration_open, it + 1)

        @block.vector
        def _(dve):
            steps = [0]

            def then(ins):
                steps[0] += 1
                ins.then_inc(dve_step, 1)
                dve.wait_ge(dve_step, steps[0])

            def setup_then(ins):
                setup[0] += 1
                ins.then_inc(setup_step, 1)
                dve.wait_ge(setup_step, setup[0])

            ts, tt, copy = nc.vector.tensor_scalar, nc.vector.tensor_tensor, nc.vector.tensor_copy
            stt = nc.vector.scalar_tensor_tensor
            setup = [0]

            dve.wait_ge(pos_loaded, 16 * 2)
            setup_then(copy(pos_f[:, :], pos_raw[:, :]))
            setup_then(ts(pos_n[:, :], pos_f[:, :], 0.0, float(T), ALU.is_lt, ALU.mult))
            setup_then(tt(pos_f[:, :], pos_f[:, :], pos_n[:, :], ALU.add))
            setup_then(ts(pos_n[:, :], pos_f[:, :], 0.0, float(T - 1), ALU.max, ALU.min))
            for k in range(TT):
                last = ts(onehot[:, k, :], pos_n[:, :], iota[:, k:k + 1], None, ALU.is_equal)
            last.then_inc(setup_dve, 1)
            dve.wait_ge(setup_pe, 1)
            copy(rot[:, :, :, :, :].rearrange("p t a b d -> p (t a b d)"), bank[0][:, 0:128]).then_inc(setup_dve, 1)
            dve.wait_ge(setup_dve, 2)

            def statistics(s, src, mean_square):
                for t in range(TT):
                    last = nc.vector.bn_stats(stats[:, s, t, :], src[:, t, :])
                then(last)
                for t in range(TT):
                    last = nc.vector.bn_aggr(mv[:, s, t, :], stats[:, s, t, :])
                then(last)
                if mean_square:
                    then(tt(ms[:, s, :], mv[:, s, :, 0], mv[:, s, :, 0], ALU.mult))
                    stt(out=ms[:, s, :], in0=ms[:, s, :], scalar=RMS_EPS, in1=mv[:, s, :, 1],
                        op0=ALU.add, op1=ALU.add).then_inc(var_ready, 1)
                else:
                    ts(ms[:, s, :], mv[:, s, :, 1], LN_EPS, None, ALU.add).then_inc(var_ready, 1)

            BEFORE_NORM = {1: ("ff2", 6), 2: ("out", 1), 5: ("out", 2), 6: ("out", 0), 10: ("out", 4)}

            with dve.Fori(0, ITERS) as it:
                dve.wait_ge(masks_loaded, it * (32 * SLOTS) + 32 * SLOTS)
                ts(media[:, :, :], media_raw[:, :, :], 0.0, NEG, ALU.is_equal, ALU.mult)
                eq = masked[:, 0, :, :]
                then(ts(eq, expert_raw[:, :, :], 1.0, None, ALU.is_equal))
                tt(expert[:, :, 0, 0:T - 1], eq[:, :, 0:T - 1], eq[:, :, 1:T], ALU.mult)
                then(nc.vector.memset(expert[:, :, 0, T - 1:T], 0.0))
                then(ts(expert[:, :, 1, :], expert[:, :, 0, :], -1.0, 1.0, ALU.mult, ALU.add))
                for step in vector_order:
                    kind, phase, s, i = step
                    what = PHASES.get(phase)
                    if kind in ("out", "hT", "qk", "ff2", "gateup", "down", "ckv", "cq", "mgate") and phase != 3 or kind == "mgate":
                        src = bank_of(step)
                        free = drained[unit[step][0]]
                    if kind == "qk" and s == 0 and i == 0:
                        dve.wait_ge(gains_loaded, 16)
                        dve.wait_ge(late_loaded, 16 * LATE_DMAS)
                    rms = phase in (1, 2, 5)
                    if kind == "stats":
                        if phase == 0 and s == 0:
                            dve.wait_ge(x_loaded, it * (16 * SLOTS) + 16 * SLOTS)
                        elif phase in BEFORE_NORM:
                            wait_drained(dve, (*BEFORE_NORM[phase], s, 0))
                        statistics(s, x[s], rms)
                    elif kind == "norm":
                        if phase == 0:
                            wait_drained(dve, ("ctxT", 0, s, 0))
                        dve.wait_ge(rstd_ready, root_no[("stats", phase, s, 0)])
                        for t in range(TT):
                            if rms:
                                last = ts(h[s][:, t, :], x[s][:, t, :], rstd[:, s, t:t + 1], None, ALU.mult)
                            else:
                                last = ts(h[s][:, t, :], x[s][:, t, :], mv[:, s, t, 0:1], rstd[:, s, t:t + 1],
                                          ALU.subtract, ALU.mult)
                        last.then_inc(h_ready, 1)
                    elif kind == "hT" and phase in (1, 5):
                        wait_filled(dve, step)
                        for k in range(KD):
                            c, cols = GAIN[phase] + k, slice(k * T, (k + 1) * T)
                            for e in range(2):
                                last = stt(out=hT[s][:, e, k, :], in0=src[:, cols], scalar=gains[:, c:c + 1],
                                           in1=expert[:, s, e, :], op0=ALU.mult, op1=ALU.mult)
                        last.then_inc(free, 1)
                    elif kind == "scores":
                        n = head_no(phase, s, i)
                        wait_filled(dve, step)
                        if n >= SMALL:
                            dve.wait_ge(exp_ready, n - SMALL + 1)
                        if what in ("x", "self"):
                            if n >= MASKED:
                                dve.wait_ge(exp_ready, n - MASKED + 1)
                            for t in range(TT):
                                if what == "x":
                                    cols, mask = T, media[:, s, :]
                                else:
                                    cols, mask = (t + 1) * P, causal[:, (TT - 1 - t) * P:TT * P]
                                last = nc.vector.tensor_tensor_reduce(
                                    out=masked[:, n % MASKED, t, 0:cols], in0=bank_of(step)[:, t * T:t * T + cols],
                                    in1=mask, scale=1.0, scalar=BIG, op0=ALU.add, op1=ALU.min,
                                    accum_out=negmax[:, n % SMALL, t:t + 1])
                            last.then_inc(negmax_ready, 1)
                        else:
                            nc.vector.tensor_reduce(negmax[:, n % SMALL, :],
                                                    bank_of(step)[:, :].rearrange("p (t k) -> p t k", t=TT),
                                                    AX_X, ALU.max, negate=True).then_inc(negmax_ready, 1)
                    elif kind == "probsT" and by_dve[head_no(phase, s, i)]:
                        n, cols = head_no(phase, s, i), 3 * P if what == "self" else 2 * T
                        dve.wait_ge(values_done, readers_no(n - PTS))
                        wait_filled(dve, step)
                        copy(probsT[:, n % PTS, 0:cols], bank_of(step)[:, 0:cols]).then_inc(drained[unit[step][0]], 1)
                    elif kind == "probs" and not narrow[head_no(phase, s, i)]:
                        n = head_no(phase, s, i)
                        dve.wait_ge(exp_ready, n + 1)
                        recip = nc.vector.reciprocal(rsum[:, n % SMALL, :], sums[:, n % SMALL, :])
                        if what == "mem":
                            recip.then_inc(probs_ready, 1)
                            continue
                        then(recip)
                        for t in range(TT):
                            cols = (t + 1) * P if what == "self" else T
                            p_t = probs[:, n % PROBS, t, 0:cols]
                            last = ts(p_t, p_t, rsum[:, n % SMALL, t:t + 1], None, ALU.mult)
                        last.then_inc(probs_ready, 1)
                    elif kind == "values":
                        key, _, closes = values_bank(phase, s, i)
                        if not closes:
                            continue
                        dve.wait_ge(values_done, nth[step])
                        O = bank_of(key)
                        if what == "x":
                            last = copy(qT[s][:, 2 * i:2 * i + 2, :], O[:, :].rearrange("p (k t) -> p k t", k=2))
                        elif what in ("self", "cross"):
                            rsums, divided = h[s][:, 0, :], h[s][:, 1, :]
                            if what == "self" and i // 2:
                                wait_drained(dve, ("O", phase, s, i // 2 - 1))
                            then(nc.vector.reciprocal(rsums, O[:, T:2 * T]))
                            if what == "self":
                                then(tt(divided, O[:, 0:T], rsums, ALU.mult))
                                for e in range(2):
                                    last = tt(hT[s][:, e, i // 2, :], divided, expert[:, s, e, :], ALU.mult)
                            else:
                                last = tt(hT[s][:, 1, 0, :], O[:, 0:T], rsums, ALU.mult)
                        else:
                            n = head_no(phase, s, 0)
                            dve.wait_ge(probs_ready, divided_no(n))
                            for t in range(TT):
                                last = ts(mctx[s][:, t, :], O[:, t * D:(t + 1) * D], rsum[:, n % SMALL, t:t + 1],
                                          None, ALU.mult)
                        last.then_inc(drained[unit[key][0]], 1)
                    elif kind in ("out", "ff2", "down"):
                        wait_filled(dve, step)
                        if step == ("out", 0, 0, 0):
                            dve.wait_ge(setup_act, 1)
                        delta = src[:, :].rearrange("p (t d) -> p t d", t=TT)
                        if kind == "ff2" or what == "x":
                            g = {0: 0, 6: 1, 4: 2, 10: 3}[phase]
                            stt(out=x[s][:, :, :], in0=delta, scalar=gates[:, g:g + 1], in1=x[s][:, :, :],
                                op0=ALU.mult, op1=ALU.add).then_inc(free, 1)
                        else:
                            tt(x[s][:, :, :], delta, x[s][:, :, :], ALU.add).then_inc(free, 1)
                    elif kind == "rotary":
                        qk = ("qk", 1, s, i)
                        wait_filled(dve, qk)
                        src = bank_of(qk)[:, :].rearrange("p (w h d) -> p w h d", w=2, h=H)
                        n = s * TT + i
                        buf, half_d = n % 2, SD // 2
                        if n >= 2:
                            wait_filled(dve, ("stackT", 1, (n - 2) // TT, 4 * ((n - 2) % TT) + 3))
                        if n:
                            dve.wait_ge(stack_ready, n)
                        cos = rot[:, i, :, 0, :].unsqueeze(2)
                        sin = rot[:, i, :, 1, :].unsqueeze(2)
                        tt(rot_a, src, cos.to_broadcast([P, 2, H, SD]), ALU.mult)
                        tt(rot_b[:, :, :, 0:half_d], src[:, :, :, half_d:SD],
                           sin[:, :, :, 0:half_d].to_broadcast([P, 2, H, half_d]), ALU.mult)
                        ins = tt(rot_b[:, :, :, half_d:SD], src[:, :, :, 0:half_d],
                                 sin[:, :, :, half_d:SD].to_broadcast([P, 2, H, half_d]), ALU.mult)
                        ins.then_inc(drained[unit[qk][0]], 1)
                        wait_drained(dve, qk)
                        then(tt(rot_a, rot_a, rot_b, ALU.add))
                        q, k = rot_a[:, 0, :, :], rot_a[:, 1, :, :]
                        q2 = q.unsqueeze(2).to_broadcast([P, H, 2, SD])
                        copy(q_tmp[:, buf, :, 0:2, :].bitcast(F32R), q2)
                        k2 = k.unsqueeze(2).to_broadcast([P, H, 2, SD])
                        then(copy(k_tmp[:, buf, :, :, 0, :].bitcast(F32R), k2))
                        tt(q_tmp[:, buf, :, 2:4, :], q2, q_tmp[:, buf, :, 0:2, :], ALU.subtract)
                        tt(k_tmp[:, buf, :, :, 1, :], k2, k_tmp[:, buf, :, :, 0, :], ALU.subtract).then_inc(stack_ready, 1)
                    elif kind == "ksplit":
                        ckv = ("ckv", 2, s, 0)
                        wait_filled(dve, ckv)
                        both = bank_of(ckv)[:, :].rearrange("p (t w h d) -> p t w h d", t=TT, w=2, h=H)
                        for t in range(TT):
                            k2 = both[:, t, 0, :, :].unsqueeze(2).to_broadcast([P, H, 2, CD])
                            last = copy(kc_tmp[:, s, H * t:H * t + H, :, 0, :].bitcast(F32R), k2)
                        then(last)
                        for t in range(TT):
                            k2 = both[:, t, 0, :, :].unsqueeze(2).to_broadcast([P, H, 2, CD])
                            last = tt(kc_tmp[:, s, H * t:H * t + H, :, 1, :], k2,
                                      kc_tmp[:, s, H * t:H * t + H, :, 0, :], ALU.subtract)
                        last.then_inc(split_ready, 1)
                        dve.wait_ge(vc_zeroed, s + 1)
                        for c in range(4):
                            for t in range(TT):
                                heads = vc[s][:, t, :, :].rearrange("p (a c) d -> p a c d", c=4)
                                vals = both[:, t, 1, :, :].rearrange("p (a c) d -> p a c d", c=4)
                                last = copy(heads[:, :, c, CD * c:CD * c + CD], vals[:, :, c, :])
                        last.then_inc(drained[unit[ckv][0]], 1)
                    elif kind == "qsplit":
                        cq = ("cq", 2, s, 0)
                        wait_filled(dve, cq)
                        flat = bank_of(cq)[:, 0:TT * DC].rearrange("p (h d) -> p h d", d=CD)
                        ins = ts(qc_raw[s][:, :, :], flat, float(CD) ** -0.5, None, ALU.mult)
                        ins.then_inc(drained[unit[cq][0]], 1)
                        wait_drained(dve, cq)
                        q2 = qc_raw[s][:, :, :].unsqueeze(2).to_broadcast([P, TT * H, 2, CD])
                        then(copy(qc_tmp[s][:, :, 0:2, :].bitcast(F32R), q2))
                        tt(qc_tmp[s][:, :, 2:4, :], q2, qc_tmp[s][:, :, 0:2, :], ALU.subtract).then_inc(split_ready, 1)
                    elif kind == "gateup":
                        rows = slice(0, P if i < MT - 1 else MLAST)
                        dve.wait_ge(silu_ready, nth[step])
                        ins = tt(sg[s][rows, i, :], src[rows, T:2 * T], sg[s][rows, i, :], ALU.mult)
                        ins.then_inc(free, 1)
                        wait_drained(dve, step)
                        for e in range(2):
                            last = tt(acts[s][rows, e, i, :], sg[s][rows, i, :], expert[rows, s, e, :], ALU.mult)
                        last.then_inc(acts_ready, 1)
                    elif kind == "mgate":
                        wait_filled(dve, step)
                        tt(mz[s][:, :, :], src[:, :].rearrange("p (t d) -> p t d", t=TT),
                           fusion_rows[:, 0:1, :].to_broadcast([P, TT, D]), ALU.add).then_inc(free, 1)
                    elif kind == "fuse":
                        dve.wait_ge(mgate_ready, s + 1)
                        then(tt(mg[s], mg[s], mctx[s], ALU.mult))
                        then(tt(x[s], x[s], mg[s], ALU.add))
                        statistics(s, x[s], True)
                        dve.wait_ge(rstd_ready, root_no[step])
                        for t in range(TT):
                            last = stt(out=x[s][:, t, :], in0=x[s][:, t, :], scalar=rstd[:, s, t:t + 1],
                                       in1=fusion_rows[:, 1, :], op0=ALU.mult, op1=ALU.mult)
                        then(last)
                dve.drain().then_inc(engines_done, 1)
                dve.wait_ge(iteration_open, it + 1)


_X = ["Wq", "Wkv", "Wo", "W1", "W2"]
_L1 = ["v_qkv", "l_qkv", "v_dense", "l_dense", "cq_w", "ckv_w", "cdense_w", "v_gate", "v_up", "v_down", "l_gate",
       "l_up", "l_down"]
_GAINS = [f"L{n}_xattn_{g}" for n in (0, 3) for g in ("ln_q_g", "ln_q_b", "ln_ff_g", "ln_ff_b")]
_GAINS += [f"L1_xattn_{g}" for g in ("ln_in_w", "ln_post_attn_w", "ln_post_cross_w")]
_GATES = [f"L{n}_xattn_{g}" for n in (0, 3) for g in ("attn_gate", "ff_gate")]


def _constants():
    f = np.float32
    causal = np.zeros((P, 2 * P), f)
    causal[:, P:] = np.triu(np.full((P, P), NEG, f), 1)
    inv = f(1.0) / np.power(f(10000.0), np.arange(0, SD, 2, dtype=f) / f(SD), dtype=f)
    angle = np.outer(np.arange(T, dtype=f), inv)
    cos, sin = np.cos(angle), np.sin(angle)
    rows = np.concatenate([cos, cos, -sin, sin], -1)
    rot = np.concatenate([rows * f(-float(SD) ** -0.5), rows], -1).astype(f)
    ones = np.zeros((6, 32), f)
    for n in range(2):
        ones[n, SD * n:SD * n + SD] = 1.0
    for n in range(4):
        ones[2 + n, CD * n:CD * n + CD] = 1.0
    ones = np.tile(ones.reshape(1, -1), (P, 1))
    iota = np.arange(T, dtype=f).reshape(TT, P).T.copy()
    return {"ident": np.eye(P, dtype=f), "causal": causal, "iota": iota, "rot": rot, "ones": ones}


def kernel(**inputs):
    import concourse.bacc as _bacc
    from concourse.bass_utils import run_bass_kernel_spmd as _run

    nc = _bacc.Bacc("TRN2", target_bir_lowering=False, num_devices=1)
    arrays = {}

    def feed(name, a):
        a = np.ascontiguousarray(a)
        arrays[name] = a
        return nc.dram_tensor(name, a.shape, mybir.dt.from_np(a.dtype), kind="ExternalInput").ap()

    x = feed("x", inputs["x"])
    ctx = feed("ctx", inputs["ctx_1024"])
    pos = feed("pos", inputs["pos_1xS"])
    media = feed("media_mask", inputs["mask_BxS2_bk0"])
    expert = feed("expert_mask", inputs["mask_BxS_ik0"])
    xw = {n: {k: feed(f"L{n}_{k}", inputs[f"L{n}_xattn_{k}"]) for k in _X} for n in (0, 3)}
    l1 = {k: feed(f"L1_{k}", inputs[f"L1_xattn_{k}"]) for k in _L1}
    l2 = {k: feed(f"L2_{k}", np.asarray(inputs[f"L2_xattn_{k}"]).T) for k in ("W_mem", "W_gate")}
    columns = [np.asarray(inputs[k]).reshape(KD, P).T for k in _GAINS]
    gains = feed("gains", np.concatenate(columns, axis=1))
    gates = feed("gates", np.concatenate([np.asarray(inputs[k]) for k in _GATES]))
    fusion_rows = feed("fusion_rows", np.stack([np.asarray(inputs["L2_xattn_b_gate"]), np.asarray(inputs["L2_xattn_norm_w"])]))
    consts = {k: feed(f"const_{k}", a) for k, a in _constants().items()}
    out = nc.dram_tensor("out", (B, T, D), F32, kind="ExternalOutput").ap()
    fused_layers(nc, x, ctx, pos, media, expert, gains, gates, fusion_rows, xw, l1, l2, consts, out)
    r = _run(nc, [arrays], core_ids=[0])
    return r.results[0]["out"]
```
